# Optimizing a Trainium2 kernel written in Bass

```python
import numpy as np
import jax
import jax.numpy as jnp

def _softmax(x, axis=-1):
    return jax.nn.softmax(x, axis=axis)

def _gelu(x):
    return jax.nn.gelu(x, approximate=True)

def _silu(x):
    return jax.nn.silu(x)

def _sigmoid(x):
    return jax.nn.sigmoid(x)

def _layernorm(x, axis=-1, eps=1e-05):
    m = jnp.mean(x, axis=axis, keepdims=True)
    v = jnp.var(x, axis=axis, keepdims=True)
    return (x - m) / jnp.sqrt(v + eps)

def _scatter_add(tgt, idx, src, axis=0):
    return tgt.at[idx].add(src)

def _segment_sum(src, seg, n):
    return jax.ops.segment_sum(src, seg, n)
kernel_name = 'mk_decoder_postln_d2_seqx_r8_3a38f2'

def setup_inputs(seed: int=0):
    np.random.seed(seed)
    _w = jnp.asarray

    def _rec_inputs():
        import jax
        import jax.numpy as jnp
        _rk = jax.random.key(seed)
        x = -0.0003929 + 0.9999 * jax.random.normal(jax.random.fold_in(_rk, 1), (16, 64, 512), jnp.float32)
        _lenS = 64 - jax.random.randint(jax.random.fold_in(_rk, 7), (16,), 0, max(1, 64 // 4) + 1, jnp.int32)
        _lenS2 = 64 - jax.random.randint(jax.random.fold_in(_rk, 8), (16,), 0, max(1, 64 // 4) + 1, jnp.int32)
        _ctx_4096P = jax.random.normal(jax.random.fold_in(_rk, 11), (16, 16, 512), jnp.float32)
        _ctx_4096c = jax.random.dirichlet(jax.random.fold_in(_rk, 511), 0.3 * jnp.ones((16,), jnp.float32), (16, 64))
        _ctx_4096t = jnp.einsum('bsk,bkd->bsd', _ctx_4096c, _ctx_4096P)
        _ctx_4096t = _ctx_4096t * jax.lax.rsqrt(jnp.mean(jnp.square(_ctx_4096t)) + 1e-12) * 0.953939
        ctx_4096 = 2.81802e-05 + 1.00001 * (_ctx_4096t + 0.3 * jax.random.normal(jax.random.fold_in(_rk, 611), (16, 64, 512), jnp.float32))
        _validS = jnp.arange(64)[None, :] < _lenS[:, None]
        _validS2 = jnp.arange(64)[None, :] < _lenS2[:, None]
        _causal = jnp.tril(jnp.ones((64, 64), dtype=bool))
        mask_1x1xSxS2_ff0 = jnp.where(jnp.ones((1, 1, 64, 64), dtype=bool), 0.0, -1000000000.0).astype(jnp.float32)
        return (x, ctx_4096, mask_1x1xSxS2_ff0)
    x, ctx_4096, mask_1x1xSxS2_ff0 = _rec_inputs()

    def _L0_attn_setup():
        import jax, jax.numpy as jnp
        import numpy as np
        D_MODEL = 512
        N_Q = 32
        N_KV = 8
        HD = 128
        SLIDE = 64

        def _gqa_swa_attention(q, k, v, slide):
            B, Hq, N, D = q.shape
            Hkv = k.shape[1]
            G = Hq // Hkv
            qg = q.reshape(B, Hkv, G, N, D)
            scale = 1.0 / jnp.sqrt(jnp.asarray(D, q.dtype))
            s = jnp.einsum('bhgnd,bhmd->bhgnm', qg, k) * scale
            i = jnp.arange(N)[:, None]
            j = jnp.arange(N)[None, :]
            mask = j <= i
            if slide > 0:
                mask = mask & (i - j < slide)
            s = jnp.where(mask[None, None, None], s, jnp.asarray(-jnp.inf, s.dtype))
            p = jax.nn.softmax(s, axis=-1)
            o = jnp.einsum('bhgnm,bhmd->bhgnd', p, v)
            return o.reshape(B, Hq, N, D)
        key = jax.random.key(seed)
        ks = jax.random.split(key, 5)
        std = 0.01
        x = jax.random.normal(ks[0], (2, 256, D_MODEL), dtype=jnp.float32)
        wq = jax.random.normal(ks[1], (N_Q * HD, D_MODEL), dtype=jnp.float32) * std
        wk = jax.random.normal(ks[2], (N_KV * HD, D_MODEL), dtype=jnp.float32) * std
        wv = jax.random.normal(ks[3], (N_KV * HD, D_MODEL), dtype=jnp.float32) * std
        wo = jax.random.normal(ks[4], (D_MODEL, N_Q * HD), dtype=jnp.float32) * std
        return {'x': x, 'wq': wq, 'wk': wk, 'wv': wv, 'wo': wo}
    _L0_attn_all = _L0_attn_setup()
    _L0_attn_in = {k: v for k, v in _L0_attn_all.items() if k in ('wq', 'wk', 'wv', 'wo')}
    del _L0_attn_all

    def _L0_xattn_setup():
        import jax, jax.numpy as jnp
        import numpy as np
        HEADS = 8
        DIM_HEAD = 64
        DIM = 64
        HIDDEN = HEADS * DIM_HEAD
        B, N = (8, 512)
        key = jax.random.key(seed)
        ks = jax.random.split(key, 7)
        s = 0.02
        return {'x': jax.random.normal(ks[0], (B, DIM, N), dtype=jnp.float32), 'context': jax.random.normal(ks[1], (B, DIM, N), dtype=jnp.float32), 'Wq': jax.random.normal(ks[2], (HIDDEN, DIM), dtype=jnp.float32) * s, 'Wkv': jax.random.normal(ks[3], (2 * HIDDEN, DIM), dtype=jnp.float32) * s, 'Wout': jax.random.normal(ks[4], (DIM, HIDDEN), dtype=jnp.float32) * s, 'b_out': jnp.zeros((DIM,), dtype=jnp.float32), 'g': jnp.ones((1, DIM, 1), dtype=jnp.float32)}
    _L0_xattn_all = _L0_xattn_setup()
    _L0_xattn_in = {k: v for k, v in _L0_xattn_all.items() if k in ('Wq', 'Wkv', 'Wout', 'b_out', 'g')}
    del _L0_xattn_all

    def _L0_ffn_setup():
        import jax, jax.numpy as jnp
        import numpy as np
        H = 512
        I = 1792
        G = 128

        def dequant(q, s, g=G):
            O, In = q.shape
            return (q.reshape(O, In // g, g).astype(s.dtype) * s[:, :, None]).reshape(O, In)
        key = jax.random.key(seed)
        ks = jax.random.split(key, 7)
        x = jax.random.normal(ks[0], (2, 256, H), dtype=jnp.float32)

        def mk_qlinear(kq, ksc, out_d, in_d):
            q = jax.random.randint(kq, (out_d, in_d), -8, 8, dtype=jnp.int32)
            s = jax.random.uniform(ksc, (out_d, in_d // G), dtype=jnp.float32, minval=0.005, maxval=0.02)
            return (q, s)
        gate_q, gate_s = mk_qlinear(ks[1], ks[2], I, H)
        up_q, up_s = mk_qlinear(ks[3], ks[4], I, H)
        down_q, down_s = mk_qlinear(ks[5], ks[6], H, I)
        return {'x': x, 'gate_q': gate_q, 'gate_s': gate_s, 'up_q': up_q, 'up_s': up_s, 'down_q': down_q, 'down_s': down_s}
    _L0_ffn_all = _L0_ffn_setup()
    _L0_ffn_in = {k: v for k, v in _L0_ffn_all.items() if k in ('gate_q', 'gate_s', 'up_q', 'up_s', 'down_q', 'down_s')}
    del _L0_ffn_all

    def _L1_attn_setup():
        import jax, jax.numpy as jnp
        import numpy as np
        import math
        NH, NKV, D = (32, 8, 128)

        def _alibi_slopes(n):
            cp2 = 2 ** math.floor(math.log2(n))
            base = 2.0 ** (-8.0 / cp2)
            slopes = base ** np.arange(1, cp2 + 1, dtype=np.float32)
            if cp2 != n:
                extra_base = 2.0 ** (-4.0 / cp2)
                extra = extra_base ** np.arange(1, 1 + 2 * (n - cp2), 2, dtype=np.float32)
                slopes = np.concatenate([slopes, extra])
            return slopes.astype(np.float32)
        key = jax.random.key(seed)
        k1, k2, k3 = jax.random.split(key, 3)
        B, S, H = (4, 128, 512)
        qkv_out = NH * D + 2 * NKV * D
        return {'hidden_states': jax.random.normal(k1, (B, S, H), jnp.float32) * 0.02, 'w_qkv': jax.random.normal(k2, (H, qkv_out), jnp.float32) * 0.02, 'w_o': jax.random.normal(k3, (NH * D, H), jnp.float32) * 0.02}
    _L1_attn_all = _L1_attn_setup()
    _L1_attn_in = {k: v for k, v in _L1_attn_all.items() if k in ('w_qkv', 'w_o')}
    del _L1_attn_all

    def _L1_xattn_setup():
        import jax, jax.numpy as jnp
        import numpy as np
        NUM_HEADS = 32
        NUM_KV_HEADS = 8
        HEAD_DIM = 128
        HIDDEN = 512
        EPS = 1e-05

        def rmsnorm(x, w, eps=EPS):
            xf = x.astype(jnp.float32)
            var = jnp.mean(xf * xf, axis=-1, keepdims=True)
            return w * (xf * jax.lax.rsqrt(var + eps)).astype(x.dtype)
        key = jax.random.key(seed)
        ks = jax.random.split(key, 10)
        B, Q, KV = (1, 128, 6404)
        s = 1.0 / np.sqrt(HIDDEN)
        return {'hidden_states': jax.random.normal(ks[0], (B, Q, HIDDEN), jnp.float32), 'cross_attention_states': jax.random.normal(ks[1], (B, KV, HIDDEN), jnp.float32), 'attention_mask': jnp.zeros((B, 1, Q, KV), jnp.float32), 'q_proj_w': jax.random.normal(ks[2], (NUM_HEADS * HEAD_DIM, HIDDEN), jnp.float32) * s, 'k_proj_w': jax.random.normal(ks[3], (NUM_KV_HEADS * HEAD_DIM, HIDDEN), jnp.float32) * s, 'v_proj_w': jax.random.normal(ks[4], (NUM_KV_HEADS * HEAD_DIM, HIDDEN), jnp.float32) * s, 'o_proj_w': jax.random.normal(ks[5], (HIDDEN, NUM_HEADS * HEAD_DIM), jnp.float32) * s, 'q_norm_w': jnp.ones((HEAD_DIM,), jnp.float32), 'k_norm_w': jnp.ones((HEAD_DIM,), jnp.float32)}
    _L1_xattn_all = _L1_xattn_setup()
    _L1_xattn_in = {k: v for k, v in _L1_xattn_all.items() if k in ('q_proj_w', 'k_proj_w', 'v_proj_w', 'o_proj_w', 'q_norm_w', 'k_norm_w')}
    del _L1_xattn_all

    def _L1_ffn_setup():
        import jax, jax.numpy as jnp
        import numpy as np
        B, S, D, O, E, R = (4, 256, 512, 512, 8, 16)
        SCALING = 32.0 / 16.0
        MAX_THRESHOLD = 0.125
        key = jax.random.key(seed)
        ks = jax.random.split(key, 8)
        return {'x': jax.random.normal(ks[0], (B, S, D), jnp.float32), 'W_base': jax.random.normal(ks[1], (O, D), jnp.float32) * (1.0 / np.sqrt(D)), 'b_base': jax.random.normal(ks[2], (O,), jnp.float32) * 0.02, 'W_gate': jax.random.normal(ks[3], (E, D), jnp.float32) * (1.0 / np.sqrt(D)), 'W_thr': jax.random.normal(ks[4], (D,), jnp.float32) * (1.0 / np.sqrt(D)), 'b_thr': jax.random.normal(ks[5], (1,), jnp.float32) * 0.02, 'A_w': jax.random.normal(ks[6], (E, R, D), jnp.float32) * (1.0 / np.sqrt(D)), 'B_w': jax.random.normal(ks[7], (E, O, R), jnp.float32) * (1.0 / np.sqrt(R))}
    _L1_ffn_all = _L1_ffn_setup()
    _L1_ffn_in = {k: v for k, v in _L1_ffn_all.items() if k in ('W_base', 'b_base', 'W_gate', 'W_thr', 'b_thr', 'A_w', 'B_w')}
    del _L1_ffn_all
    return {'x': x, 'ctx_4096': ctx_4096, 'mask_1x1xSxS2_ff0': mask_1x1xSxS2_ff0, 'L0_attn_wq': _L0_attn_in['wq'], 'L0_attn_wk': _L0_attn_in['wk'], 'L0_attn_wv': _L0_attn_in['wv'], 'L0_attn_wo': _L0_attn_in['wo'], 'L0_xattn_Wq': _L0_xattn_in['Wq'], 'L0_xattn_Wkv': _L0_xattn_in['Wkv'], 'L0_xattn_Wout': _L0_xattn_in['Wout'], 'L0_xattn_b_out': _L0_xattn_in['b_out'], 'L0_xattn_g': _L0_xattn_in['g'], 'L0_ffn_gate_q': _L0_ffn_in['gate_q'], 'L0_ffn_gate_s': _L0_ffn_in['gate_s'], 'L0_ffn_up_q': _L0_ffn_in['up_q'], 'L0_ffn_up_s': _L0_ffn_in['up_s'], 'L0_ffn_down_q': _L0_ffn_in['down_q'], 'L0_ffn_down_s': _L0_ffn_in['down_s'], 'L1_attn_w_qkv': _L1_attn_in['w_qkv'], 'L1_attn_w_o': _L1_attn_in['w_o'], 'L1_xattn_q_proj_w': _L1_xattn_in['q_proj_w'], 'L1_xattn_k_proj_w': _L1_xattn_in['k_proj_w'], 'L1_xattn_v_proj_w': _L1_xattn_in['v_proj_w'], 'L1_xattn_o_proj_w': _L1_xattn_in['o_proj_w'], 'L1_xattn_q_norm_w': _L1_xattn_in['q_norm_w'], 'L1_xattn_k_norm_w': _L1_xattn_in['k_norm_w'], 'L1_ffn_W_base': _L1_ffn_in['W_base'], 'L1_ffn_b_base': _L1_ffn_in['b_base'], 'L1_ffn_W_gate': _L1_ffn_in['W_gate'], 'L1_ffn_W_thr': _L1_ffn_in['W_thr'], 'L1_ffn_b_thr': _L1_ffn_in['b_thr'], 'L1_ffn_A_w': _L1_ffn_in['A_w'], 'L1_ffn_B_w': _L1_ffn_in['B_w']}

def reference(x, ctx_4096, mask_1x1xSxS2_ff0, L0_attn_wq, L0_attn_wk, L0_attn_wv, L0_attn_wo, L0_xattn_Wq, L0_xattn_Wkv, L0_xattn_Wout, L0_xattn_b_out, L0_xattn_g, L0_ffn_gate_q, L0_ffn_gate_s, L0_ffn_up_q, L0_ffn_up_s, L0_ffn_down_q, L0_ffn_down_s, L1_attn_w_qkv, L1_attn_w_o, L1_xattn_q_proj_w, L1_xattn_k_proj_w, L1_xattn_v_proj_w, L1_xattn_o_proj_w, L1_xattn_q_norm_w, L1_xattn_k_norm_w, L1_ffn_W_base, L1_ffn_b_base, L1_ffn_W_gate, L1_ffn_W_thr, L1_ffn_b_thr, L1_ffn_A_w, L1_ffn_B_w):
    import jax
    import jax.numpy as jnp

    def _L0_attn_ref(x, wq, wk, wv, wo):
        import jax, jax.numpy as jnp
        import numpy as np
        D_MODEL = 512
        N_Q = 32
        N_KV = 8
        HD = 128
        SLIDE = 64

        def _gqa_swa_attention(q, k, v, slide):
            B, Hq, N, D = q.shape
            Hkv = k.shape[1]
            G = Hq // Hkv
            qg = q.reshape(B, Hkv, G, N, D)
            scale = 1.0 / jnp.sqrt(jnp.asarray(D, q.dtype))
            s = jnp.einsum('bhgnd,bhmd->bhgnm', qg, k) * scale
            i = jnp.arange(N)[:, None]
            j = jnp.arange(N)[None, :]
            mask = j <= i
            if slide > 0:
                mask = mask & (i - j < slide)
            s = jnp.where(mask[None, None, None], s, jnp.asarray(-jnp.inf, s.dtype))
            p = jax.nn.softmax(s, axis=-1)
            o = jnp.einsum('bhgnm,bhmd->bhgnd', p, v)
            return o.reshape(B, Hq, N, D)
        B, N, _ = x.shape
        q = (x @ wq.T).reshape(B, N, N_Q, HD).transpose(0, 2, 1, 3)
        k = (x @ wk.T).reshape(B, N, N_KV, HD).transpose(0, 2, 1, 3)
        v = (x @ wv.T).reshape(B, N, N_KV, HD).transpose(0, 2, 1, 3)
        o = _gqa_swa_attention(q, k, v, SLIDE)
        o = o.transpose(0, 2, 1, 3).reshape(B, N, N_Q * HD)
        return o @ wo.T

    def _L0_xattn_ref(x, context, Wq, Wkv, Wout, b_out, g):
        import jax, jax.numpy as jnp
        import numpy as np
        HEADS = 8
        DIM_HEAD = 64
        DIM = 64
        HIDDEN = HEADS * DIM_HEAD
        B, N = (8, 512)
        scale = DIM_HEAD ** (-0.5)
        q = jnp.einsum('oc,bcn->bon', Wq, x)
        kv = jnp.einsum('oc,bcn->bon', Wkv, context)
        k, v = jnp.split(kv, 2, axis=1)

        def split_heads(t):
            b, hc, n = t.shape
            return t.reshape(b, HEADS, DIM_HEAD, n)
        q = jax.nn.softmax(split_heads(q), axis=-2) * scale
        k = jax.nn.softmax(split_heads(k), axis=-1)
        v = split_heads(v)
        ctx = jnp.einsum('bhdn,bhen->bhde', k, v)
        out = jnp.einsum('bhde,bhdn->bhen', ctx, q)
        b, h, e, n = out.shape
        out = out.reshape(b, h * e, n)
        out = jnp.einsum('oc,bcn->bon', Wout, out) + b_out[None, :, None]
        mean = jnp.mean(out, axis=1, keepdims=True)
        var = jnp.var(out, axis=1, keepdims=True)
        return (out - mean) * jax.lax.rsqrt(var + 1e-05) * g

    def _L0_ffn_ref(x, gate_q, gate_s, up_q, up_s, down_q, down_s):
        import jax, jax.numpy as jnp
        import numpy as np
        H = 512
        I = 1792
        G = 128

        def dequant(q, s, g=G):
            O, In = q.shape
            return (q.reshape(O, In // g, g).astype(s.dtype) * s[:, :, None]).reshape(O, In)
        Wg = dequant(gate_q, gate_s)
        Wu = dequant(up_q, up_s)
        Wd = dequant(down_q, down_s)
        gate_score = jax.nn.silu(jnp.einsum('bsh,ih->bsi', x, Wg))
        intermediate = gate_score * jnp.einsum('bsh,ih->bsi', x, Wu)
        return jnp.einsum('bsi,hi->bsh', intermediate, Wd)

    def _L1_attn_ref(hidden_states, w_qkv, w_o):
        import jax, jax.numpy as jnp
        import numpy as np
        import math
        NH, NKV, D = (32, 8, 128)

        def _alibi_slopes(n):
            cp2 = 2 ** math.floor(math.log2(n))
            base = 2.0 ** (-8.0 / cp2)
            slopes = base ** np.arange(1, cp2 + 1, dtype=np.float32)
            if cp2 != n:
                extra_base = 2.0 ** (-4.0 / cp2)
                extra = extra_base ** np.arange(1, 1 + 2 * (n - cp2), 2, dtype=np.float32)
                slopes = np.concatenate([slopes, extra])
            return slopes.astype(np.float32)
        B, S, H = hidden_states.shape
        G = NH // NKV
        scale = D ** (-0.5)
        qkv = hidden_states @ w_qkv
        q = qkv[..., :NH * D].reshape(B, S, NKV, G, D)
        k = qkv[..., NH * D:NH * D + NKV * D].reshape(B, S, NKV, D)
        v = qkv[..., NH * D + NKV * D:].reshape(B, S, NKV, D)
        scores = jnp.einsum('bqhgd,bkhd->bhgqk', q, k) * scale
        slopes = jnp.asarray(_alibi_slopes(NH)).reshape(NKV, G)
        pos = jnp.arange(S)
        rel = pos[:, None] - pos[None, :]
        sqrt_dist = jnp.sqrt(jnp.maximum(rel, 0).astype(jnp.float32))
        bias = -slopes[:, :, None, None] * sqrt_dist
        bias = jnp.where(rel[None, None] >= 0, bias, -jnp.inf)
        attn = jax.nn.softmax(scores + bias[None], axis=-1)
        out = jnp.einsum('bhgqk,bkhd->bqhgd', attn, v).reshape(B, S, NH * D)
        return out @ w_o

    def _L1_xattn_ref(hidden_states, cross_attention_states, attention_mask, q_proj_w, k_proj_w, v_proj_w, o_proj_w, q_norm_w, k_norm_w):
        import jax, jax.numpy as jnp
        import numpy as np
        NUM_HEADS = 32
        NUM_KV_HEADS = 8
        HEAD_DIM = 128
        HIDDEN = 512
        EPS = 1e-05

        def rmsnorm(x, w, eps=EPS):
            xf = x.astype(jnp.float32)
            var = jnp.mean(xf * xf, axis=-1, keepdims=True)
            return w * (xf * jax.lax.rsqrt(var + eps)).astype(x.dtype)
        B, Q, _ = hidden_states.shape
        KV = cross_attention_states.shape[1]
        n_rep = NUM_HEADS // NUM_KV_HEADS
        q = (hidden_states @ q_proj_w.T).reshape(B, Q, NUM_HEADS, HEAD_DIM).transpose(0, 2, 1, 3)
        k = (cross_attention_states @ k_proj_w.T).reshape(B, KV, NUM_KV_HEADS, HEAD_DIM).transpose(0, 2, 1, 3)
        v = (cross_attention_states @ v_proj_w.T).reshape(B, KV, NUM_KV_HEADS, HEAD_DIM).transpose(0, 2, 1, 3)
        q = rmsnorm(q, q_norm_w)
        k = jnp.repeat(k, n_rep, axis=1)
        v = jnp.repeat(v, n_rep, axis=1)
        k = rmsnorm(k, k_norm_w)
        scale = 1.0 / np.sqrt(HEAD_DIM)
        scores = jnp.einsum('bhqd,bhkd->bhqk', q, k) * scale + attention_mask
        attn = jax.nn.softmax(scores.astype(jnp.float32), axis=-1).astype(q.dtype)
        out = jnp.einsum('bhqk,bhkd->bhqd', attn, v)
        out = out.transpose(0, 2, 1, 3).reshape(B, Q, NUM_HEADS * HEAD_DIM)
        return out @ o_proj_w.T

    def _L1_ffn_ref(x, W_base, b_base, W_gate, W_thr, b_thr, A_w, B_w):
        import jax, jax.numpy as jnp
        import numpy as np
        B, S, D, O, E, R = (4, 256, 512, 512, 8, 16)
        SCALING = 32.0 / 16.0
        MAX_THRESHOLD = 0.125
        base = jnp.einsum('bsd,od->bso', x, W_base) + b_base
        xf = x.reshape(-1, D)
        gate = jax.nn.softmax(xf @ W_gate.T, axis=-1)
        thr = jax.nn.sigmoid(xf @ W_thr + b_thr[0]) * MAX_THRESHOLD
        adapted = gate - thr[:, None]
        selected = (adapted >= 0).astype(x.dtype)
        w = adapted * selected
        wsum = jnp.sum(w, axis=-1, keepdims=True)
        wsum = jnp.where(wsum == 0, jnp.ones_like(wsum), wsum)
        w = w / wsum
        h = jnp.einsum('nd,erd->ner', xf, A_w)
        moe = jnp.einsum('ner,ne,eor->no', h, w, B_w) * SCALING
        return base + moe.reshape(base.shape)
    x = _layernorm(x + _L0_attn_ref(x, L0_attn_wq, L0_attn_wk, L0_attn_wv, L0_attn_wo), axis=-1)
    x = _layernorm(x + _L0_xattn_ref(x, ctx_4096, L0_xattn_Wq, L0_xattn_Wkv, L0_xattn_Wout, L0_xattn_b_out, L0_xattn_g), axis=-1)
    x = _layernorm(x + _L0_ffn_ref(x, L0_ffn_gate_q, L0_ffn_gate_s, L0_ffn_up_q, L0_ffn_up_s, L0_ffn_down_q, L0_ffn_down_s), axis=-1)
    x = _layernorm(x + _L1_attn_ref(x, L1_attn_w_qkv, L1_attn_w_o), axis=-1)
    x = _layernorm(x + _L1_xattn_ref(x, ctx_4096, mask_1x1xSxS2_ff0, L1_xattn_q_proj_w, L1_xattn_k_proj_w, L1_xattn_v_proj_w, L1_xattn_o_proj_w, L1_xattn_q_norm_w, L1_xattn_k_norm_w), axis=-1)
    x = _layernorm(x + _L1_ffn_ref(x, L1_ffn_W_base, L1_ffn_b_base, L1_ffn_W_gate, L1_ffn_W_thr, L1_ffn_b_thr, L1_ffn_A_w, L1_ffn_B_w), axis=-1)
    return x

_drawn_inputs = setup_inputs


def setup_inputs(seed=0):
    import zlib

    import numpy as np

    out = dict(_drawn_inputs(seed))
    spreads = {'L0_xattn_b_out': (0.0, 0.8),
     'L0_xattn_g': (1.0, 0.6),
     'L1_xattn_q_norm_w': (1.0, 0.2),
     'L1_xattn_k_norm_w': (1.0, 0.2)}
    factors = {'L0_attn_wq': 8.0,
     'L0_attn_wk': 8.0,
     'L0_xattn_Wq': 8.0,
     'L0_xattn_Wkv': 8.0,
     'L0_xattn_Wout': 8.0,
     'L1_ffn_b_base': 5.222}
    for name, (base, spread) in spreads.items():
        noise = np.random.default_rng([zlib.crc32(name.encode()), seed]).standard_normal(out[name].shape)
        drawn = base * np.exp(spread * noise) if base else spread * noise
        out[name] = jnp.asarray(drawn.astype(out[name].dtype))
    for name, factor in factors.items():
        out[name] = (out[name] * factor).astype(out[name].dtype)
    return out
```

```python
from contextlib import ExitStack

import concourse.bass as bass
from concourse import mybir

F32 = mybir.dt.float32
F32R = mybir.dt.float32r
I32 = mybir.dt.int32
ALU = mybir.AluOpType
ACT = mybir.ActivationFunctionType
AX_X = mybir.AxisListType.X

P = 128
B, S, DM = 16, 64, 512
TOK = B * S
NT = TOK // P
KT = DM // P
NKV, G, HD = 8, 4, 128
HALF = TOK // 2
EPS = 1e-5

XH, XD = 8, 64
XW = XH * XD

FI = 1792
FSTEP = 256
NF = FI // FSTEP

E_, R_ = 8, 16
GC = E_ * R_ + E_ + 2

NEG = -1.0e30


def wait(eng, sem, n):
    if isinstance(n, int) and n <= 0:
        return
    eng.wait_ge(sem, n)


def carry_waits(eng, waits_passed):
    eng.sem_inc(waits_passed, 1)


def units(rms):
    q = [("q", g, n) for g in range(G) for n in range(2)]
    if rms:
        return [("kv", 0, n) for n in range(4)] + q
    return [("k", 0, 0), ("k", 0, 1)] + q + [("v", 0, 0), ("v", 0, 1)]


def schedule(rms, project, attend):
    ev = []
    n_u = 12
    first_sc = 5 if rms else 3
    done = [0]
    def unit():
        u = done[0]
        if project and u < n_u:
            ev.append(("U", u))
            if rms and u in (3, 4):
                ev.append(("KT", u - 3))
            j = u - first_sc
            if 0 <= j < 8:
                if rms:
                    ev.append(("SQ", j))
                ev.append(("SC", j))
            if u == n_u - 1:
                for j in range(n_u - first_sc, 8):
                    if rms:
                        ev.append(("SQ", j))
                    ev.append(("SC", j))
        done[0] += 1
    unit()
    if attend:
        ev.append(("T", 0))
    unit()
    for t in range(NT):
        if attend:
            ev.append(("PV", t))
            if t + 1 < NT:
                ev.append(("T", t + 1))
        unit()
        if attend:
            ev.append(("WO", t))
    unit()
    if project:
        ev.append(("WS", 0))
    unit()
    return ev


def later(events, kinds, by):
    out, held = [], []
    for e in events:
        if e[0] in kinds:
            held.append([by, e])
            continue
        out.append(e)
        for h in held:
            h[0] -= 1
        while held and held[0][0] <= 0:
            out.append(held.pop(0)[1])
    return out + [h[1] for h in held]


def program(nc, a):
    with ExitStack() as ctx:
        def sem(name):
            return ctx.enter_context(nc.semaphore(name))

        def keep(name, shape, dt=F32):
            return ctx.enter_context(nc.sbuf_tensor(name, shape, dt))

        X = keep("X", [P, NT * DM])
        xTh = keep("xTh", [P, KT, TOK], F32R)
        xTl = keep("xTl", [P, KT, TOK], F32R)
        cTh = keep("cTh", [P, KT, TOK], F32R)
        cTl = keep("cTl", [P, KT, TOK], F32R)
        ident = keep("ident", [P, P])
        st6 = keep("st6", [P, NT, 6])
        mv = keep("mv", [P, NT, 2])
        var_eps = keep("var_eps", [P, NT])
        rstd = keep("rstd", [P, NT])
        mhalf = keep("mhalf", [P, 32])
        onecol = keep("onecol", [P, 1])
        own_half = keep("own_half", [P, 2])

        pb = [ctx.enter_context(nc.psum_tensor(f"pb{i}", [P, 512], F32)) for i in range(8)]

        xT, cT = (xTh, xTl), (cTh, cTl)

        with ExitStack() as sa:
            def sb(name, shape, dt=F32):
                return sa.enter_context(nc.sbuf_tensor(name, shape, dt))
            wh = sb("wh", [P, 6, KT, P], F32R)
            wl = sb("wl", [P, 6, KT, P], F32R)
            woh = sb("woh", [P, G, DM], F32R)
            wol = sb("wol", [P, G, DM], F32R)
            qh = sb("qh", [P, 2, HALF], F32R)
            ql = sb("ql", [P, 2, HALF], F32R)
            kh = sb("kh", [P, TOK], F32R)
            kl = sb("kl", [P, TOK], F32R)
            vh = sb("vh", [P, NT, HD], F32R)
            vl = sb("vl", [P, NT, HD], F32R)
            pth = sb("pth", [P, G * P], F32R)
            ptl = sb("ptl", [P, G * P], F32R)
            oth = sb("oth", [P, G * P], F32R)
            otl = sb("otl", [P, G * P], F32R)
            raw = sb("raw", [P, 5, 512])
            vst = sb("vst", [P, NT, HD])
            sc_sb = sb("sc_sb", [P, NT, G, S])
            probs = sb("probs", [P, NT, G, P])
            smax = sb("smax", [P, NT, G])
            ssum = sb("ssum", [P, NT, G])
            rs = sb("rs", [P, NT, G])
            rs2 = sb("rs2", [P, NT, G, 2])
            bias = sb("bias", [P, G, S])
            sq = sb("sq", [P, HALF])
            kst = sb("kst", [P, NT, HD])
            junk = sb("junk", [P, HD])
            kss = sb("kss", [P, NT])
            kms = sb("kms", [P, NT])
            rk = sb("rk", [P, NT])
            qms = sb("qms", [P, NT, G])
            rq = sb("rq", [P, NT, G])
            norm_w = sb("norm_w", [P, 2])
            kfac = sb("kfac", [P, 1])

        with ExitStack() as sx:
            def sb(name, shape, dt=F32):
                return sx.enter_context(nc.sbuf_tensor(name, shape, dt))
            x_wraw = sb("x_wraw", [P, 2, XW])
            x_wh = sb("x_wh", [P, 2, XW], F32R)
            x_wl = sb("x_wl", [P, 2, XW], F32R)
            x_wv = sb("x_wv", [P, 4, S])
            x_wo = sb("x_wo", [P, 4, S])
            x_wos = sb("x_wos", [P, 4])
            x_woc = sb("x_woc", [P, 4, S])
            x_u = sb("x_u", [64, XH * S])
            x_bg = sb("x_bg", [P, 2])
            x_bc = sb("x_bc", [P, 1])
            x_blk = sb("x_blk", [P, P])
            x_eps = sb("x_eps", [P, 1])
            x_xh = sb("x_xh", [P, DM], F32R)
            x_xl = sb("x_xl", [P, DM], F32R)
            x_craw = sb("x_craw", [P, DM])
            x_ch = sb("x_ch", [P, DM], F32R)
            x_cl = sb("x_cl", [P, DM], F32R)
            x_ct = sb("x_ct", [P, KT, P])
            x_kmx = sb("x_kmx", [P, 8])
            x_knm = sb("x_knm", [P, 8])
            x_kz = sb("x_kz", [P, 8])
            x_krz = sb("x_krz", [P, 8])
            x_ek = sb("x_ek", [P, 2, 512])
            x_ekT = sb("x_ekT", [P, 2, 4, 512])
            x_e = sb("x_e", [P, 4, 512])
            x_qmx = sb("x_qmx", [P, 4, XH])
            x_qs = sb("x_qs", [P, 4, XH])
            x_qr = sb("x_qr", [P, 4, XH])
            x_en = sb("x_en", [P, 2, 512])
            x_q = sb("x_q", [P, 2, 4, 512])
            x_gt = sb("x_gt", [64, 2, 512])
            x_m = sb("x_m", [P, 4, 2, P])
            x_oc = sb("x_oc", [P, DM])
            x_sq = sb("x_sq", [P, DM])
            x_sd = sb("x_sd", [P, DM])
            x_rd = sb("x_rd", [P, DM])
            x_y = sb("x_y", [P, DM])
            x_r = sb("x_r", [P, DM])
            x_xn = sb("x_xn", [P, DM])

        with ExitStack() as sf:
            def sb(name, shape, dt=F32):
                return sf.enter_context(nc.sbuf_tensor(name, shape, dt))
            f_q = sb("f_q", [P, 3, 1024], I32)
            f_s = sb("f_s", [P, 3, 1024])
            f_w = sb("f_w", [P, 3, 1024])
            f_wh = sb("f_wh", [P, 3, 1024], F32R)
            f_wl = sb("f_wl", [P, 3, 1024], F32R)
            f_sg = sb("f_sg", [P, 2, HALF])
            f_it = sb("f_it", [P, 2, HALF])
            f_ih = sb("f_ih", [P, 2, TOK], F32R)
            f_il = sb("f_il", [P, 2, TOK], F32R)
            f_c = sb("f_c", [P, 2, TOK])

        with ExitStack() as sg:
            def sb(name, shape, dt=F32):
                return sg.enter_context(nc.sbuf_tensor(name, shape, dt))
            g_raw = sb("g_raw", [P, KT * DM + KT * GC + DM])
            g_h = sb("g_h", [P, KT * DM + KT * GC + DM], F32R)
            g_l = sb("g_l", [P, KT * DM + KT * GC + DM], F32R)
            g_bb = sb("g_bb", [P, DM])
            g_bt = sb("g_bt", [P, 1])
            g_hid = sb("g_hid", [P, NT, GC])
            g_mx = sb("g_mx", [P, NT])
            g_e = sb("g_e", [P, NT, 10])
            g_sum = sb("g_sum", [P, NT, 2])
            g_rec = sb("g_rec", [P, NT, 2])
            g_ad = sb("g_ad", [P, NT, E_])
            g_w = sb("g_w", [P, NT, E_])
            g_ws = sb("g_ws", [P, NT, 2])
            g_wr = sb("g_wr", [P, NT])
            g_wn = sb("g_wn", [P, NT, E_])
            g_z = sb("g_z", [P, NT, P])
            g_zh = sb("g_zh", [P, 2, P], F32R)
            g_zl = sb("g_zl", [P, 2, P], F32R)
            g_o = sb("g_o", [P, 2, DM])

        def f32(ap):
            return ap.bitcast(F32)

        def mm3(out, w, x, start, stop):
            (w_hi, w_lo), (x_hi, x_lo) = w, x
            nc.tensor.matmul(out, w_hi, x_hi, start=start, stop=False)
            nc.tensor.matmul(out, w_hi, x_lo, start=False, stop=False)
            return nc.tensor.matmul(out, w_lo, x_hi, start=False, stop=stop)

        def xtile(t):
            return X[:, t * DM:(t + 1) * DM] if isinstance(t, int) else X[:, bass.ds(t * DM, DM)]

        const_in = sem("const_in")
        const_set = sem("const_set")
        pool_passed = sem("pool_passed")
        dve_passed = sem("dve_passed")
        x_in = sem("x_in")
        xr_in = [sem("xr_in0"), sem("xr_in1")]
        x0_hi = sem("x0_hi")
        x0_ready = sem("x0_ready")

        ln_bn = sem("ln_bn")
        ln_ag = sem("ln_ag")
        ln_stat = sem("ln_stat")
        ln_rstd = sem("ln_rstd")
        ln_done = sem("ln_done")
        xt_done = sem("xt_done")
        xt_hi = sem("xt_hi")
        xt_ready = sem("xt_ready")
        LN_NORMS = {"attn0": 0, "xattn0": 1, "ffn0": 2, "attn1": 3, "xattn1": 4, "ffn1": 5}
        XT_NORMS = {"xattn0": 0, "ffn0": 1, "attn1": 2, "xattn1": 3}

        names = dict(
            proj_done=96,
            t_done=64,
            pv_done=64,
            wo_done=64,
            sc_done=64,
            proj_hi=80,
            pt_hi=64, o_hi=64,
            exp_done=64,
            wo_hi=32,
            proj_free=96,
            pt_ready=64, o_ready=64,
            wo_ready=32,
            x_added=64,
            s_out=64,
            s_max=64, s_sub=64, s_sum=64, s_inv=64, s_rec=64,
            w_hi=48, w_ready=48,
            v_hi=16, v_ready=16,
            p_ready=64,
        )
        A = {n: sem(n) for n in names}
        for n in ("q_sq", "k_ss", "k_ms", "k_rs", "k_nrm", "kt_done", "kt_hi", "kt_ready", "ss_done", "ss_out",
                  "q_rs", "s_msk", "kf_ready"):
            A[n] = sem(n)
        ld_w = [sem(f"ld_w{c}") for c in range(6)]
        ld_o = [sem(f"ld_o{c}") for c in range(4)]
        ld_b = sem("ld_b")

        xs = {n: sem("x_" + n) for n in (
            "w0", "w1", "w2", "wsp", "wos", "woc", "u", "u_out", "bm", "bc", "zero", "cin", "ctin", "xhi", "xsp", "chi",
            "csp", "k", "kmax", "kneg", "kexp", "kt", "ekt", "g", "gt", "m", "krz", "mr", "q", "qmax", "qsub", "qexp",
            "qsum", "qrec", "qn", "qt", "qcp", "out", "oc", "osq", "var", "sd", "rd", "y", "r", "xcp")}
        fs = {n: sem("f_" + n) for n in (
            "in0", "in1", "in2", "dq", "whi", "w", "gu", "sg", "it", "ihi", "i", "dn", "add", "cin", "chi", "c")}
        gs = {n: sem("g_" + n) for n in (
            "in", "hi", "w", "p1", "ev", "ch", "exp", "z", "zt", "zhi", "zr", "p2", "res", "out0", "out1")}

        def stage_end(name):
            return {"attn0": (A["x_added"], 64), "xattn0": (xs["xcp"], 8), "ffn0": (fs["add"], NF * NT),
                    "attn1": (A["x_added"], 128), "xattn1": (A["x_added"], 192)}[name]

        def dve_norm_stats(dve, name, t, src):
            n = 8 * LN_NORMS[name]
            nc.vector.bn_stats(st6[:, t, :], src).then_inc(ln_bn, 1)
            dve.wait_ge(ln_bn, n + t + 1)
            nc.vector.bn_aggr(mv[:, t, :], st6[:, t, :]).then_inc(ln_ag, 1)
            dve.wait_ge(ln_ag, n + t + 1)
            nc.vector.tensor_scalar(var_eps[:, t:t + 1], mv[:, t, 1:2], EPS, None, ALU.add).then_inc(ln_stat, 1)

        def pool_norm_root(pool, name, t):
            n = 8 * LN_NORMS[name]
            pool.wait_ge(ln_stat, n + t + 1)
            nc.gpsimd.tensor_tensor(rstd[:, t:t + 1], var_eps[:, t:t + 1], mhalf[:, 0:1],
                                    ALU.pow).then_inc(ln_rstd, 1)

        def dve_normalise(dve, name, t, src, dst):
            dve.wait_ge(ln_rstd, 8 * LN_NORMS[name] + t + 1)
            nc.vector.tensor_scalar(dst, src, mv[:, t, 0:1], rstd[:, t:t + 1],
                                    ALU.subtract, ALU.mult).then_inc(ln_done, 1)

        def pe_transpose_tile(pe, name, t, bank, free):
            n = 8 * XT_NORMS[name]
            pe.wait_ge(ln_done, 8 * LN_NORMS[name] + t + 1)
            wait(pe, *free) if t < 2 else pe.wait_ge(xt_ready, n + t - 1)
            for k in range(KT):
                last = nc.tensor.transpose(bank[:, k * P:(k + 1) * P], X[:, t * DM + k * P:t * DM + (k + 1) * P],
                                           ident[:, :])
            last.then_inc(xt_done, 1)

        def act_transpose_tile(act, name, t, bank):
            n = 8 * XT_NORMS[name]
            act.wait_ge(xt_done, n + t + 1)
            nc.scalar.activation(xTh[:, :, t * P:(t + 1) * P], bank[:, :].rearrange("p (k n) -> p k n", k=KT),
                                 ACT.Copy).then_inc(xt_hi, 1)

        def dve_transpose_tile(dve, name, t, bank):
            n = 8 * XT_NORMS[name]
            dve.wait_ge(xt_hi, n + t + 1)
            nc.vector.tensor_tensor(xTl[:, :, t * P:(t + 1) * P], bank[:, :].rearrange("p (k n) -> p k n", k=KT),
                                    f32(xTh[:, :, t * P:(t + 1) * P]), ALU.subtract).then_inc(xt_ready, 1)

        class Stage:
            def __init__(self, name, index, rms, before, w_in, w_out, bias_in, per_head_bias, scale):
                self.name, self.index, self.rms, self.before = name, index, rms, before
                self.w_in, self.w_out, self.bias_in = w_in, w_out, bias_in
                self.per_head_bias, self.scale = per_head_bias, scale
                self.units = units(rms)
                self.k_c, self.v_c, self.q_c = (0, 1, 2) if rms else (0, 5, 1)
                self.src = cT if rms else xT

            def chunk_of(self, u):
                kind, g, _ = self.units[u]
                return {"k": self.k_c, "v": self.v_c, "kv": self.v_c, "q": self.q_c + g}[kind]

            def last_unit_of(self, c):
                if self.rms and c < 2:
                    return 3
                return max(u for u in range(12) if self.chunk_of(u) == c)

            def at(self, name, n):
                return A[name], names.get(name, 0) * self.index + n

            def need(self, eng, name, n):
                if isinstance(n, int) and n <= 0:
                    return
                eng.wait_ge(*self.at(name, n))

        stages = [
            Stage("attn0", 0, False, None, a["a0_in"], a["a0_out"], a["causal"], False, HD ** -0.5),
            Stage("attn1", 1, False, "ffn0", a["a1_in"], a["a1_out"], a["alibi"], True, HD ** -0.5),
            Stage("xattn1", 2, True, "attn1", a["a2_in"], a["a2_out"], a["mask"], False, 1.0),
        ]

        def hn(ap4, g, n):
            return ap4[:, 4 * n:4 * n + 4, g]

        def sp_attention(sp, st):
            def load_w(i, c, slot):
                src = st.w_in[i, c] if isinstance(i, int) else \
                    st.w_in[bass.ds(i, 1), c].rearrange("o p n -> p (o n)")
                sp.dma_start(raw[:, slot, :], src).then_inc(ld_w[c], 16)

            def load_o(i, c, slot):
                src = st.w_out[i, c] if isinstance(i, int) else \
                    st.w_out[bass.ds(i, 1), c].rearrange("o p n -> p (o n)")
                sp.dma_start(raw[:, slot, :], src).then_inc(ld_o[c], 16)

            def load_bias(i):
                if st.per_head_bias:
                    src = st.bias_in[i] if isinstance(i, int) else \
                        st.bias_in[bass.ds(i, 1)].rearrange("o p n -> p (o n)")
                    st.need(sp, "s_msk" if st.rms else "s_out", 8 * i)
                    sp.dma_start(bias[:, :, :].rearrange("p g s -> p (g s)"), src).then_inc(ld_b, 16)

            if st.before:
                sp.wait_ge(*stage_end(st.before))
            if not st.per_head_bias:
                sp.dma_start(bias[:, 0, :], st.bias_in).then_inc(ld_b, 16)
            if st.rms:
                sp.dma_start(norm_w[:, :], a["norm_w"]).then_inc(const_in, 16)
            for c in range(5):
                load_w(0, c, c)
            load_bias(0)
            st.need(sp, "w_ready", 5)
            load_w(0, 5, 4)

            def step(i, more):
                if more:
                    for c in range(5):
                        if c < 4:
                            st.need(sp, "wo_ready", 4 * (i - 1) + c + 1)
                        else:
                            st.need(sp, "w_ready", 6 * i + 6)
                        load_w(i + 1, c, c)
                for c in range(4):
                    if more:
                        st.need(sp, "w_ready", 6 * (i + 1) + c + 1)
                    else:
                        st.need(sp, "wo_ready", 4 * (i - 1) + c + 1)
                    load_o(i, c, c)
                if more:
                    load_bias(i + 1)
                    st.need(sp, "w_ready", 6 * (i + 1) + 5)
                    load_w(i + 1, 5, 4)

            step(0, True)
            with sp.Fori(1, NKV - 1) as i:
                step(i, True)
            step(NKV - 1, False)

        def pe_attention(pe, st):
            def unit(i, u):
                kind, g, n = st.units[u]
                c = st.chunk_of(u)
                st.need(pe, "w_ready", 6 * i + c + 1)
                st.need(pe, "proj_free", 12 * i + u - 1)
                bank = pb[u % 2]
                w = lambda k: (wh[:, c, k, :], wl[:, c, k, :])
                if kind in "kq":
                    cols = slice(n * HALF, (n + 1) * HALF)
                    for k in range(KT):
                        last = mm3(bank[:, :], w(k), (xTh[:, k, cols], xTl[:, k, cols]), k == 0, k == KT - 1)
                elif kind == "v":
                    for m in range(4):
                        t = 4 * n + m
                        for k in range(KT):
                            last = mm3(bank[:, m * HD:(m + 1) * HD],
                                       (xTh[:, k, t * P:(t + 1) * P], xTl[:, k, t * P:(t + 1) * P]), w(k),
                                       k == 0, k == KT - 1)
                else:
                    for m in range(2):
                        t = 2 * n + m
                        for k in range(KT):
                            last = mm3(bank[:, 2 * m * HD:2 * (m + 1) * HD],
                                       (cTh[:, k, t * P:(t + 1) * P], cTl[:, k, t * P:(t + 1) * P]),
                                       (wh[:, 0:2, k, :], wl[:, 0:2, k, :]), k == 0, k == KT - 1)
                last.then_inc(A["proj_done"], 1)

            def scores(i, j):
                g, n = j // 2, j % 2
                u = (4 if st.rms else 2) + j
                st.need(pe, "proj_free", 12 * i + u + 1)
                if st.rms:
                    st.need(pe, "kt_ready", 2 * i + 2)
                st.need(pe, "s_out", 8 * i + j - 1)
                bank = pb[2 + j % 2]
                for m in range(4):
                    t = 4 * n + m
                    last = mm3(bank[:, m * P:(m + 1) * P],
                               (qh[:, j % 2, m * P:(m + 1) * P], ql[:, j % 2, m * P:(m + 1) * P]),
                               (kh[:, t * P:(t + 1) * P], kl[:, t * P:(t + 1) * P]), True, True)
                last.then_inc(A["sc_done"], 1)

            def square_sums(i, j):
                st.need(pe, "q_sq", 8 * i + j + 1)
                st.need(pe, "ss_out", 8 * i + j)
                for m in range(4):
                    last = nc.tensor.matmul(pb[7][:, m:m + 1], sq[:, m * P:(m + 1) * P], onecol[:, :],
                                            start=True, stop=True)
                last.then_inc(A["ss_done"], 1)

            def transpose_k(i, n):
                st.need(pe, "k_nrm", 4 * i + 2 * n + 2)
                st.need(pe, "s_out", 8 * i)
                for m in range(4):
                    last = nc.tensor.transpose(pb[2 + n][:, m * P:(m + 1) * P], kst[:, 4 * n + m, :], ident[:, :])
                last.then_inc(A["kt_done"], 1)

            def transpose_probs(i, t):
                st.need(pe, "p_ready", 8 * i + t + 1)
                st.need(pe, "pt_ready", 8 * i + t)
                for g in range(G):
                    last = nc.tensor.transpose(pb[4][:, g * P:(g + 1) * P], probs[:, t, g, :], ident[:, :])
                last.then_inc(A["t_done"], 1)

            def probs_v(i, t):
                st.need(pe, "pt_ready", 8 * i + t + 1)
                st.need(pe, "v_ready", 2 * i + 1 + t // 4)
                st.need(pe, "o_ready", 8 * i + t)
                mm3(pb[5][:, :], (vh[:, t, :], vl[:, t, :]), (pth[:, :], ptl[:, :]), True,
                    True).then_inc(A["pv_done"], 1)

            def project_out(i, t):
                st.need(pe, "o_ready", 8 * i + t + 1)
                st.need(pe, "wo_ready", 4 * i + 4)
                st.need(pe, "x_added", 8 * i + t)
                for g in range(G):
                    last = mm3(pb[6][:, :], (oth[:, g * P:(g + 1) * P], otl[:, g * P:(g + 1) * P]),
                               (woh[:, g, :], wol[:, g, :]), g == 0, g == G - 1)
                last.then_inc(A["wo_done"], 1)

            def run(i, events):
                for kind, n in events:
                    if kind == "U":
                        unit(i, n)
                    elif kind == "SC":
                        scores(i, n)
                    elif kind == "SQ":
                        square_sums(i, n)
                    elif kind == "KT":
                        transpose_k(i, n)
                    elif kind == "T":
                        transpose_probs(i - 1, n)
                    elif kind == "PV":
                        probs_v(i - 1, n)
                    elif kind == "WO":
                        project_out(i - 1, n)

            if st.name == "attn0":
                pe.wait_ge(const_in, 32)
                pe.wait_ge(x0_ready, 2)
            else:
                pe.wait_ge(const_set, 2)
                pe.wait_ge(xt_ready, 8 * (2 if st.name == "attn1" else 3))
            if st.rms:
                pe.wait_ge(fs["c"], 4)
            run(0, schedule(st.rms, True, False))
            with pe.Fori(1, NKV) as i:
                run(i, schedule(st.rms, True, True))
            i = NKV
            for kind, t in schedule(st.rms, False, True):
                run(i, [(kind, t)])
                if kind == "PV" and t >= 2 and st.name != "attn0":
                    pe_transpose_tile(pe, st.name, t - 2, pb[t % 2], st.at("proj_free", 96))
            if st.name != "attn0":
                for t in (NT - 2, NT - 1):
                    pe_transpose_tile(pe, st.name, t, pb[t % 2], st.at("proj_free", 96))

        def act_attention(act, st):
            def unit(i, u):
                kind, g, n = st.units[u]
                if kind == "v":
                    return
                if kind == "kv":
                    for m in range(2):
                        st.need(act, "k_ss", 8 * i + 2 * n + m)
                        st.need(act, "proj_free", 12 * i + u + 1)
                        st.need(act, "k_ms", 4 * (i - 1) + n + 1)
                        nc.scalar.activation(junk[:, :], kst[:, 2 * n + m, :], ACT.Square,
                                             accum_out=kss[:, 2 * n + m:2 * n + m + 1]).then_inc(A["k_ss"], 1)
                    return
                st.need(act, "proj_done", 12 * i + u + 1)
                if st.rms:
                    j = u - 4
                    st.need(act, "ss_done", 8 * i + j)
                    nc.scalar.activation(sq[:, :], pb[u % 2][:, :], ACT.Square).then_inc(A["q_sq"], 1)
                if kind == "k":
                    dst = kh[:, n * HALF:(n + 1) * HALF]
                else:
                    dst = qh[:, (2 * g + n) % 2, :]
                nc.scalar.activation(dst, pb[u % 2][:, :], ACT.Copy).then_inc(A["proj_hi"], 1)

            def k_high(i, n):
                st.need(act, "kt_done", 2 * i + n + 1)
                st.need(act, "kf_ready", 1)
                nc.scalar.activation(kh[:, n * HALF:(n + 1) * HALF], pb[2 + n][:, :], ACT.Copy,
                                     scale=kfac[:, 0:1]).then_inc(A["kt_hi"], 1)

            def exponentials(i, j):
                g, n = j // 2, j % 2
                st.need(act, "s_sub", 8 * i + j + 1)
                nc.scalar.activation(hn(sc_sb, g, n), hn(sc_sb, g, n), ACT.Exp).then_inc(A["exp_done"], 1)

            def run(i, events):
                for kind, n in events:
                    if kind == "U":
                        unit(i, n)
                    elif kind == "KT":
                        k_high(i, n)
                    elif kind == "SC":
                        exponentials(i, n)
                    elif kind == "T":
                        st.need(act, "t_done", 8 * (i - 1) + n + 1)
                        nc.scalar.activation(pth[:, :], pb[4][:, :], ACT.Copy).then_inc(A["pt_hi"], 1)
                    elif kind == "PV":
                        st.need(act, "pv_done", 8 * (i - 1) + n + 1)
                        nc.scalar.activation(oth[:, :], pb[5][:, :], ACT.Copy).then_inc(A["o_hi"], 1)
                    elif kind == "WS":
                        st.need(act, "wo_done", 8 * i)
                        for c in range(G):
                            act.wait_ge(ld_o[c], 16 * (NKV * st.index + i + 1))
                            nc.scalar.activation(woh[:, c, :], raw[:, c, :], ACT.Copy).then_inc(A["wo_hi"], 1)

            if st.before:
                act.wait_ge(*stage_end(st.before))
            lag = 3 if st.rms else 1
            run(0, later(schedule(st.rms, True, False), ("SC",), lag))
            with act.Fori(1, NKV) as i:
                run(i, later(schedule(st.rms, True, True), ("SC",), lag))
            for kind, t in schedule(st.rms, False, True):
                run(NKV, [(kind, t)])
                if kind == "PV" and t >= 2 and st.name != "attn0":
                    act_transpose_tile(act, st.name, t - 2, pb[t % 2])
            if st.name != "attn0":
                for t in (NT - 2, NT - 1):
                    act_transpose_tile(act, st.name, t, pb[t % 2])

        def dve_attention(dve, st):
            def unit(i, u):
                kind, g, n = st.units[u]
                bank = pb[u % 2]
                if kind == "v":
                    st.need(dve, "proj_done", 12 * i + u + 1)
                    st.need(dve, "v_ready", 2 * (i - 1) + n + 1)
                    nc.vector.tensor_copy(vst[:, 4 * n:4 * n + 4, :],
                                          bank[:, :].rearrange("p (t d) -> p t d", t=4)).then_inc(A["proj_free"], 1)
                    return
                if kind == "kv":
                    st.need(dve, "proj_done", 12 * i + u + 1)
                    st.need(dve, "v_ready", 2 * (i - 1) + n // 2 + 1)
                    kv = bank[:, :].rearrange("p (t c d) -> p t c d", t=2, c=2)
                    nc.vector.tensor_copy(kst[:, 2 * n:2 * n + 2, :], kv[:, :, 0, :])
                    nc.vector.tensor_copy(vst[:, 2 * n:2 * n + 2, :], kv[:, :, 1, :]).then_inc(A["proj_free"], 1)
                    return
                j = u - (4 if st.rms else 0)
                st.need(dve, "proj_hi", (8 if st.rms else 10) * i + j + 1)
                if kind == "k":
                    hi, lo = kh[:, n * HALF:(n + 1) * HALF], kl[:, n * HALF:(n + 1) * HALF]
                else:
                    hi, lo = qh[:, (2 * g + n) % 2, :], ql[:, (2 * g + n) % 2, :]
                nc.vector.tensor_tensor(lo, bank[:, :], f32(hi), ALU.subtract).then_inc(A["proj_free"], 1)

            def k_mean_square(i, n):
                st.need(dve, "k_ss", 8 * i + 2 * n + 2)
                nc.vector.tensor_scalar(kms[:, 2 * n:2 * n + 2], kss[:, 2 * n:2 * n + 2], 1.0 / HD, EPS,
                                        ALU.mult, ALU.add).then_inc(A["k_ms"], 1)

            def k_normalise(i, n):
                st.need(dve, "k_rs", 4 * i + n + 1)
                for m in range(2):
                    t = 2 * n + m
                    last = nc.vector.tensor_scalar(kst[:, t, :], kst[:, t, :], rk[:, t:t + 1], None, ALU.mult)
                last.then_inc(A["k_nrm"], 1)

            def k_low(i, n):
                st.need(dve, "kt_hi", 2 * i + n + 1)
                cols = slice(n * HALF, (n + 1) * HALF)
                nc.vector.scalar_tensor_tensor(kl[:, cols], pb[2 + n][:, :], kfac[:, 0:1], f32(kh[:, cols]),
                                               ALU.mult, ALU.subtract).then_inc(A["kt_ready"], 1)

            def q_mean_square(i, j):
                g, n = j // 2, j % 2
                st.need(dve, "ss_done", 8 * i + j + 1)
                st.need(dve, "q_rs", 8 * (i - 1) + j + 1)
                nc.vector.tensor_scalar(qms[:, 4 * n:4 * n + 4, g], pb[7][:, 0:4], 1.0 / HD, EPS,
                                        ALU.mult, ALU.add).then_inc(A["ss_out"], 1)

            def scores(i, j):
                g, n = j // 2, j % 2
                bank = pb[2 + j % 2][:, :].rearrange("p (t s) -> p t s", t=4)
                dst = hn(sc_sb, g, n)
                st.need(dve, "sc_done", 8 * i + j + 1)
                st.need(dve, "p_ready", 8 * i)
                if st.per_head_bias:
                    dve.wait_ge(ld_b, 16 * (1 + i + 1))
                else:
                    dve.wait_ge(ld_b, 16 * (1 if st.index == 0 else 10))
                b = bias[:, g if st.per_head_bias else 0, :].rearrange("p (o s) -> p o s", o=1)
                if st.rms:
                    st.need(dve, "q_rs", 8 * i + j + 1)
                for h in range(2):
                    p0, p1 = 64 * h, 64 * h + 64
                    if st.rms:
                        last = nc.vector.tensor_tensor(
                            dst[p0:p1], bank[p0:p1, :, p0:p1],
                            hn(rq, g, n)[p0:p1].rearrange("p (t o) -> p t o", o=1).to_broadcast([64, 4, S]), ALU.mult)
                    else:
                        last = nc.vector.scalar_tensor_tensor(
                            dst[p0:p1], bank[p0:p1, :, p0:p1], st.scale, b[p0:p1].to_broadcast([64, 4, S]),
                            ALU.mult, ALU.add)
                last.then_inc(A["s_out"], 1)
                st.need(dve, "s_out", 8 * i + j + 1)
                if st.rms:
                    nc.vector.tensor_tensor(dst, dst, b.to_broadcast([P, 4, S]), ALU.add).then_inc(A["s_msk"], 1)
                    st.need(dve, "s_msk", 8 * i + j + 1)
                nc.vector.tensor_reduce(hn(smax, g, n), dst, AX_X, ALU.max).then_inc(A["s_max"], 1)
                st.need(dve, "s_max", 8 * i + j + 1)
                nc.vector.tensor_tensor(
                    dst, dst, hn(smax, g, n).rearrange("p (t o) -> p t o", o=1).to_broadcast([P, 4, S]),
                    ALU.subtract).then_inc(A["s_sub"], 1)

            def sums(i, j):
                g, n = j // 2, j % 2
                st.need(dve, "exp_done", 8 * i + j + 1)
                nc.vector.tensor_reduce(hn(ssum, g, n), hn(sc_sb, g, n), AX_X, ALU.add).then_inc(A["s_sum"], 1)
                st.need(dve, "s_sum", 8 * i + j + 1)
                nc.vector.reciprocal(hn(rs, g, n), hn(ssum, g, n)).then_inc(A["s_inv"], 1)
                st.need(dve, "s_inv", 8 * i + j + 1)
                nc.vector.tensor_tensor(
                    hn(rs2, g, n), hn(rs, g, n).rearrange("p (t o) -> p t o", o=1).to_broadcast([P, 4, 2]),
                    own_half[:, :].rearrange("p (o c) -> p o c", o=1).to_broadcast([P, 4, 2]),
                    ALU.mult).then_inc(A["s_rec"], 1)

            def run(i, events):
                for kind, n in events:
                    if kind == "U":
                        unit(i, n)
                        if st.rms and n < 4:
                            k_mean_square(i, n)
                            if n >= 1:
                                k_normalise(i, n - 1)
                            if n == 3:
                                k_normalise(i, 3)
                    elif kind == "KT":
                        k_low(i, n)
                    elif kind == "SQ":
                        q_mean_square(i, n)
                    elif kind == "SC":
                        scores(i, n)
                    elif kind == "SUM":
                        sums(i, n)
                    elif kind == "T":
                        st.need(dve, "pt_hi", 8 * (i - 1) + n + 1)
                        nc.vector.tensor_tensor(ptl[:, :], pb[4][:, :], f32(pth[:, :]),
                                                ALU.subtract).then_inc(A["pt_ready"], 1)
                    elif kind == "PV":
                        st.need(dve, "o_hi", 8 * (i - 1) + n + 1)
                        nc.vector.tensor_tensor(otl[:, :], pb[5][:, :], f32(oth[:, :]),
                                                ALU.subtract).then_inc(A["o_ready"], 1)
                    elif kind == "WO":
                        st.need(dve, "wo_done", 8 * (i - 1) + n + 1)
                        nc.vector.tensor_tensor(xtile(n), pb[6][:, :], xtile(n), ALU.add).then_inc(A["x_added"], 1)
                    elif kind == "WS":
                        for c in range(G):
                            st.need(dve, "wo_hi", 4 * i + c + 1)
                            nc.vector.tensor_tensor(wol[:, c, :], raw[:, c, :], f32(woh[:, c, :]),
                                                    ALU.subtract).then_inc(A["wo_ready"], 1)

            def order(project, attend):
                ev = schedule(st.rms, project, attend)
                ev = later(ev, ("SC",), 2 if st.rms else 0) if st.rms else ev
                both = []
                for e in ev:
                    both.append(e)
                    if e[0] == "SC":
                        both.append(("SUM", e[1]))
                return later(both, ("SUM",), 3 if st.rms else 2)

            if st.before:
                dve.wait_ge(*stage_end(st.before))
            else:
                dve.wait_ge(x_in, 16)
                dve.wait_ge(const_in, 32)
            if st.rms:
                dve.wait_ge(const_in, 16 * 3)
                nc.vector.scalar_tensor_tensor(kfac[:, :], norm_w[:, 0:1], HD ** -0.5, norm_w[:, 1:2],
                                               ALU.mult, ALU.mult).then_inc(A["kf_ready"], 1)
                dve.wait_ge(A["kf_ready"], 1)
            run(0, order(True, False))
            with dve.Fori(1, NKV) as i:
                run(i, order(True, True))
            for kind, t in schedule(st.rms, False, True):
                run(NKV, [(kind, t)])
                if kind == "WO":
                    st.need(dve, "x_added", 56 + t + 1)
                    dve_norm_stats(dve, st.name, t, xtile(t))
                    if t >= 1:
                        dve_normalise(dve, st.name, t - 1, xtile(t - 1), xtile(t - 1))
                if kind == "PV" and t >= 2 and st.name != "attn0":
                    dve_transpose_tile(dve, st.name, t - 2, pb[t % 2])
            dve_normalise(dve, st.name, NT - 1, xtile(NT - 1), xtile(NT - 1))
            if st.name != "attn0":
                for t in (NT - 2, NT - 1):
                    dve_transpose_tile(dve, st.name, t, pb[t % 2])

        def pool_attention(pool, st):
            def split_chunk(i, c):
                slot = c if c < 5 else 4
                pool.wait_ge(ld_w[c], 16 * (NKV * st.index + i + 1))
                st.need(pool, "proj_done", 12 * (i - 1) + st.last_unit_of(c) + 1)
                src = raw[:, slot, :]
                hi, lo = (w[:, c].rearrange("p k n -> p (k n)") for w in (wh, wl))
                carry_waits(pool, pool_passed)
                nc.gpsimd.tensor_scalar(hi, src, 1.0, 0.0, ALU.mult, ALU.add).then_inc(A["w_hi"], 1)
                st.need(pool, "w_hi", 6 * i + c + 1)
                nc.gpsimd.tensor_tensor(lo, src, f32(hi), ALU.subtract).then_inc(A["w_ready"], 1)

            def split_v(i, n):
                done = (2 * n + 2) if st.rms else (11 + n)
                st.need(pool, "proj_free", 12 * i + done)
                st.need(pool, "pv_done", 8 * (i - 1) + 4 * n + 4)
                hi, lo, src = vh[:, 4 * n:4 * n + 4, :], vl[:, 4 * n:4 * n + 4, :], vst[:, 4 * n:4 * n + 4, :]
                carry_waits(pool, pool_passed)
                nc.gpsimd.tensor_scalar(hi, src, 1.0, 0.0, ALU.mult, ALU.add).then_inc(A["v_hi"], 1)
                st.need(pool, "v_hi", 2 * i + n + 1)
                nc.gpsimd.tensor_tensor(lo, src, f32(hi), ALU.subtract).then_inc(A["v_ready"], 1)

            def normalise(i, t):
                st.need(pool, "s_rec", 8 * i + (7 if t < 4 else 8))
                st.need(pool, "t_done", 8 * (i - 1) + t + 1)
                nc.gpsimd.tensor_tensor(
                    probs[:, t, :, :].rearrange("p g (c s) -> p g c s", c=2),
                    sc_sb[:, t, :, :].rearrange("p g (o s) -> p g o s", o=1).to_broadcast([P, G, 2, S]),
                    rs2[:, t, :, :].rearrange("p g (c o) -> p g c o", o=1).to_broadcast([P, G, 2, S]),
                    ALU.mult).then_inc(A["p_ready"], 1)

            def k_root(i, n):
                st.need(pool, "k_ms", 4 * i + n + 1)
                nc.gpsimd.tensor_tensor(rk[:, 2 * n:2 * n + 2], kms[:, 2 * n:2 * n + 2], mhalf[:, 0:2],
                                        ALU.pow).then_inc(A["k_rs"], 1)

            def q_root(i, j):
                g, n = j // 2, j % 2
                st.need(pool, "ss_out", 8 * i + j + 1)
                nc.gpsimd.tensor_tensor(hn(rq, g, n), hn(qms, g, n), mhalf[:, 0:4], ALU.pow).then_inc(A["q_rs"], 1)

            def step(i, more):
                if st.rms:
                    for n in range(4):
                        k_root(i, n)
                    if more:
                        split_chunk(i + 1, 0)
                        split_chunk(i + 1, 1)
                    for j in range(8):
                        q_root(i, j)
                        if more and j % 2 and j < 6:
                            split_chunk(i + 1, 2 + j // 2)
                    split_v(i, 0)
                    for t in range(4):
                        normalise(i, t)
                    split_v(i, 1)
                    for t in range(4, NT):
                        normalise(i, t)
                    if more:
                        split_chunk(i + 1, 5)
                else:
                    if more:
                        for c in range(5):
                            split_chunk(i + 1, c)
                    split_v(i, 0)
                    for t in range(4):
                        normalise(i, t)
                    split_v(i, 1)
                    for t in range(4, NT):
                        normalise(i, t)
                    if more:
                        split_chunk(i + 1, 5)

            if st.before:
                pool.wait_ge(*stage_end(st.before))
            for c in range(2):
                split_chunk(0, c)
            if not st.before:
                pool.wait_ge(x0_ready, 2)
            for c in range(2, 6):
                split_chunk(0, c)
            step(0, True)
            with pool.Fori(1, NKV - 1) as i:
                step(i, True)
            step(NKV - 1, False)
            for t in range(NT):
                pool_norm_root(pool, st.name, t)

        XB = dict(k=pb[0], q=(pb[1], pb[2]), kt=pb[3], qt=pb[4], gm=pb[5], out=pb[6], post=pb[7])

        def sp_xattn(sp):
            sp.wait_ge(*stage_end("attn0"))
            sp.dma_start(x_wraw[:, :, :], a["x_wqk"]).then_inc(xs["w0"], 16)
            sp.dma_start(x_wv[:, :, :], a["x_wv"]).then_inc(xs["w1"], 16)
            sp.dma_start(x_wo[:, :, :], a["x_wo"]).then_inc(xs["w1"], 16)
            sp.dma_start(x_bg[:, :], a["x_bg"]).then_inc(xs["w2"], 16)
            sp.dma_start(x_blk[:, :], a["x_blk"]).then_inc(xs["w2"], 16)

            def load(p):
                wait(sp, xs["csp"], p)
                src = a["ctx"][p] if isinstance(p, int) else a["ctx"][bass.ds(p, 1)].rearrange("o p n -> p (o n)")
                sp.dma_start(x_craw[:, :], src).then_inc(xs["cin"], 16)
                wait(sp, xs["g"], 2 * p)
                src = a["ctxT_pair"][p] if isinstance(p, int) else \
                    a["ctxT_pair"][bass.ds(p, 1)].rearrange("o p n -> p (o n)")
                sp.dma_start(x_ct[:, :, :].rearrange("p k n -> p (k n)"), src).then_inc(xs["ctin"], 16)
            load(0)
            with sp.Fori(1, NT) as p:
                load(p)

        def x_steps(p, project, post):
            ev = []
            if project:
                for u in range(8):
                    ev += [("K", u), ("Q", u)]
                    if u >= 1:
                        ev.append(("KT", u - 1))
                    if u >= 2:
                        ev.append(("QT", u - 2))
                    if u == 1 and post:
                        ev.append(("VAR", 0))
                    if u == 4:
                        ev += [("G", 0)]
                    if u == 5:
                        ev += [("M", 0)]
                    if u == 5 and post:
                        ev.append(("XT", 0))
                    if u == 6:
                        ev += [("OUT", 0)]
                ev += [("KT", 7), ("QT", 6), ("G", 1), ("QT", 7), ("M", 1), ("OUT", 1)]
            else:
                ev = [("VAR", 0), ("XT", 0)]
            return ev

        def pe_xattn(pe):
            pe.wait_ge(xs["woc"], 1)
            for h in range(XH):
                r0 = 64 * (h % 2)
                last = nc.tensor.matmul(pb[5 + h % 2][0:64, (h // 2) * S:(h // 2 + 1) * S], x_wv[r0:r0 + 64, h // 2, :],
                                        x_woc[r0:r0 + 64, h // 2, :], start=True, stop=True)
            last.then_inc(xs["u"], 1)
            pe.wait_ge(xs["w2"], 32)
            nc.tensor.matmul(pb[7][:, 0:1], x_blk[:, :], x_bg[:, 0:1], start=True, stop=True).then_inc(xs["bm"], 1)
            pe.wait_ge(xs["wsp"], 1)
            pe.wait_ge(xs["u_out"], 1)
            pe.wait_ge(xs["bc"], 1)
            pe.wait_ge(xs["zero"], 1)

            def run(p, events):
                for kind, u in events:
                    b, s = u // 4, u % 4
                    r = slice(64 * b, 64 * b + 64)
                    if kind == "K":
                        if u == 0:
                            wait(pe, xs["csp"], p + 1)
                        wait(pe, xs["kexp"], 8 * p + u)
                        cols = slice(s * P, (s + 1) * P)
                        mm3(XB["k"][:, :], (x_wh[r, 1, cols], x_wl[r, 1, cols]), (x_ch[r, :], x_cl[r, :]), True,
                            True).then_inc(xs["k"], 1)
                    elif kind == "Q":
                        if u == 0:
                            wait(pe, xs["xsp"], p + 1)
                        wait(pe, xs["qsub"], 8 * p + u - 1)
                        cols = slice(s * P, (s + 1) * P)
                        mm3(XB["q"][u % 2][:, :], (x_xh[r, cols], x_xl[r, cols]), (x_wh[r, 0, :], x_wl[r, 0, :]), True,
                            True).then_inc(xs["q"], 1)
                    elif kind == "KT":
                        wait(pe, xs["kexp"], 8 * p + u + 1)
                        wait(pe, xs["ekt"], 8 * p + u)
                        for n in range(4):
                            last = nc.tensor.transpose(XB["kt"][:, n * P:(n + 1) * P],
                                                       x_ek[:, u % 2, n * P:(n + 1) * P], ident[:, :])
                        last.then_inc(xs["kt"], 1)
                    elif kind == "QT":
                        wait(pe, xs["qn"], 8 * p + u + 1)
                        wait(pe, xs["qcp"], 8 * p + u)
                        for n in range(4):
                            last = nc.tensor.transpose(XB["qt"][:, n * P:(n + 1) * P],
                                                       x_en[:, u % 2, n * P:(n + 1) * P], ident[:, :])
                        last.then_inc(xs["qt"], 1)
                    elif kind == "G":
                        wait(pe, xs["ekt"], 8 * p + 4 * u + 4)
                        wait(pe, xs["ctin"], 16 * (p + 1))
                        wait(pe, xs["mr"], 2 * p + u)
                        for n in range(4):
                            last = nc.tensor.matmul(XB["gm"][0:64, :], x_ct[:, n, 64 * u:64 * u + 64],
                                                    x_ekT[:, u, n, :], start=n == 0, stop=n == 3)
                        last.then_inc(xs["g"], 1)
                    elif kind == "M":
                        wait(pe, xs["gt"], 2 * p + u + 1)
                        for n in range(4):
                            last = nc.tensor.matmul(XB["gm"][:, n * P:(n + 1) * P], x_gt[0:64, u, n * P:(n + 1) * P],
                                                    x_u[0:64, n * P:(n + 1) * P], start=True, stop=True)
                        last.then_inc(xs["m"], 1)
                    elif kind == "OUT":
                        wait(pe, xs["mr"], 2 * p + u + 1)
                        wait(pe, xs["qcp"], 8 * p + 4 * u + 4)
                        wait(pe, xs["osq"], p)
                        for n in range(4):
                            last = nc.tensor.matmul(XB["out"][:, :], x_m[:, n, u, :], x_q[:, u, n, :],
                                                    start=(u == 0 and n == 0), stop=(u == 1 and n == 3))
                        last.then_inc(xs["out"], 1)
                    elif kind == "VAR":
                        wait(pe, xs["osq"], p)
                        wait(pe, xt_ready, p - 1)
                        nc.tensor.matmul(XB["post"][:, :], x_blk[:, :], x_sq[:, :], start=True,
                                         stop=True).then_inc(xs["var"], 1)
                    elif kind == "XT":
                        wait(pe, ln_done, 8 + p)
                        wait(pe, xs["sd"], p)
                        for k in range(KT):
                            last = nc.tensor.transpose(XB["post"][:, k * P:(k + 1) * P], x_xn[:, k * P:(k + 1) * P],
                                                       ident[:, :])
                        last.then_inc(xt_done, 1)
            run(0, x_steps(0, True, False))
            with pe.Fori(1, NT) as p:
                run(p, x_steps(p, True, True))
            run(NT, x_steps(NT, False, True))

        def x_order(p, project, post):
            ev = x_steps(p, project, post)
            out = []
            if project and post:
                out.append(("OC", 0))
            for e in ev:
                out.append(e)
            if not project:
                out = [("OC", 0)] + out
            return out

        def act_xattn(act):
            act.wait_ge(*stage_end("attn0"))
            act.wait_ge(xs["w0"], 16)
            nc.scalar.activation(x_wh[:, :, :], x_wraw[:, :, :], ACT.Copy).then_inc(xs["chi"], 1)
            act.wait_ge(xs["u"], 1)
            for h in range(2):
                last = nc.scalar.activation(
                    x_u[0:64, :].rearrange("p (k c o) -> p k c o", k=4, c=2)[:, :, h, :],
                    pb[5 + h][0:64, 0:4 * S].rearrange("p (k o) -> p k o", k=4), ACT.Copy)
            last.then_inc(xs["u_out"], 1)
            act.wait_ge(xs["bc"], 1)

            def run(p, events):
                for kind, u in events:
                    b, s = u // 4, u % 4
                    if kind == "K":
                        if u == 0:
                            wait(act, xs["cin"], 16 * (p + 1))
                            wait(act, xs["k"], 8 * p)
                            nc.scalar.activation(x_ch[:, :], x_craw[:, :], ACT.Copy).then_inc(xs["chi"], 1)
                            if isinstance(p, int):
                                act.wait_ge(ln_done, 8)
                            wait(act, xs["q"], 8 * p)
                            nc.scalar.activation(x_xh[:, :], xtile(p), ACT.Copy).then_inc(xs["xhi"], 1)
                        wait(act, xs["kneg"], 8 * p + u + 1)
                        wait(act, xs["kt"], 8 * p + u - 1)
                        wait(act, xs["krz"], 2 * (p - 1) + b + 1)
                        nc.scalar.activation(x_ek[:, u % 2, :], XB["k"][:, :], ACT.Exp, bias=x_knm[:, u:u + 1],
                                             accum_out=x_kz[:, u:u + 1]).then_inc(xs["kexp"], 1)
                    elif kind == "Q":
                        wait(act, xs["qsub"], 8 * p + u + 1)
                        nc.scalar.activation(x_e[:, s, :], x_e[:, s, :], ACT.Exp).then_inc(xs["qexp"], 1)
                    elif kind == "KT":
                        wait(act, xs["kt"], 8 * p + u + 1)
                        wait(act, xs["g"], 2 * (p - 1) + b + 1)
                        nc.scalar.activation(x_ekT[:, b, :, s * P:(s + 1) * P],
                                             XB["kt"][:, :].rearrange("p (n d) -> p n d", n=4),
                                             ACT.Copy).then_inc(xs["ekt"], 1)
                    elif kind == "QT":
                        wait(act, xs["qt"], 8 * p + u + 1)
                        wait(act, xs["out"], 2 * (p - 1) + b + 1)
                        nc.scalar.activation(x_q[:, b, :, s * P:(s + 1) * P],
                                             XB["qt"][:, :].rearrange("p (h n) -> p h n", h=4),
                                             ACT.Copy).then_inc(xs["qcp"], 1)
                    elif kind == "G":
                        wait(act, xs["g"], 2 * p + u + 1)
                        nc.scalar.activation(x_gt[0:64, u, :], XB["gm"][0:64, :], ACT.Copy).then_inc(xs["gt"], 1)
                    elif kind == "OC":
                        wait(act, xs["out"], 2 * p)
                        wait(act, xs["y"], p - 1)
                        nc.scalar.activation(x_oc[:, :], XB["out"][:, :], ACT.Identity,
                                             bias=x_bc[:, 0:1]).then_inc(xs["oc"], 1)
                        wait(act, xs["var"], p - 1)
                        nc.scalar.activation(x_sq[:, :], XB["out"][:, :], ACT.Square,
                                             bias=x_bc[:, 0:1]).then_inc(xs["osq"], 1)
                    elif kind == "VAR":
                        wait(act, xs["var"], p)
                        wait(act, xs["rd"], p - 1)
                        nc.scalar.activation(x_sd[:, :], XB["post"][:, :], ACT.Sqrt,
                                             bias=x_eps[:, 0:1]).then_inc(xs["sd"], 1)
                    elif kind == "XT":
                        wait(act, xt_done, p)
                        t0 = (p - 1) * P
                        cols = slice(t0, t0 + P) if isinstance(p, int) else bass.ds(t0, P)
                        nc.scalar.activation(xTh[:, :, cols], XB["post"][:, :].rearrange("p (k n) -> p k n", k=KT),
                                             ACT.Copy).then_inc(xt_hi, 1)
                        wait(act, ln_done, 8 + p)
                        nc.scalar.activation(xtile(p - 1), x_xn[:, :], ACT.Copy).then_inc(xs["xcp"], 1)
            run(0, x_order(0, True, False))
            with act.Fori(1, NT) as p:
                run(p, x_order(p, True, True))
            run(NT, x_order(NT, False, True))

        def dve_xattn(dve):
            dve.wait_ge(xs["w1"], 32)
            nc.vector.tensor_reduce(x_wos[:, :], x_wo[:, :, :], AX_X, ALU.add).then_inc(xs["wos"], 1)
            dve.wait_ge(xs["wos"], 1)
            nc.vector.scalar_tensor_tensor(
                x_woc[:, :, :], x_wos[:, :].rearrange("p (k o) -> p k o", o=1).to_broadcast([P, 4, S]), -1.0 / S,
                x_wo[:, :, :], ALU.mult, ALU.add).then_inc(xs["woc"], 1)
            dve.wait_ge(xs["chi"], 1)
            nc.vector.tensor_tensor(x_wl[:, :, :], x_wraw[:, :, :], f32(x_wh[:, :, :]),
                                    ALU.subtract).then_inc(xs["wsp"], 1)
            nc.vector.memset(x_eps[:, :], EPS)
            dve.wait_ge(xs["bm"], 1)
            nc.vector.tensor_tensor(x_bc[:, :], x_bg[:, 0:1], pb[7][:, 0:1], ALU.subtract).then_inc(xs["bc"], 1)

            def q_sums(p, u):
                b, s = u // 4, u % 4
                wait(dve, xs["qexp"], 8 * p + u + 1)
                nc.vector.tensor_reduce(x_qs[:, s, :], x_e[:, s, :].rearrange("p (h d) -> p h d", h=XH), AX_X,
                                        ALU.add).then_inc(xs["qsum"], 1)
                wait(dve, xs["qsum"], 8 * p + u + 1)
                nc.vector.reciprocal(x_qr[:, s, :], x_qs[:, s, :]).then_inc(xs["qrec"], 1)

            def run(p, events):
                for kind, u in events:
                    b, s = u // 4, u % 4
                    if kind == "K":
                        if u == 0:
                            wait(dve, xs["chi"], p + 2)
                            nc.vector.tensor_tensor(x_cl[:, :], x_craw[:, :], f32(x_ch[:, :]),
                                                    ALU.subtract).then_inc(xs["csp"], 1)
                            wait(dve, xs["xhi"], p + 1)
                            nc.vector.tensor_tensor(x_xl[:, :], xtile(p), f32(x_xh[:, :]),
                                                    ALU.subtract).then_inc(xs["xsp"], 1)
                        wait(dve, xs["k"], 8 * p + u + 1)
                        nc.vector.tensor_reduce(x_kmx[:, u:u + 1], XB["k"][:, :], AX_X,
                                                ALU.max).then_inc(xs["kmax"], 1)
                        wait(dve, xs["kmax"], 8 * p + u + 1)
                        wait(dve, xs["kexp"], 8 * (p - 1) + u + 1)
                        nc.vector.tensor_scalar(x_knm[:, u:u + 1], x_kmx[:, u:u + 1], -1.0, None,
                                                ALU.mult).then_inc(xs["kneg"], 1)
                    elif kind == "Q":
                        bank = XB["q"][u % 2][:, :].rearrange("p (h d) -> p h d", h=XH)
                        wait(dve, xs["q"], 8 * p + u + 1)
                        nc.vector.tensor_reduce(x_qmx[:, s, :], bank, AX_X, ALU.max).then_inc(xs["qmax"], 1)
                        wait(dve, xs["qmax"], 8 * p + u + 1)
                        wait(dve, xs["qn"], 8 * p + u - 3)
                        nc.vector.tensor_tensor(
                            x_e[:, s, :].rearrange("p (h d) -> p h d", h=XH), bank,
                            x_qmx[:, s, :].rearrange("p (h o) -> p h o", o=1).to_broadcast([P, XH, XD]),
                            ALU.subtract).then_inc(xs["qsub"], 1)
                        if u >= 1:
                            q_sums(p, u - 1)
                    elif kind == "KT" and u == 7:
                        q_sums(p, 7)
                    elif kind == "G":
                        wait(dve, xs["kexp"], 8 * p + 4 * u + 4)
                        wait(dve, xs["mr"], 2 * (p - 1) + u + 1)
                        nc.vector.reciprocal(x_krz[:, 4 * u:4 * u + 4], x_kz[:, 4 * u:4 * u + 4]).then_inc(xs["krz"], 1)
                    elif kind == "M":
                        wait(dve, xs["m"], 2 * p + u + 1)
                        wait(dve, xs["krz"], 2 * p + u + 1)
                        wait(dve, xs["out"], 2 * (p - 1) + u + 1)
                        bank = XB["gm"][:, :].rearrange("p (h o) -> p h o", h=4)
                        for h in range(2):
                            r = slice(64 * h, 64 * h + 64)
                            last = nc.vector.scalar_tensor_tensor(
                                x_m[r, :, u, 64 * u:64 * u + 64], bank[r, :, 64 * h:64 * h + 64], XD ** -0.5,
                                x_krz[r, 4 * u:4 * u + 4].rearrange("p (h o) -> p h o", o=1).to_broadcast([64, 4, S]),
                                ALU.mult, ALU.mult)
                        last.then_inc(xs["mr"], 1)
                    elif kind == "VAR":
                        wait(dve, xs["sd"], p)
                        wait(dve, xs["y"], p - 1)
                        nc.vector.reciprocal(x_rd[:, :], x_sd[:, :]).then_inc(xs["rd"], 1)
                        wait(dve, xs["rd"], p)
                        wait(dve, xs["r"], p - 1)
                        nc.vector.scalar_tensor_tensor(x_y[:, :], x_oc[:, :], x_bg[:, 1:2], x_rd[:, :], ALU.mult,
                                                       ALU.mult).then_inc(xs["y"], 1)
                        wait(dve, xs["y"], p)
                        nc.vector.tensor_tensor(x_r[:, :], x_y[:, :], xtile(p - 1), ALU.add).then_inc(xs["r"], 1)
                        wait(dve, xs["r"], p)
                        nc.vector.bn_stats(st6[:, 0, :], x_r[:, :]).then_inc(ln_bn, 1)
                        dve.wait_ge(ln_bn, 8 + p)
                        carry_waits(dve, dve_passed)
                        nc.vector.bn_aggr(mv[:, 0, :], st6[:, 0, :]).then_inc(ln_ag, 1)
                        dve.wait_ge(ln_ag, 8 + p)
                        nc.vector.tensor_scalar(var_eps[:, 0:1], mv[:, 0, 1:2], EPS, None,
                                                ALU.add).then_inc(ln_stat, 1)
                    elif kind == "XT":
                        dve.wait_ge(ln_rstd, 8 + p)
                        wait(dve, xs["xcp"], p - 1)
                        nc.vector.tensor_scalar(x_xn[:, :], x_r[:, :], mv[:, 0, 0:1], rstd[:, 0:1],
                                                ALU.subtract, ALU.mult).then_inc(ln_done, 1)
                        dve.wait_ge(xt_hi, p)
                        t0 = (p - 1) * P
                        cols = slice(t0, t0 + P) if isinstance(p, int) else bass.ds(t0, P)
                        nc.vector.tensor_tensor(xTl[:, :, cols], XB["post"][:, :].rearrange("p (k n) -> p k n", k=KT),
                                                f32(xTh[:, :, cols]), ALU.subtract).then_inc(xt_ready, 1)

            def order(p, project, post):
                return x_order(p, project, post)
            run(0, order(0, True, False))
            with dve.Fori(1, NT) as p:
                run(p, order(p, True, True))
            run(NT, order(NT, False, True))

        def pool_xattn(pool):
            pool.wait_ge(*stage_end("attn0"))
            nc.gpsimd.memset(x_m[:, :, :, :], 0.0).then_inc(xs["zero"], 1)

            def run(p, project, post):
                for u in range(8):
                    s = u % 4
                    if project:
                        wait(pool, xs["qrec"], 8 * p + u + 1)
                        wait(pool, xs["qt"], 8 * p + u - 1)
                        nc.gpsimd.tensor_tensor(
                            x_en[:, u % 2, :].rearrange("p (h d) -> p h d", h=XH),
                            x_e[:, s, :].rearrange("p (h d) -> p h d", h=XH),
                            x_qr[:, s, :].rearrange("p (h o) -> p h o", o=1).to_broadcast([P, XH, XD]),
                            ALU.mult).then_inc(xs["qn"], 1)
                    if post and u == 3:
                        pool.wait_ge(ln_stat, 8 + p)
                        nc.gpsimd.tensor_tensor(rstd[:, 0:1], var_eps[:, 0:1], mhalf[:, 0:1],
                                                ALU.pow).then_inc(ln_rstd, 1)
            run(0, True, False)
            with pool.Fori(1, NT) as p:
                run(p, True, True)
            run(NT, False, True)

        def sp_ffn0(sp):
            sp.wait_ge(*stage_end("xattn0"))
            for h in range(2):
                sp.dma_start(f_c[:, :, :], a["ctxT"][:, 2 * h:2 * h + 2, :]).then_inc(fs["cin"], 16) if h == 0 else None

            def load(i):
                for c in range(3):
                    wait(sp, fs["dq"], 3 * (i - 1) + c + 1)
                    q, s = a["f_q"], a["f_s"]
                    if isinstance(i, int):
                        q, s = q[i, c], s[i:i + 1, c].to_broadcast([P, 1024])
                    else:
                        q = q[bass.ds(i, 1), c].rearrange("o p n -> p (o n)")
                        s = s[bass.ds(i, 1), c].to_broadcast([P, 1024])
                    sp.dma_start(f_q[:, c, :], q).then_inc(fs[f"in{c}"], 16)
                    sp.dma_start(f_s[:, c, :], s).then_inc(fs[f"in{c}"], 16)
            load(0)
            load(1)
            sp.wait_ge(fs["c"], 2)
            sp.dma_start(f_c[:, :, :], a["ctxT"][:, 2:4, :]).then_inc(fs["cin"], 16)
            with sp.Fori(2, NF) as i:
                load(i)

        def f_gate(m, which, k):
            return slice((which * KT + k) * P, (which * KT + k + 1) * P)

        def pe_ffn0(pe):
            pe.wait_ge(xt_ready, 8)

            def step(i):
                for u in range(4):
                    n, m = u // 2, u % 2
                    wait(pe, fs["w"], 3 * i + m + 1)
                    wait(pe, fs["it"], 4 * i + u - 1)
                    cols = slice(n * HALF, (n + 1) * HALF)
                    for which in range(2):
                        for k in range(KT):
                            w = f_gate(m, which, k)
                            last = mm3(pb[2 * which + u % 2][:, :], (f_wh[:, m, w], f_wl[:, m, w]),
                                       (xTh[:, k, cols], xTl[:, k, cols]), k == 0, k == KT - 1)
                    last.then_inc(fs["gu"], 1)
                for t in range(NT):
                    wait(pe, fs["w"], 3 * i + 3)
                    wait(pe, fs["i"], 4 * i + (2 if t < 4 else 4))
                    wait(pe, fs["add"], 8 * i + t - 1)
                    for m in range(2):
                        h = slice(t * P, (t + 1) * P)
                        w = slice(m * DM, (m + 1) * DM)
                        last = mm3(pb[4 + t % 2][:, :], (f_ih[:, m, h], f_il[:, m, h]),
                                   (f_wh[:, 2, w], f_wl[:, 2, w]), m == 0, m == 1)
                    last.then_inc(fs["dn"], 1)
            step(0)
            with pe.Fori(1, NF) as i:
                step(i)
            for t in range(NT):
                pe_transpose_tile(pe, "ffn0", t, pb[t % 2], (fs["it"], 4 * NF))

        def act_ffn0(act):
            act.wait_ge(*stage_end("xattn0"))

            def high_weight(i, c):
                wait(act, fs["dq"], 3 * i + c + 1)
                if c < 2:
                    wait(act, fs["gu"], 4 * (i - 1) + 3 + c)
                else:
                    wait(act, fs["dn"], 8 * i)
                nc.scalar.activation(f_wh[:, c, :], f_w[:, c, :], ACT.Copy).then_inc(fs["whi"], 1)

            def silu(i, u):
                wait(act, fs["gu"], 4 * i + u + 1)
                wait(act, fs["it"], 4 * i + u - 1)
                nc.scalar.activation(f_sg[:, u % 2, :], pb[u % 2][:, :], ACT.Silu).then_inc(fs["sg"], 1)

            def high_hidden(i, u):
                n, m = u // 2, u % 2
                wait(act, fs["it"], 4 * i + u + 1)
                wait(act, fs["dn"], 8 * (i - 1) + 4 * n + 4)
                nc.scalar.activation(f_ih[:, m, n * HALF:(n + 1) * HALF], f_it[:, u % 2, :],
                                     ACT.Copy).then_inc(fs["ihi"], 1)

            def step(i, more):
                for u in range(4):
                    silu(i, u)
                    if u >= 1:
                        high_hidden(i, u - 1)
                    if u == 2 and more:
                        high_weight(i + 1, 0)
                high_hidden(i, 3)
                if more:
                    high_weight(i + 1, 1)
                    high_weight(i + 1, 2)
            for c in range(3):
                high_weight(0, c)
            step(0, True)
            with act.Fori(1, NF - 1) as i:
                step(i, True)
            step(NF - 1, False)
            for t in range(NT):
                act_transpose_tile(act, "ffn0", t, pb[t % 2])

        def dve_ffn0(dve):
            def dequantise(i, c):
                for s in (f"in{c}",):
                    wait(dve, fs[s], 32 * (i + 1))
                wait(dve, fs["w"], 3 * (i - 1) + c + 1)
                nc.vector.tensor_tensor(f_w[:, c, :], f_q[:, c, :], f_s[:, c, :], ALU.mult).then_inc(fs["dq"], 1)

            def hidden(i, u):
                wait(dve, fs["sg"], 4 * i + u + 1)
                wait(dve, fs["i"], 4 * i + u - 1)
                nc.vector.tensor_tensor(f_it[:, u % 2, :], pb[2 + u % 2][:, :], f_sg[:, u % 2, :],
                                        ALU.mult).then_inc(fs["it"], 1)

            def step(i, more, last):
                hidden(i, 0)
                hidden(i, 1)
                hidden(i, 2)
                if more:
                    dequantise(i + 1, 0)
                hidden(i, 3)
                if more:
                    dequantise(i + 1, 1)
                    dequantise(i + 1, 2)
                for t in range(NT):
                    wait(dve, fs["dn"], 8 * i + t + 1)
                    wait(dve, fs["add"], 8 * (i - 1) + t + 1)
                    nc.vector.tensor_tensor(xtile(t), pb[4 + t % 2][:, :], xtile(t), ALU.add).then_inc(fs["add"], 1)
                    if last:
                        wait(dve, fs["add"], 8 * i + t + 1)
                        dve_norm_stats(dve, "ffn0", t, xtile(t))
                        if t >= 1:
                            dve_normalise(dve, "ffn0", t - 1, xtile(t - 1), xtile(t - 1))
            dve.wait_ge(xs["xcp"], 8)
            for c in range(3):
                dequantise(0, c)
            step(0, True, False)
            with dve.Fori(1, NF - 1) as i:
                step(i, True, False)
            step(NF - 1, False, True)
            dve_normalise(dve, "ffn0", NT - 1, xtile(NT - 1), xtile(NT - 1))
            for t in range(NT):
                dve_transpose_tile(dve, "ffn0", t, pb[t % 2])

        def pool_ffn0(pool):
            def low_weight(i, c):
                wait(pool, fs["whi"], 3 * i + c + 1)
                nc.gpsimd.tensor_tensor(f_wl[:, c, :], f_w[:, c, :], f32(f_wh[:, c, :]),
                                        ALU.subtract).then_inc(fs["w"], 1)

            def low_hidden(i, u):
                n, m = u // 2, u % 2
                cols = slice(n * HALF, (n + 1) * HALF)
                wait(pool, fs["ihi"], 4 * i + u + 1)
                nc.gpsimd.tensor_tensor(f_il[:, m, cols], f_it[:, u % 2, :], f32(f_ih[:, m, cols]),
                                        ALU.subtract).then_inc(fs["i"], 1)

            def split_context(h):
                pool.wait_ge(fs["cin"], 16 * (h + 1))
                for m in range(2):
                    k = 2 * h + m
                    carry_waits(pool, pool_passed)
                    nc.gpsimd.tensor_scalar(cTh[:, k, :], f_c[:, m, :], 1.0, 0.0, ALU.mult,
                                            ALU.add).then_inc(fs["chi"], 1)
                    pool.wait_ge(fs["chi"], k + 1)
                    nc.gpsimd.tensor_tensor(cTl[:, k, :], f_c[:, m, :], f32(cTh[:, k, :]),
                                            ALU.subtract).then_inc(fs["c"], 1)

            def step(i, more):
                for u in range(4):
                    low_hidden(i, u)
                    if u == 2 and more:
                        low_weight(i + 1, 0)
                if more:
                    low_weight(i + 1, 1)
                    low_weight(i + 1, 2)
            for c in range(3):
                low_weight(0, c)
            step(0, True)
            split_context(0)
            split_context(1)
            with pool.Fori(1, NF - 1) as i:
                step(i, True)
            step(NF - 1, False)
            for t in range(NT):
                pool_norm_root(pool, "ffn0", t)

        def g_part(tile, k, what):
            if what == "base":
                return tile[:, k * DM:(k + 1) * DM]
            if what == "gate":
                return tile[:, KT * DM + k * GC:KT * DM + (k + 1) * GC]
            return tile[:, KT * DM + KT * GC:]

        def sp_ffn1(sp):
            sp.wait_ge(*stage_end("xattn1"))
            sp.dma_start(g_raw[:, 0:KT * DM], a["g_base"]).then_inc(gs["in"], 16)
            sp.dma_start(g_raw[:, KT * DM:KT * DM + KT * GC], a["g_gate"]).then_inc(gs["in"], 16)
            sp.dma_start(g_raw[:, KT * DM + KT * GC:], a["g_b"]).then_inc(gs["in"], 16)
            sp.dma_start(g_bb[:, :], a["g_bbase"].to_broadcast([P, DM])).then_inc(gs["in"], 16)
            sp.dma_start(g_bt[:, :], a["g_bthr"].to_broadcast([P, 1])).then_inc(gs["in"], 16)
            for t in range(NT):
                sp.wait_ge(ln_done, 8 * LN_NORMS["ffn1"] + t + 1)
                sp.dma_start(a["out"][t * P:(t + 1) * P, :], g_o[:, t % 2, :]).then_inc(gs[f"out{t % 2}"], 16)
            for h in range(2):
                sp.wait_ge(gs[f"out{h}"], 16 * (NT // 2))

        def dve_ffn1(dve):
            dve.wait_ge(gs["hi"], 1)
            nc.vector.tensor_tensor(g_l[:, :], g_raw[:, :], f32(g_h[:, :]), ALU.subtract).then_inc(gs["w"], 1)
            NG = E_ * R_
            count = [0]

            def link(ins):
                ins.then_inc(gs["ch"], 1)
                count[0] += 1
                dve.wait_ge(gs["ch"], count[0])

            def route(t):
                dve.wait_ge(gs["p1"], t + 1)
                nc.vector.tensor_copy(g_hid[:, t, :], pb[2 + t % 2][:, 0:GC]).then_inc(gs["ev"], 1)
                dve.wait_ge(gs["ev"], t + 1)
                link(nc.vector.tensor_reduce(g_mx[:, t:t + 1], g_hid[:, t, NG:NG + E_], AX_X, ALU.max))
                nc.vector.tensor_scalar(g_e[:, t, E_:E_ + 2], g_hid[:, t, NG + E_:NG + E_ + 2], g_bt[:, 0:1], -1.0,
                                        ALU.add, ALU.mult)
                nc.vector.tensor_scalar(g_e[:, t, 0:E_], g_hid[:, t, NG:NG + E_], g_mx[:, t:t + 1], None,
                                        ALU.subtract).then_inc(gs["res"], 1)
                dve.wait_ge(gs["exp"], t + 1)
                nc.vector.tensor_scalar(g_sum[:, t, 1:2], g_e[:, t, E_:E_ + 1], 1.0, None, ALU.add)
                link(nc.vector.tensor_reduce(g_sum[:, t, 0:1], g_e[:, t, 0:E_], AX_X, ALU.add))
                link(nc.vector.reciprocal(g_rec[:, t, :], g_sum[:, t, :]))
                link(nc.vector.tensor_scalar(g_ad[:, t, :], g_e[:, t, 0:E_], g_rec[:, t, 0:1], None, ALU.mult))
                link(nc.vector.scalar_tensor_tensor(g_w[:, t, :], g_rec[:, t, 1:2].to_broadcast([P, E_]), -0.125,
                                                    g_ad[:, t, :], ALU.mult, ALU.add))
                link(nc.vector.tensor_scalar(g_wn[:, t, :], g_w[:, t, :], 0.0, None, ALU.max))
                link(nc.vector.tensor_reduce(g_ws[:, t, 0:1], g_wn[:, t, :], AX_X, ALU.add))
                link(nc.vector.tensor_scalar(g_ws[:, t, 1:2], g_ws[:, t, 0:1], 0.0, None, ALU.is_equal))
                link(nc.vector.tensor_tensor(g_ws[:, t, 0:1], g_ws[:, t, 0:1], g_ws[:, t, 1:2], ALU.add))
                link(nc.vector.reciprocal(g_wr[:, t:t + 1], g_ws[:, t, 0:1]))
                link(nc.vector.tensor_scalar(g_wn[:, t, :], g_wn[:, t, :], g_wr[:, t:t + 1], 2.0, ALU.mult, ALU.mult))
                nc.vector.tensor_tensor(
                    g_z[:, t, :].rearrange("p (e r) -> p e r", e=E_),
                    g_hid[:, t, 0:NG].rearrange("p (e r) -> p e r", e=E_),
                    g_wn[:, t, :].rearrange("p (e o) -> p e o", o=1).to_broadcast([P, E_, R_]),
                    ALU.mult).then_inc(gs["z"], 1)

            def low_z(t):
                dve.wait_ge(gs["zhi"], t + 1)
                nc.vector.tensor_tensor(g_zl[:, t % 2, :], pb[4 + t % 2][:, 0:P], f32(g_zh[:, t % 2, :]),
                                        ALU.subtract).then_inc(gs["zr"], 1)

            def finish(t):
                dve.wait_ge(gs["p2"], t + 1)
                link(nc.vector.tensor_tensor(xtile(t), pb[t % 2][:, :], xtile(t), ALU.add))
                link(nc.vector.tensor_tensor(xtile(t), xtile(t), g_bb[:, :], ALU.add))
                dve_norm_stats(dve, "ffn1", t, xtile(t))

            def emit(t):
                if t >= 2:
                    dve.wait_ge(gs[f"out{t % 2}"], 16 * (t // 2))
                dve_normalise(dve, "ffn1", t, xtile(t), g_o[:, t % 2, :])
            for t in range(NT):
                route(t)
                if t >= 1:
                    low_z(t - 1)
                if t >= 2:
                    finish(t - 2)
                if t >= 3:
                    emit(t - 3)
            low_z(NT - 1)
            finish(NT - 2)
            emit(NT - 3)
            finish(NT - 1)
            emit(NT - 2)
            emit(NT - 1)

        def pe_ffn1(pe):
            pe.wait_ge(gs["w"], 1)
            pe.wait_ge(xt_ready, 32)

            def first(t):
                h = slice(t * P, (t + 1) * P)
                if t >= 2:
                    pe.wait_ge(gs["ev"], t - 1)
                for k in range(KT):
                    last = mm3(pb[2 + t % 2][:, 0:GC], (xTh[:, k, h], xTl[:, k, h]),
                               (g_part(g_h, k, "gate"), g_part(g_l, k, "gate")), k == 0, k == KT - 1)
                last.then_inc(gs["p1"], 1)

            def base(t):
                h = slice(t * P, (t + 1) * P)
                if t >= 2:
                    pe.wait_ge(ln_bn, 8 * LN_NORMS["ffn1"] + t - 1)
                for k in range(KT):
                    mm3(pb[t % 2][:, :], (xTh[:, k, h], xTl[:, k, h]),
                        (g_part(g_h, k, "base"), g_part(g_l, k, "base")), k == 0, False)

            def transpose(t):
                pe.wait_ge(gs["z"], t + 1)
                if t >= 2:
                    pe.wait_ge(gs["zr"], t - 1)
                nc.tensor.transpose(pb[4 + t % 2][:, 0:P], g_z[:, t, :], ident[:, :]).then_inc(gs["zt"], 1)

            def experts(t):
                pe.wait_ge(gs["zr"], t + 1)
                mm3(pb[t % 2][:, :], (g_zh[:, t % 2, :], g_zl[:, t % 2, :]),
                    (g_part(g_h, 0, "up"), g_part(g_l, 0, "up")), False, True).then_inc(gs["p2"], 1)
            first(0)
            first(1)
            for t in range(NT):
                base(t)
                transpose(t)
                if t + 2 < NT:
                    first(t + 2)
                experts(t)

        def act_ffn1(act):
            act.wait_ge(*stage_end("xattn1"))
            act.wait_ge(gs["in"], 80)
            nc.scalar.activation(g_h[:, :], g_raw[:, :], ACT.Copy).then_inc(gs["hi"], 1)

            def high_z(t):
                act.wait_ge(gs["zt"], t + 1)
                if t >= 2:
                    act.wait_ge(gs["p2"], t - 1)
                nc.scalar.activation(g_zh[:, t % 2, :], pb[4 + t % 2][:, 0:P], ACT.Copy).then_inc(gs["zhi"], 1)
            for t in range(NT):
                act.wait_ge(gs["res"], t + 1)
                nc.scalar.activation(g_e[:, t, :], g_e[:, t, :], ACT.Exp).then_inc(gs["exp"], 1)
                high_z(t)

        block = ctx.enter_context(nc.Block())

        @block.sync
        def _(sp):
            sp.dma_start(ident[:, :], a["ident"]).then_inc(const_in, 16)
            sp.dma_start(own_half[:, :], a["own_half"]).then_inc(const_in, 16)
            for n in range(2):
                cols = slice(n * HALF, (n + 1) * HALF)
                sp.dma_start(probs[:, :, :, :].rearrange("p t g n -> p (t g n)").rearrange(
                    "p (k n) -> p k n", k=KT)[:, :, cols], a["xT"][:, :, cols]).then_inc(xr_in[n], 16)
            sp.dma_start(X[:, :].rearrange("p (t d) -> p t d", t=NT), a["x"]).then_inc(x_in, 16)
            sp_attention(sp, stages[0])
            sp_xattn(sp)
            sp_ffn0(sp)
            sp_attention(sp, stages[1])
            sp_attention(sp, stages[2])
            sp_ffn1(sp)

        @block.tensor
        def _(pe):
            pe_attention(pe, stages[0])
            pe_xattn(pe)
            pe_ffn0(pe)
            pe_attention(pe, stages[1])
            pe_attention(pe, stages[2])
            pe_ffn1(pe)

        @block.scalar
        def _(act):
            xin = probs[:, :, :, :].rearrange("p t g n -> p (t g n)").rearrange("p (k n) -> p k n", k=KT)
            for n in range(2):
                cols = slice(n * HALF, (n + 1) * HALF)
                act.wait_ge(xr_in[n], 16)
                nc.scalar.activation(xTh[:, :, cols], xin[:, :, cols], ACT.Copy).then_inc(x0_hi, 1)
            act_attention(act, stages[0])
            act_xattn(act)
            act_ffn0(act)
            act_attention(act, stages[1])
            act_attention(act, stages[2])
            act_ffn1(act)

        @block.vector
        def _(dve):
            xin = probs[:, :, :, :].rearrange("p t g n -> p (t g n)").rearrange("p (k n) -> p k n", k=KT)
            for n in range(2):
                cols = slice(n * HALF, (n + 1) * HALF)
                dve.wait_ge(x0_hi, n + 1)
                nc.vector.tensor_tensor(xTl[:, :, cols], xin[:, :, cols], f32(xTh[:, :, cols]),
                                        ALU.subtract).then_inc(x0_ready, 1)
            dve_attention(dve, stages[0])
            dve_xattn(dve)
            dve_ffn0(dve)
            dve_attention(dve, stages[1])
            dve_attention(dve, stages[2])
            dve_ffn1(dve)

        @block.gpsimd
        def _(pool):
            nc.gpsimd.memset(mhalf[:, :], -0.5).then_inc(const_set, 1)
            nc.gpsimd.memset(onecol[:, :], 1.0).then_inc(const_set, 1)
            pool.wait_ge(const_set, 2)
            pool_attention(pool, stages[0])
            pool_xattn(pool)
            pool_ffn0(pool)
            pool_attention(pool, stages[1])
            pool_attention(pool, stages[2])
            for t in range(NT):
                pool_norm_root(pool, "ffn1", t)


def kernel(**inputs):
    import numpy as np
    import concourse.bacc as bacc
    from concourse.bass_utils import run_bass_kernel_spmd

    v = {k: np.asarray(x) for k, x in inputs.items()}

    def col(w):
        return w.T.reshape(-1, P, w.shape[0]).transpose(1, 0, 2)

    def chunks(wq, wk, wv, order):
        q = col(wq).reshape(P, KT, NKV, G, HD).transpose(2, 3, 0, 1, 4)
        k = col(wk).reshape(P, KT, NKV, 1, HD).transpose(2, 3, 0, 1, 4)
        w = col(wv).reshape(P, KT, NKV, 1, HD).transpose(2, 3, 0, 1, 4)
        parts = {"q": q, "k": k, "v": w}
        return np.concatenate([parts[o] for o in order], axis=1).reshape(NKV, 6, P, KT * HD)

    def outs(wo):
        return wo.T.reshape(NKV, G, HD, DM)

    x2 = v["x"].reshape(TOK, DM)
    c2 = v["ctx_4096"].reshape(TOK, DM)
    cT = c2.T.reshape(KT, P, TOK).transpose(1, 0, 2)
    nq = NKV * G * HD
    wqkv = v["L1_attn_w_qkv"].T
    wkv = v["L0_xattn_Wkv"]
    twice = lambda w: np.concatenate([w, w], axis=0)

    def ffn_in(q):
        return q.T.reshape(KT, P, NF, 2, P)
    gq, uq = ffn_in(v["L0_ffn_gate_q"]), ffn_in(v["L0_ffn_up_q"])
    gu = np.stack([gq, uq]).transpose(3, 4, 2, 0, 1, 5).reshape(NF, 2, P, 1024)
    dq = v["L0_ffn_down_q"].T.reshape(NF, 1, 2, P, DM).transpose(0, 1, 3, 2, 4).reshape(NF, 1, P, 1024)
    f_q = np.concatenate([gu, dq], axis=1)
    sc = lambda s: s.T.reshape(KT, NF, 2, P)
    gus = np.stack([sc(v["L0_ffn_gate_s"]), sc(v["L0_ffn_up_s"])]).transpose(2, 3, 0, 1, 4).reshape(NF, 2, 1024)
    ds = v["L0_ffn_down_s"].T.reshape(NF, 1, 1024)
    f_s = np.concatenate([gus, ds], axis=1)

    pos = np.arange(S)
    rel = np.tile(pos[:, None] - pos[None, :], (2, 1))
    causal = np.where(rel >= 0, 0.0, NEG).astype(np.float32)
    slopes = ((2.0 ** (-8.0 / (NKV * G))) ** np.arange(1, NKV * G + 1, dtype=np.float32)).astype(np.float32)
    root = np.sqrt(np.maximum(rel, 0).astype(np.float32))
    alibi = np.where(rel[None] >= 0, -slopes[:, None, None] * root[None], np.float32(NEG)).astype(np.float32)
    alibi = alibi.reshape(NKV, G, P, S).transpose(0, 2, 1, 3).reshape(NKV, P, G * S)
    blk = np.kron(np.eye(2), np.full((S, S), 1.0 / S)).astype(np.float32)

    gate = np.concatenate([v["L1_ffn_A_w"].reshape(E_ * R_, DM), v["L1_ffn_W_gate"], v["L1_ffn_W_thr"][None],
                           np.zeros((1, DM), np.float32)], axis=0)
    up = v["L1_ffn_B_w"].transpose(0, 2, 1).reshape(E_ * R_, DM)

    data = {
        "x": x2.reshape(NT, P, DM).transpose(1, 0, 2),
        "xT": x2.T.reshape(KT, P, TOK).transpose(1, 0, 2),
        "ctx": c2.reshape(NT, P, DM),
        "ctxT": cT,
        "ctxT_pair": cT.reshape(P, KT, NT, P).transpose(2, 0, 1, 3).reshape(NT, P, KT * P),
        "ident": np.eye(P, dtype=np.float32),
        "own_half": np.kron(np.eye(2), np.ones((S, 1))).astype(np.float32),
        "causal": causal, "alibi": alibi,
        "mask": twice(v["mask_1x1xSxS2_ff0"].reshape(S, S)),
        "norm_w": np.stack([v["L1_xattn_q_norm_w"], v["L1_xattn_k_norm_w"]], axis=1),
        "a0_in": chunks(v["L0_attn_wq"], v["L0_attn_wk"], v["L0_attn_wv"], "kqv"),
        "a0_out": outs(v["L0_attn_wo"]),
        "a1_in": chunks(wqkv[:nq], wqkv[nq:nq + NKV * HD], wqkv[nq + NKV * HD:], "kqv"),
        "a1_out": outs(v["L1_attn_w_o"].T),
        "a2_in": chunks(v["L1_xattn_q_proj_w"], v["L1_xattn_k_proj_w"], v["L1_xattn_v_proj_w"], "kvq"),
        "a2_out": outs(v["L1_xattn_o_proj_w"]),
        "x_wqk": np.stack([twice(v["L0_xattn_Wq"].T), twice(wkv[:XW].T)], axis=1),
        "x_wv": wkv[XW:].reshape(4, P, S).transpose(1, 0, 2),
        "x_wo": v["L0_xattn_Wout"].T.reshape(4, P, S).transpose(1, 0, 2),
        "x_bg": np.stack([np.tile(v["L0_xattn_b_out"], 2), np.tile(v["L0_xattn_g"].reshape(S), 2)], axis=1),
        "x_blk": blk,
        "f_q": f_q, "f_s": f_s,
        "g_base": col(v["L1_ffn_W_base"]).reshape(P, KT * DM),
        "g_gate": col(gate).reshape(P, KT * GC),
        "g_b": up,
        "g_bbase": v["L1_ffn_b_base"].reshape(1, DM),
        "g_bthr": v["L1_ffn_b_thr"].reshape(1, 1),
    }
    nc = bacc.Bacc("TRN2", target_bir_lowering=False, num_devices=1)
    arrays, args = {}, {}
    for name, x in data.items():
        x = np.ascontiguousarray(x)
        arrays["in_" + name] = x
        args[name] = nc.dram_tensor("in_" + name, x.shape, mybir.dt.from_np(x.dtype), kind="ExternalInput").ap()
    args["out"] = nc.dram_tensor("out_0", (TOK, DM), F32, kind="ExternalOutput").ap()
    program(nc, args)
    r = run_bass_kernel_spmd(nc, [arrays], core_ids=[0])
    return r.results[0]["out_0"].reshape(B, S, DM)
```

```python
from contextlib import ExitStack

import concourse.bass as bass
from concourse import mybir

F32 = mybir.dt.float32
F32R = mybir.dt.float32r
I32 = mybir.dt.int32
ALU = mybir.AluOpType
ACT = mybir.ActivationFunctionType
AX_X = mybir.AxisListType.X

P = 128
B, S, DM = 16, 64, 512
TOK = B * S
NT = TOK // P
KT = DM // P
NKV, G, HD = 8, 4, 128
HALF = TOK // 2
EPS = 1e-5

XH, XD = 8, 64
XW = XH * XD

FI = 1792
FSTEP = 256
NF = FI // FSTEP

E_, R_ = 8, 16
GC = E_ * R_ + E_ + 2

NEG = -1.0e30


def wait(eng, sem, n):
    if isinstance(n, int) and n <= 0:
        return
    eng.wait_ge(sem, n)


def carry_waits(eng, waits_passed):
    eng.sem_inc(waits_passed, 1)


def units(rms):
    q = [("q", g, n) for g in range(G) for n in range(2)]
    if rms:
        return [("kv", 0, n) for n in range(4)] + q
    return [("k", 0, 0), ("k", 0, 1)] + q + [("v", 0, 0), ("v", 0, 1)]


def schedule(rms, project, attend):
    first_sc = 5 if rms else 3
    ev = []

    def score(j):
        ev.extend([("SQ", j), ("SC", j)] if rms else [("SC", j)])

    def unit(u):
        if not project:
            return
        ev.append(("U", u))
        if rms and u in (3, 5):
            ev.append(("KT", u // 4))
        if 0 <= u - first_sc < 8:
            score(u - first_sc)
        if not rms and u == 11:
            ev.append(("VT", 0))

    unit(0)
    unit(1)
    if attend:
        ev.append(("WS", 0))
    unit(2)
    if attend:
        ev.append(("T", 0))
    unit(3)
    for t in range(NT):
        if attend:
            ev.append(("PV", t))
            if t + 1 < NT:
                ev.append(("T", t + 1))
        unit(4 + t)
        if attend:
            ev.append(("WO", t))
    if project:
        if rms:
            score(7)
        else:
            ev.append(("VT", 1))
    return ev


def later(events, kinds, by):
    out, held = [], []
    for e in events:
        if e[0] in kinds:
            held.append([by, e])
            continue
        out.append(e)
        for h in held:
            h[0] -= 1
        while held and held[0][0] <= 0:
            out.append(held.pop(0)[1])
    return out + [h[1] for h in held]


def program(nc, a):
    with ExitStack() as ctx:
        def sem(name):
            return ctx.enter_context(nc.semaphore(name))

        def keep(name, shape, dt=F32):
            return ctx.enter_context(nc.sbuf_tensor(name, shape, dt))

        X = keep("X", [P, NT * DM])
        xTh = keep("xTh", [P, KT, TOK], F32R)
        xTl = keep("xTl", [P, KT, TOK], F32R)
        cTh = keep("cTh", [P, KT, TOK], F32R)
        cTl = keep("cTl", [P, KT, TOK], F32R)
        ident = keep("ident", [P, P])
        st6 = keep("st6", [P, NT, 6])
        mv = keep("mv", [P, NT, 2])
        var_eps = keep("var_eps", [P, NT])
        rstd = keep("rstd", [P, NT])
        mhalf = keep("mhalf", [P, 32])
        onecol = keep("onecol", [P, 1])
        own_half = keep("own_half", [P, 2])

        pb = [ctx.enter_context(nc.psum_tensor(f"pb{i}", [P, 512], F32)) for i in range(8)]

        xT, cT = (xTh, xTl), (cTh, cTl)

        with ExitStack() as sa:
            def sb(name, shape, dt=F32):
                return sa.enter_context(nc.sbuf_tensor(name, shape, dt))
            wh = sb("wh", [P, 6, KT, P], F32R)
            wl = sb("wl", [P, 6, KT, P], F32R)
            woh = sb("woh", [P, G, DM], F32R)
            wol = sb("wol", [P, G, DM], F32R)
            q_sb = sb("q_sb", [P, 2, HALF])
            k_sb = sb("k_sb", [P, TOK])
            vh = sb("vh", [P, NT, HD], F32R)
            vl = sb("vl", [P, NT, HD], F32R)
            pth = sb("pth", [P, G * P], F32R)
            ptl = sb("ptl", [P, G * P], F32R)
            oth = sb("oth", [P, G * P], F32R)
            otl = sb("otl", [P, G * P], F32R)
            raw = sb("raw", [P, 5, 512])
            vst = sb("vst", [P, NT, HD])
            sc_sb = sb("sc_sb", [P, NT, G, S])
            probs = sb("probs", [P, NT, G, P])
            smax = sb("smax", [P, NT, G])
            ssum = sb("ssum", [P, NT, G])
            rs = sb("rs", [P, NT, G])
            rs2 = sb("rs2", [P, NT, G, 2])
            bias = sb("bias", [P, G, S])
            sq = sb("sq", [P, HALF])
            kst = sb("kst", [P, NT, HD])
            junk = sb("junk", [P, HD])
            kss = sb("kss", [P, NT])
            kms = sb("kms", [P, NT])
            rk = sb("rk", [P, NT])
            qms = sb("qms", [P, NT, G])
            rq = sb("rq", [P, NT, G])
            norm_w = sb("norm_w", [P, 2])
            kfac = sb("kfac", [P, 1])

        with ExitStack() as sx:
            def sb(name, shape, dt=F32):
                return sx.enter_context(nc.sbuf_tensor(name, shape, dt))
            x_wraw = sb("x_wraw", [P, 2, XW])
            x_wh = sb("x_wh", [P, 2, XW], F32R)
            x_wl = sb("x_wl", [P, 2, XW], F32R)
            x_wv = sb("x_wv", [P, 4, S])
            x_wo = sb("x_wo", [P, 4, S])
            x_wos = sb("x_wos", [P, 4])
            x_woc = sb("x_woc", [P, 4, S])
            x_u = sb("x_u", [64, XH * S])
            x_bg = sb("x_bg", [P, 2])
            x_bc = sb("x_bc", [P, 1])
            x_blk = sb("x_blk", [P, P])
            x_eps = sb("x_eps", [P, 1])
            x_xh = sb("x_xh", [P, DM], F32R)
            x_xl = sb("x_xl", [P, DM], F32R)
            x_craw = sb("x_craw", [P, DM])
            x_ch = sb("x_ch", [P, DM], F32R)
            x_cl = sb("x_cl", [P, DM], F32R)
            x_ct = sb("x_ct", [P, KT, P])
            x_kmx = sb("x_kmx", [P, 8])
            x_knm = sb("x_knm", [P, 8])
            x_kz = sb("x_kz", [P, 8])
            x_krz = sb("x_krz", [P, 8])
            x_ek = sb("x_ek", [P, 2, 512])
            x_ekT = sb("x_ekT", [P, 2, 4, 512])
            x_e = sb("x_e", [P, 4, 512])
            x_qmx = sb("x_qmx", [P, 4, XH])
            x_qs = sb("x_qs", [P, 4, XH])
            x_qr = sb("x_qr", [P, 4, XH])
            x_en = sb("x_en", [P, 2, 512])
            x_q = sb("x_q", [P, 2, 4, 512])
            x_gt = sb("x_gt", [64, 2, 512])
            x_m = sb("x_m", [P, 4, 2, P])
            x_oc = sb("x_oc", [P, DM])
            x_sq = sb("x_sq", [P, DM])
            x_sd = sb("x_sd", [P, DM])
            x_rd = sb("x_rd", [P, DM])
            x_y = sb("x_y", [P, DM])
            x_r = sb("x_r", [P, DM])
            x_xn = sb("x_xn", [P, DM])

        with ExitStack() as sf:
            def sb(name, shape, dt=F32):
                return sf.enter_context(nc.sbuf_tensor(name, shape, dt))
            f_q = sb("f_q", [P, 3, 1024], I32)
            f_s = sb("f_s", [P, 3, 1024])
            f_w = sb("f_w", [P, 3, 1024])
            f_wh = sb("f_wh", [P, 3, 1024], F32R)
            f_wl = sb("f_wl", [P, 3, 1024], F32R)
            f_sg = sb("f_sg", [P, 2, HALF])
            f_it = sb("f_it", [P, 2, HALF])
            f_ih = sb("f_ih", [P, 2, TOK], F32R)
            f_il = sb("f_il", [P, 2, TOK], F32R)
            f_c = sb("f_c", [P, 2, TOK])

        with ExitStack() as sg:
            def sb(name, shape, dt=F32):
                return sg.enter_context(nc.sbuf_tensor(name, shape, dt))
            g_raw = sb("g_raw", [P, KT * DM + KT * GC + DM])
            g_h = sb("g_h", [P, KT * DM + KT * GC + DM], F32R)
            g_l = sb("g_l", [P, KT * DM + KT * GC + DM], F32R)
            g_bb = sb("g_bb", [P, DM])
            g_bt = sb("g_bt", [P, 1])
            g_hid = sb("g_hid", [P, NT, GC])
            g_mx = sb("g_mx", [P, NT])
            g_e = sb("g_e", [P, NT, 10])
            g_sum = sb("g_sum", [P, NT, 2])
            g_rec = sb("g_rec", [P, NT, 2])
            g_ad = sb("g_ad", [P, NT, E_])
            g_w = sb("g_w", [P, NT, E_])
            g_ws = sb("g_ws", [P, NT, 2])
            g_wr = sb("g_wr", [P, NT])
            g_wn = sb("g_wn", [P, NT, E_])
            g_z = sb("g_z", [P, NT, P])
            g_zh = sb("g_zh", [P, 2, P], F32R)
            g_zl = sb("g_zl", [P, 2, P], F32R)
            g_o = sb("g_o", [P, 2, DM])

        def f32(ap):
            return ap.bitcast(F32)

        def mm3(out, w, x, start, stop):
            (w_hi, w_lo), (x_hi, x_lo) = w, x
            nc.tensor.matmul(out, w_hi, x_hi, start=start, stop=False)
            nc.tensor.matmul(out, w_hi, x_lo, start=False, stop=False)
            return nc.tensor.matmul(out, w_lo, x_hi, start=False, stop=stop)

        def xtile(t):
            return X[:, t * DM:(t + 1) * DM] if isinstance(t, int) else X[:, bass.ds(t * DM, DM)]

        const_in = sem("const_in")
        const_set = sem("const_set")
        pool_passed = sem("pool_passed")
        dve_passed = sem("dve_passed")
        x_in = sem("x_in")
        xr_in = [sem("xr_in0"), sem("xr_in1")]
        x0_hi = sem("x0_hi")
        x0_ready = sem("x0_ready")

        ln_bn = sem("ln_bn")
        ln_ag = sem("ln_ag")
        ln_stat = sem("ln_stat")
        ln_rstd = sem("ln_rstd")
        ln_done = sem("ln_done")
        xt_done = sem("xt_done")
        xt_hi = sem("xt_hi")
        xt_ready = sem("xt_ready")
        LN_NORMS = {"attn0": 0, "xattn0": 1, "ffn0": 2, "attn1": 3, "xattn1": 4, "ffn1": 5}
        XT_NORMS = {"xattn0": 0, "ffn0": 1, "attn1": 2, "xattn1": 3}

        names = dict(
            proj_done=96,
            t_done=64,
            pv_done=64,
            wo_done=64,
            sc_done=64,
            pt_hi=64, o_hi=64,
            exp_done=64,
            wo_hi=32,
            proj_free=96,
            pt_ready=64, o_ready=64,
            wo_ready=32,
            x_added=64,
            s_out=64,
            s_max=64, s_sub=64, s_sum=64, s_inv=64, s_rec=64,
            w_hi=48, w_ready=48,
            vt_done=16,
            v_hi=16, v_ready=16,
            p_ready=64,
        )
        A = {n: sem(n) for n in names}
        for n in ("q_sq", "k_ss", "k_ms", "k_rs", "k_nrm", "kt_done", "kt_ready", "kv_free", "q_free", "ss_done", "ss_out",
                  "q_rs", "s_msk", "kf_ready"):
            A[n] = sem(n)
        ld_w = [sem(f"ld_w{c}") for c in range(6)]
        ld_o = [sem(f"ld_o{c}") for c in range(4)]
        ld_b = sem("ld_b")

        xs = {n: sem("x_" + n) for n in (
            "w0", "w1", "w2", "wsp", "wos", "woc", "u", "u_out", "bm", "bc", "zero", "cin", "ctin", "xhi", "xsp", "chi",
            "csp", "k", "kmax", "kneg", "kexp", "kt", "ekt", "g", "gt", "m", "krz", "mr", "q", "qmax", "qsub", "qexp",
            "qsum", "qrec", "qn", "qt", "qcp", "out", "oc", "osq", "var", "sd", "rd", "y", "r", "xcp")}
        fs = {n: sem("f_" + n) for n in (
            "in0", "in1", "in2", "dq", "whi", "w", "gu", "sg", "it", "ihi", "i", "dn", "add", "cin", "chi", "c")}
        gs = {n: sem("g_" + n) for n in (
            "in", "hi", "w", "p1", "ev", "ch", "exp", "z", "zt", "zhi", "zr", "p2", "res", "out0", "out1")}

        def stage_end(name):
            return {"attn0": (A["x_added"], 64), "xattn0": (xs["xcp"], 8), "ffn0": (fs["add"], NF * NT),
                    "attn1": (A["x_added"], 128), "xattn1": (A["x_added"], 192)}[name]

        def dve_norm_stats(dve, name, t, src):
            n = 8 * LN_NORMS[name]
            nc.vector.bn_stats(st6[:, t, :], src).then_inc(ln_bn, 1)
            dve.wait_ge(ln_bn, n + t + 1)
            nc.vector.bn_aggr(mv[:, t, :], st6[:, t, :]).then_inc(ln_ag, 1)
            dve.wait_ge(ln_ag, n + t + 1)
            nc.vector.tensor_scalar(var_eps[:, t:t + 1], mv[:, t, 1:2], EPS, None, ALU.add).then_inc(ln_stat, 1)

        def pool_norm_root(pool, name, t):
            n = 8 * LN_NORMS[name]
            pool.wait_ge(ln_stat, n + t + 1)
            nc.gpsimd.tensor_tensor(rstd[:, t:t + 1], var_eps[:, t:t + 1], mhalf[:, 0:1],
                                    ALU.pow).then_inc(ln_rstd, 1)

        def dve_normalise(dve, name, t, src, dst):
            dve.wait_ge(ln_rstd, 8 * LN_NORMS[name] + t + 1)
            nc.vector.tensor_scalar(dst, src, mv[:, t, 0:1], rstd[:, t:t + 1],
                                    ALU.subtract, ALU.mult).then_inc(ln_done, 1)

        def pe_transpose_tile(pe, name, t, bank, free):
            n = 8 * XT_NORMS[name]
            pe.wait_ge(ln_done, 8 * LN_NORMS[name] + t + 1)
            wait(pe, *free) if t < 2 else pe.wait_ge(xt_ready, n + t - 1)
            for k in range(KT):
                last = nc.tensor.transpose(bank[:, k * P:(k + 1) * P], X[:, t * DM + k * P:t * DM + (k + 1) * P],
                                           ident[:, :])
            last.then_inc(xt_done, 1)

        def act_transpose_tile(act, name, t, bank):
            n = 8 * XT_NORMS[name]
            act.wait_ge(xt_done, n + t + 1)
            nc.scalar.activation(xTh[:, :, t * P:(t + 1) * P], bank[:, :].rearrange("p (k n) -> p k n", k=KT),
                                 ACT.Copy).then_inc(xt_hi, 1)

        def dve_transpose_tile(dve, name, t, bank):
            n = 8 * XT_NORMS[name]
            dve.wait_ge(xt_hi, n + t + 1)
            nc.vector.tensor_tensor(xTl[:, :, t * P:(t + 1) * P], bank[:, :].rearrange("p (k n) -> p k n", k=KT),
                                    f32(xTh[:, :, t * P:(t + 1) * P]), ALU.subtract).then_inc(xt_ready, 1)

        class Stage:
            def __init__(self, name, index, rms, before, w_in, w_out, bias_in, per_head_bias, scale):
                self.name, self.index, self.rms, self.before = name, index, rms, before
                self.w_in, self.w_out, self.bias_in = w_in, w_out, bias_in
                self.per_head_bias, self.scale = per_head_bias, scale
                self.units = units(rms)
                self.k_c, self.v_c, self.q_c = (0, 1, 2) if rms else (0, 5, 1)

            def unit_read(self, i, u):
                if u < 0:
                    i, u = i - 1, u + 12
                if not self.rms:
                    return self.at("proj_free", 12 * i + u + 1)
                if u < 4:
                    return A["kv_free"], 4 * i + u + 1
                return A["q_free"], 8 * i + u - 3

            def chunk_of(self, u):
                kind, g, _ = self.units[u]
                return {"k": self.k_c, "v": self.v_c, "kv": self.v_c, "q": self.q_c + g}[kind]

            def last_unit_of(self, c):
                if self.rms and c < 2:
                    return 3
                return max(u for u in range(12) if self.chunk_of(u) == c)

            def at(self, name, n):
                return A[name], names.get(name, 0) * self.index + n

            def need(self, eng, name, n):
                if isinstance(n, int) and n <= 0:
                    return
                eng.wait_ge(*self.at(name, n))

        stages = [
            Stage("attn0", 0, False, None, a["a0_in"], a["a0_out"], a["causal"], False, HD ** -0.5),
            Stage("attn1", 1, False, "ffn0", a["a1_in"], a["a1_out"], a["alibi"], True, HD ** -0.5),
            Stage("xattn1", 2, True, "attn1", a["a2_in"], a["a2_out"], a["mask"], False, 1.0),
        ]

        def hn(ap4, g, n):
            return ap4[:, 4 * n:4 * n + 4, g]

        def sp_attention(sp, st):
            def load_w(i, c, slot):
                src = st.w_in[i, c] if isinstance(i, int) else \
                    st.w_in[bass.ds(i, 1), c].rearrange("o p n -> p (o n)")
                sp.dma_start(raw[:, slot, :], src).then_inc(ld_w[c], 16)

            def load_o(i, c, slot):
                src = st.w_out[i, c] if isinstance(i, int) else \
                    st.w_out[bass.ds(i, 1), c].rearrange("o p n -> p (o n)")
                sp.dma_start(raw[:, slot, :], src).then_inc(ld_o[c], 16)

            def load_bias(i):
                if st.per_head_bias:
                    src = st.bias_in[i] if isinstance(i, int) else \
                        st.bias_in[bass.ds(i, 1)].rearrange("o p n -> p (o n)")
                    st.need(sp, "s_msk" if st.rms else "s_out", 8 * i)
                    sp.dma_start(bias[:, :, :].rearrange("p g s -> p (g s)"), src).then_inc(ld_b, 16)

            if st.before:
                sp.wait_ge(*stage_end(st.before))
            if not st.per_head_bias:
                sp.dma_start(bias[:, 0, :], st.bias_in).then_inc(ld_b, 16)
            if st.rms:
                sp.dma_start(norm_w[:, :], a["norm_w"]).then_inc(const_in, 16)
            for c in range(5):
                load_w(0, c, c)
            load_bias(0)
            st.need(sp, "w_ready", 5)
            load_w(0, 5, 4)

            def step(i, more):
                if more:
                    for c in range(5):
                        if c < 4:
                            st.need(sp, "wo_ready", 4 * (i - 1) + c + 1)
                        else:
                            st.need(sp, "w_ready", 6 * i + 6)
                        load_w(i + 1, c, c)
                for c in range(4):
                    if more:
                        st.need(sp, "w_ready", 6 * (i + 1) + c + 1)
                    else:
                        st.need(sp, "wo_ready", 4 * (i - 1) + c + 1)
                    load_o(i, c, c)
                if more:
                    load_bias(i + 1)
                    st.need(sp, "w_ready", 6 * (i + 1) + 5)
                    load_w(i + 1, 5, 4)

            step(0, True)
            with sp.Fori(1, NKV - 1) as i:
                step(i, True)
            step(NKV - 1, False)

        def pe_attention(pe, st):
            def unit(i, u):
                kind, g, n = st.units[u]
                c = st.chunk_of(u)
                if n == 0:
                    st.need(pe, "w_ready", 6 * i + c + 1)
                if st.name == "attn0" and isinstance(i, int) and u < 2:
                    pe.wait_ge(x0_ready, u + 1)
                if not (isinstance(i, int) and i == 0 and u < 2):
                    wait(pe, *st.unit_read(i, u - 2))
                bank = pb[u % 2]
                w = lambda k: (wh[:, c, k, :], wl[:, c, k, :])
                if kind != "kv":
                    cols = slice(n * HALF, (n + 1) * HALF)
                    for k in range(KT):
                        last = mm3(bank[:, :], w(k), (xTh[:, k, cols], xTl[:, k, cols]), k == 0, k == KT - 1)
                else:
                    for m in range(2):
                        t = 2 * n + m
                        for k in range(KT):
                            last = mm3(bank[:, 2 * m * HD:2 * (m + 1) * HD],
                                       (cTh[:, k, t * P:(t + 1) * P], cTl[:, k, t * P:(t + 1) * P]),
                                       (wh[:, 0:2, k, :], wl[:, 0:2, k, :]), k == 0, k == KT - 1)
                last.then_inc(A["proj_done"], 1)

            def scores(i, j):
                g, n = j // 2, j % 2
                u = (4 if st.rms else 2) + j
                wait(pe, *st.unit_read(i, u))
                if st.rms:
                    st.need(pe, "kt_ready", 2 * i + 2)
                st.need(pe, "s_out", 8 * i + j - 1)
                bank = pb[2 + j % 2]
                for m in range(4):
                    t = 4 * n + m
                    last = nc.tensor.matmul(bank[:, m * P:(m + 1) * P], q_sb[:, j % 2, m * P:(m + 1) * P],
                                            k_sb[:, t * P:(t + 1) * P], start=True, stop=True)
                last.then_inc(A["sc_done"], 1)

            def square_sums(i, j):
                st.need(pe, "q_sq", 8 * i + j + 1)
                st.need(pe, "ss_out", 8 * i + j)
                for m in range(4):
                    last = nc.tensor.matmul(pb[7][:, m:m + 1], sq[:, m * P:(m + 1) * P], onecol[:, :],
                                            start=True, stop=True)
                last.then_inc(A["ss_done"], 1)

            def transpose_k(i, n):
                st.need(pe, "k_nrm", 4 * i + 2 * n + 2)
                st.need(pe, "s_out", 8 * i)
                for m in range(4):
                    last = nc.tensor.transpose(pb[2 + n][:, m * P:(m + 1) * P], kst[:, 4 * n + m, :], ident[:, :])
                last.then_inc(A["kt_done"], 1)

            def transpose_v(i, n):
                st.need(pe, "proj_free", 12 * i + 11 + n)
                st.need(pe, "v_ready", 2 * i + n)
                for m in range(4):
                    last = nc.tensor.transpose(pb[7][:, m * P:(m + 1) * P], vst[:, 4 * n + m, :], ident[:, :])
                last.then_inc(A["vt_done"], 1)

            def transpose_probs(i, t):
                st.need(pe, "p_ready", 8 * i + t + 1)
                st.need(pe, "pt_ready", 8 * i + t)
                for g in range(G):
                    last = nc.tensor.transpose(pb[4][:, g * P:(g + 1) * P], probs[:, t, g, :], ident[:, :])
                last.then_inc(A["t_done"], 1)

            def probs_v(i, t):
                st.need(pe, "pt_ready", 8 * i + t + 1)
                st.need(pe, "v_ready", 2 * i + 1 + t // 4)
                st.need(pe, "o_ready", 8 * i + t)
                mm3(pb[5][:, :], (vh[:, t, :], vl[:, t, :]), (pth[:, :], ptl[:, :]), True,
                    True).then_inc(A["pv_done"], 1)

            def project_out(i, t):
                st.need(pe, "o_ready", 8 * i + t + 1)
                st.need(pe, "wo_ready", 4 * i + 4)
                st.need(pe, "x_added", 8 * i + t)
                for g in range(G):
                    last = mm3(pb[6][:, :], (oth[:, g * P:(g + 1) * P], otl[:, g * P:(g + 1) * P]),
                               (woh[:, g, :], wol[:, g, :]), g == 0, g == G - 1)
                last.then_inc(A["wo_done"], 1)

            def run(i, events):
                for kind, n in events:
                    if kind == "U":
                        unit(i, n)
                    elif kind == "SC":
                        scores(i, n)
                    elif kind == "SQ":
                        square_sums(i, n)
                    elif kind == "KT":
                        transpose_k(i, n)
                    elif kind == "VT":
                        transpose_v(i, n)
                    elif kind == "T":
                        transpose_probs(i - 1, n)
                    elif kind == "PV":
                        probs_v(i - 1, n)
                    elif kind == "WO":
                        project_out(i - 1, n)

            if st.name == "attn0":
                pe.wait_ge(const_in, 32)
            else:
                pe.wait_ge(const_set, 2)
                pe.wait_ge(xt_ready, 8 * (2 if st.name == "attn1" else 3))
            if st.rms:
                pe.wait_ge(fs["c"], 4)
            run(0, schedule(st.rms, True, False))
            with pe.Fori(1, NKV) as i:
                run(i, schedule(st.rms, True, True))
            i = NKV
            for kind, t in schedule(st.rms, False, True):
                run(i, [(kind, t)])
                if kind == "PV" and t >= 2 and st.name != "attn0":
                    pe_transpose_tile(pe, st.name, t - 2, pb[t % 2], st.unit_read(NKV, -1))
            if st.name != "attn0":
                for t in (NT - 2, NT - 1):
                    pe_transpose_tile(pe, st.name, t, pb[t % 2], st.unit_read(NKV, -1))

        def act_attention(act, st):
            def unit(i, u):
                kind, g, n = st.units[u]
                if kind == "kv":
                    for m in range(2):
                        st.need(act, "k_ss", 8 * i + 2 * n + m)
                        wait(act, *st.unit_read(i, u))
                        st.need(act, "k_ms", 4 * (i - 1) + n + 1)
                        nc.scalar.activation(junk[:, :], kst[:, 2 * n + m, :], ACT.Square,
                                             accum_out=kss[:, 2 * n + m:2 * n + m + 1]).then_inc(A["k_ss"], 1)
                    return
                st.need(act, "proj_done", 12 * i + u + 1)
                if st.rms:
                    j = u - 4
                    st.need(act, "ss_done", 8 * i + j)
                    nc.scalar.activation(sq[:, :], pb[u % 2][:, :], ACT.Square).then_inc(A["q_sq"], 1)
                cols = slice(n * HALF, (n + 1) * HALF)
                if kind == "k":
                    dst = k_sb[:, cols]
                elif kind == "v":
                    dst = vst[:, :, :].rearrange("p t d -> p (t d)")[:, cols]
                else:
                    dst = q_sb[:, (2 * g + n) % 2, :]
                nc.scalar.activation(dst, pb[u % 2][:, :],
                                     ACT.Copy).then_inc(A["q_free" if st.rms else "proj_free"], 1)

            def k_scale(i, n):
                st.need(act, "kt_done", 2 * i + n + 1)
                st.need(act, "kf_ready", 1)
                nc.scalar.activation(k_sb[:, n * HALF:(n + 1) * HALF], pb[2 + n][:, :], ACT.Copy,
                                     scale=kfac[:, 0:1]).then_inc(A["kt_ready"], 1)

            def v_high(i, n):
                st.need(act, "vt_done", 2 * i + n + 1)
                nc.scalar.activation(vh[:, 4 * n:4 * n + 4, :], pb[7][:, :].rearrange("p (t d) -> p t d", t=4),
                                     ACT.Copy).then_inc(A["v_hi"], 1)

            def exponentials(i, j):
                g, n = j // 2, j % 2
                st.need(act, "s_sub", 8 * i + j + 1)
                nc.scalar.activation(hn(sc_sb, g, n), hn(sc_sb, g, n), ACT.Exp).then_inc(A["exp_done"], 1)

            def run(i, events):
                for kind, n in events:
                    if kind == "U":
                        unit(i, n)
                    elif kind == "KT":
                        k_scale(i, n)
                    elif kind == "VT":
                        v_high(i, n)
                    elif kind == "SC":
                        exponentials(i, n)
                    elif kind == "T":
                        st.need(act, "t_done", 8 * (i - 1) + n + 1)
                        nc.scalar.activation(pth[:, :], pb[4][:, :], ACT.Copy).then_inc(A["pt_hi"], 1)
                    elif kind == "PV":
                        st.need(act, "pv_done", 8 * (i - 1) + n + 1)
                        nc.scalar.activation(oth[:, :], pb[5][:, :], ACT.Copy).then_inc(A["o_hi"], 1)
                    elif kind == "WS":
                        if not (isinstance(i, int) and i == NKV):
                            st.need(act, "proj_done", 12 * i + 1)
                        else:
                            st.need(act, "wo_done", 8 * (i - 1))
                        for c in range(G):
                            act.wait_ge(ld_o[c], 16 * (NKV * st.index + i))
                            nc.scalar.activation(woh[:, c, :], raw[:, c, :], ACT.Copy).then_inc(A["wo_hi"], 1)

            if st.before:
                act.wait_ge(*stage_end(st.before))
            lag = 3 if st.rms else 1
            run(0, later(schedule(st.rms, True, False), ("SC",), lag))
            with act.Fori(1, NKV) as i:
                run(i, later(schedule(st.rms, True, True), ("SC",), lag))
            for kind, t in schedule(st.rms, False, True):
                run(NKV, [(kind, t)])
                if kind == "PV" and t >= 2 and st.name != "attn0":
                    act_transpose_tile(act, st.name, t - 2, pb[t % 2])
            if st.name != "attn0":
                for t in (NT - 2, NT - 1):
                    act_transpose_tile(act, st.name, t, pb[t % 2])

        def dve_attention(dve, st):
            def unit(i, u):
                kind, g, n = st.units[u]
                bank = pb[u % 2]
                if kind == "kv":
                    st.need(dve, "proj_done", 12 * i + u + 1)
                    st.need(dve, "v_ready", 2 * (i - 1) + n // 2 + 1)
                    kv = bank[:, :].rearrange("p (t c d) -> p t c d", t=2, c=2)
                    nc.vector.tensor_copy(kst[:, 2 * n:2 * n + 2, :], kv[:, :, 0, :])
                    nc.vector.tensor_copy(vst[:, 2 * n:2 * n + 2, :], kv[:, :, 1, :]).then_inc(A["kv_free"], 1)

            def k_mean_square(i, n):
                st.need(dve, "k_ss", 8 * i + 2 * n + 2)
                nc.vector.tensor_scalar(kms[:, 2 * n:2 * n + 2], kss[:, 2 * n:2 * n + 2], 1.0 / HD, EPS,
                                        ALU.mult, ALU.add).then_inc(A["k_ms"], 1)

            def k_normalise(i, n):
                st.need(dve, "k_rs", 4 * i + n + 1)
                for m in range(2):
                    t = 2 * n + m
                    last = nc.vector.tensor_scalar(kst[:, t, :], kst[:, t, :], rk[:, t:t + 1], None, ALU.mult)
                last.then_inc(A["k_nrm"], 1)

            def v_low(i, n):
                st.need(dve, "v_hi", 2 * i + n + 1)
                nc.vector.tensor_tensor(vl[:, 4 * n:4 * n + 4, :], pb[7][:, :].rearrange("p (t d) -> p t d", t=4),
                                        f32(vh[:, 4 * n:4 * n + 4, :]), ALU.subtract).then_inc(A["v_ready"], 1)

            def q_mean_square(i, j):
                g, n = j // 2, j % 2
                st.need(dve, "ss_done", 8 * i + j + 1)
                st.need(dve, "q_rs", 8 * (i - 1) + j + 1)
                nc.vector.tensor_scalar(qms[:, 4 * n:4 * n + 4, g], pb[7][:, 0:4], 1.0 / HD, EPS,
                                        ALU.mult, ALU.add).then_inc(A["ss_out"], 1)

            def scores(i, j):
                g, n = j // 2, j % 2
                bank = pb[2 + j % 2][:, :].rearrange("p (t s) -> p t s", t=4)
                dst = hn(sc_sb, g, n)
                st.need(dve, "sc_done", 8 * i + j + 1)
                st.need(dve, "p_ready", 8 * i)
                if st.per_head_bias:
                    dve.wait_ge(ld_b, 16 * (1 + i + 1))
                else:
                    dve.wait_ge(ld_b, 16 * (1 if st.index == 0 else 10))
                b = bias[:, g if st.per_head_bias else 0, :].rearrange("p (o s) -> p o s", o=1)
                if st.rms:
                    st.need(dve, "q_rs", 8 * i + j + 1)
                for h in range(2):
                    p0, p1 = 64 * h, 64 * h + 64
                    if st.rms:
                        last = nc.vector.tensor_tensor(
                            dst[p0:p1], bank[p0:p1, :, p0:p1],
                            hn(rq, g, n)[p0:p1].rearrange("p (t o) -> p t o", o=1).to_broadcast([64, 4, S]), ALU.mult)
                    else:
                        last = nc.vector.scalar_tensor_tensor(
                            dst[p0:p1], bank[p0:p1, :, p0:p1], st.scale, b[p0:p1].to_broadcast([64, 4, S]),
                            ALU.mult, ALU.add)
                last.then_inc(A["s_out"], 1)
                st.need(dve, "s_out", 8 * i + j + 1)
                if st.rms:
                    nc.vector.tensor_tensor(dst, dst, b.to_broadcast([P, 4, S]), ALU.add).then_inc(A["s_msk"], 1)
                    st.need(dve, "s_msk", 8 * i + j + 1)
                nc.vector.tensor_reduce(hn(smax, g, n), dst, AX_X, ALU.max).then_inc(A["s_max"], 1)
                st.need(dve, "s_max", 8 * i + j + 1)
                nc.vector.tensor_tensor(
                    dst, dst, hn(smax, g, n).rearrange("p (t o) -> p t o", o=1).to_broadcast([P, 4, S]),
                    ALU.subtract).then_inc(A["s_sub"], 1)

            def sums(i, j):
                g, n = j // 2, j % 2
                st.need(dve, "exp_done", 8 * i + j + 1)
                nc.vector.tensor_reduce(hn(ssum, g, n), hn(sc_sb, g, n), AX_X, ALU.add).then_inc(A["s_sum"], 1)
                st.need(dve, "s_sum", 8 * i + j + 1)
                nc.vector.reciprocal(hn(rs, g, n), hn(ssum, g, n)).then_inc(A["s_inv"], 1)
                st.need(dve, "s_inv", 8 * i + j + 1)
                nc.vector.tensor_tensor(
                    hn(rs2, g, n), hn(rs, g, n).rearrange("p (t o) -> p t o", o=1).to_broadcast([P, 4, 2]),
                    own_half[:, :].rearrange("p (o c) -> p o c", o=1).to_broadcast([P, 4, 2]),
                    ALU.mult).then_inc(A["s_rec"], 1)

            def run(i, events):
                for kind, n in events:
                    if kind == "U":
                        unit(i, n)
                        if st.rms and n < 4:
                            k_mean_square(i, n)
                            if n >= 1:
                                k_normalise(i, n - 1)
                            if n == 3:
                                k_normalise(i, 3)
                    elif kind == "VT":
                        v_low(i, n)
                    elif kind == "SQ":
                        q_mean_square(i, n)
                    elif kind == "SC":
                        scores(i, n)
                    elif kind == "SUM":
                        sums(i, n)
                    elif kind == "T":
                        st.need(dve, "pt_hi", 8 * (i - 1) + n + 1)
                        nc.vector.tensor_tensor(ptl[:, :], pb[4][:, :], f32(pth[:, :]),
                                                ALU.subtract).then_inc(A["pt_ready"], 1)
                    elif kind == "PV":
                        st.need(dve, "o_hi", 8 * (i - 1) + n + 1)
                        nc.vector.tensor_tensor(otl[:, :], pb[5][:, :], f32(oth[:, :]),
                                                ALU.subtract).then_inc(A["o_ready"], 1)
                    elif kind == "WO":
                        st.need(dve, "wo_done", 8 * (i - 1) + n + 1)
                        nc.vector.tensor_tensor(xtile(n), pb[6][:, :], xtile(n), ALU.add).then_inc(A["x_added"], 1)
                    elif kind == "WS":
                        for c in range(G):
                            st.need(dve, "wo_hi", 4 * (i - 1) + c + 1)
                            nc.vector.tensor_tensor(wol[:, c, :], raw[:, c, :], f32(woh[:, c, :]),
                                                    ALU.subtract).then_inc(A["wo_ready"], 1)

            def order(project, attend):
                ev = schedule(st.rms, project, attend)
                ev = later(ev, ("SC",), 2 if st.rms else 0) if st.rms else ev
                both = []
                for e in ev:
                    both.append(e)
                    if e[0] == "SC":
                        both.append(("SUM", e[1]))
                return later(both, ("SUM",), 3 if st.rms else 2)

            if st.before:
                dve.wait_ge(*stage_end(st.before))
            else:
                dve.wait_ge(x_in, 16)
                dve.wait_ge(const_in, 32)
            if st.rms:
                dve.wait_ge(const_in, 16 * 3)
                nc.vector.scalar_tensor_tensor(kfac[:, :], norm_w[:, 0:1], HD ** -0.5, norm_w[:, 1:2],
                                               ALU.mult, ALU.mult).then_inc(A["kf_ready"], 1)
                dve.wait_ge(A["kf_ready"], 1)
            run(0, order(True, False))
            with dve.Fori(1, NKV) as i:
                run(i, order(True, True))
            for kind, t in schedule(st.rms, False, True):
                run(NKV, [(kind, t)])
                if kind == "WO":
                    st.need(dve, "x_added", 56 + t + 1)
                    dve_norm_stats(dve, st.name, t, xtile(t))
                    if t >= 1:
                        dve_normalise(dve, st.name, t - 1, xtile(t - 1), xtile(t - 1))
                if kind == "PV" and t >= 2 and st.name != "attn0":
                    dve_transpose_tile(dve, st.name, t - 2, pb[t % 2])
            dve_normalise(dve, st.name, NT - 1, xtile(NT - 1), xtile(NT - 1))
            if st.name != "attn0":
                for t in (NT - 2, NT - 1):
                    dve_transpose_tile(dve, st.name, t, pb[t % 2])

        def pool_attention(pool, st):
            def split_chunk(i, c):
                slot = c if c < 5 else 4
                pool.wait_ge(ld_w[c], 16 * (NKV * st.index + i + 1))
                st.need(pool, "proj_done", 12 * (i - 1) + st.last_unit_of(c) + 1)
                src = raw[:, slot, :]
                hi, lo = (w[:, c].rearrange("p k n -> p (k n)") for w in (wh, wl))
                carry_waits(pool, pool_passed)
                nc.gpsimd.tensor_scalar(hi, src, 1.0, 0.0, ALU.mult, ALU.add).then_inc(A["w_hi"], 1)
                st.need(pool, "w_hi", 6 * i + c + 1)
                nc.gpsimd.tensor_tensor(lo, src, f32(hi), ALU.subtract).then_inc(A["w_ready"], 1)

            def split_v(i, n):
                st.need(pool, "kv_free", 4 * i + 2 * n + 2)
                st.need(pool, "pv_done", 8 * (i - 1) + 4 * n + 4)
                hi, lo, src = vh[:, 4 * n:4 * n + 4, :], vl[:, 4 * n:4 * n + 4, :], vst[:, 4 * n:4 * n + 4, :]
                carry_waits(pool, pool_passed)
                nc.gpsimd.tensor_scalar(hi, src, 1.0, 0.0, ALU.mult, ALU.add).then_inc(A["v_hi"], 1)
                st.need(pool, "v_hi", 2 * i + n + 1)
                nc.gpsimd.tensor_tensor(lo, src, f32(hi), ALU.subtract).then_inc(A["v_ready"], 1)

            def normalise(i, t):
                st.need(pool, "s_rec", 8 * i + (7 if t < 4 else 8))
                st.need(pool, "t_done", 8 * (i - 1) + t + 1)
                nc.gpsimd.tensor_tensor(
                    probs[:, t, :, :].rearrange("p g (c s) -> p g c s", c=2),
                    sc_sb[:, t, :, :].rearrange("p g (o s) -> p g o s", o=1).to_broadcast([P, G, 2, S]),
                    rs2[:, t, :, :].rearrange("p g (c o) -> p g c o", o=1).to_broadcast([P, G, 2, S]),
                    ALU.mult).then_inc(A["p_ready"], 1)

            def k_root(i, n):
                st.need(pool, "k_ms", 4 * i + n + 1)
                nc.gpsimd.tensor_tensor(rk[:, 2 * n:2 * n + 2], kms[:, 2 * n:2 * n + 2], mhalf[:, 0:2],
                                        ALU.pow).then_inc(A["k_rs"], 1)

            def q_root(i, j):
                g, n = j // 2, j % 2
                st.need(pool, "ss_out", 8 * i + j + 1)
                nc.gpsimd.tensor_tensor(hn(rq, g, n), hn(qms, g, n), mhalf[:, 0:4], ALU.pow).then_inc(A["q_rs"], 1)

            def step(i, more):
                if st.rms:
                    for n in range(4):
                        k_root(i, n)
                    if more:
                        split_chunk(i + 1, 0)
                        split_chunk(i + 1, 1)
                    for j in range(8):
                        q_root(i, j)
                        if more and j % 2 and j < 6:
                            split_chunk(i + 1, 2 + j // 2)
                    split_v(i, 0)
                    for t in range(4):
                        normalise(i, t)
                    split_v(i, 1)
                    for t in range(4, NT):
                        normalise(i, t)
                    if more:
                        split_chunk(i + 1, 5)
                else:
                    if more:
                        for c in range(5):
                            split_chunk(i + 1, c)
                    for t in range(NT):
                        normalise(i, t)
                    if more:
                        split_chunk(i + 1, 5)

            if st.before:
                pool.wait_ge(*stage_end(st.before))
            for c in range(2):
                split_chunk(0, c)
            if not st.before:
                pool.wait_ge(x0_ready, 2)
            for c in range(2, 6):
                split_chunk(0, c)
            step(0, True)
            with pool.Fori(1, NKV - 1) as i:
                step(i, True)
            step(NKV - 1, False)
            for t in range(NT):
                pool_norm_root(pool, st.name, t)

        XB = dict(k=(pb[0], pb[7]), q=(pb[1], pb[2]), kt=pb[3], qt=pb[4], gm=pb[5], out=pb[6])

        def sp_xattn(sp):
            sp.wait_ge(*stage_end("attn0"))
            sp.dma_start(x_wraw[:, :, :], a["x_wqk"]).then_inc(xs["w0"], 16)
            sp.dma_start(x_wv[:, :, :], a["x_wv"]).then_inc(xs["w1"], 16)
            sp.dma_start(x_wo[:, :, :], a["x_wo"]).then_inc(xs["w1"], 16)
            sp.dma_start(x_bg[:, :], a["x_bg"]).then_inc(xs["w2"], 16)
            sp.dma_start(x_blk[:, :], a["x_blk"]).then_inc(xs["w2"], 16)

            def load(p):
                wait(sp, xs["csp"], p)
                src = a["ctx"][p] if isinstance(p, int) else a["ctx"][bass.ds(p, 1)].rearrange("o p n -> p (o n)")
                sp.dma_start(x_craw[:, :], src).then_inc(xs["cin"], 16)
                wait(sp, xs["g"], 2 * p)
                src = a["ctxT_pair"][p] if isinstance(p, int) else \
                    a["ctxT_pair"][bass.ds(p, 1)].rearrange("o p n -> p (o n)")
                sp.dma_start(x_ct[:, :, :].rearrange("p k n -> p (k n)"), src).then_inc(xs["ctin"], 16)
            load(0)
            with sp.Fori(1, NT) as p:
                load(p)

        def x_steps(new, mid, old):
            ev = [("OUT", 0, 1), ("KT", 7, 1), ("QT", 6, 1), ("K", 0, 0), ("Q", 0, 0), ("QS", 7, 1), ("RD", 0, 2)]
            ev += [("K", 1, 0), ("Q", 1, 0), ("QS", 0, 0), ("KT", 0, 0), ("QT", 7, 1), ("RD", 1, 2)]
            ev += [("K", 2, 0), ("Q", 2, 0), ("QS", 1, 0), ("KT", 1, 0), ("QT", 0, 0), ("G", 1, 1), ("Y", 0, 2)]
            ev += [("K", 3, 0), ("Q", 3, 0), ("QS", 2, 0), ("KT", 2, 0), ("QT", 1, 0), ("M", 1, 1), ("XN", 0, 2)]
            ev += [("OUT", 1, 1), ("K", 4, 0), ("Q", 4, 0), ("QS", 3, 0), ("KT", 3, 0), ("QT", 2, 0), ("XT", 0, 2)]
            ev += [("OC", 0, 1), ("K", 5, 0), ("Q", 5, 0), ("QS", 4, 0), ("KT", 4, 0), ("QT", 3, 0), ("G", 0, 0)]
            ev += [("K", 6, 0), ("Q", 6, 0), ("QS", 5, 0), ("KT", 5, 0), ("QT", 4, 0), ("M", 0, 0)]
            ev += [("K", 7, 0), ("Q", 7, 0), ("QS", 6, 0), ("SP", 0, -1), ("KT", 6, 0), ("QT", 5, 0), ("VAR", 0, 1)]
            live = {-1: new, 0: new, 1: mid, 2: old}
            return [e for e in ev if live[e[2]]]

        def x_run(run):
            run(0, x_steps(True, False, False))
            run(1, x_steps(True, True, False))

        def x_end(run):
            run(NT - 1, [e for e in x_steps(True, True, True) if e[0] != "SP"])
            run(NT, x_steps(False, True, True))
            run(NT + 1, x_steps(False, False, True))

        def pe_xattn(pe):
            pe.wait_ge(xs["woc"], 1)
            for h in range(XH):
                r0 = 64 * (h % 2)
                last = nc.tensor.matmul(pb[5 + h % 2][0:64, (h // 2) * S:(h // 2 + 1) * S], x_wv[r0:r0 + 64, h // 2, :],
                                        x_woc[r0:r0 + 64, h // 2, :], start=True, stop=True)
            last.then_inc(xs["u"], 1)
            pe.wait_ge(xs["w2"], 32)
            nc.tensor.matmul(pb[7][:, 0:1], x_blk[:, :], x_bg[:, 0:1], start=True, stop=True).then_inc(xs["bm"], 1)
            pe.wait_ge(xs["wsp"], 1)
            pe.wait_ge(xs["u_out"], 1)
            pe.wait_ge(xs["bc"], 1)
            pe.wait_ge(xs["zero"], 1)

            def run(p, events):
                for kind, u, age in events:
                    b, s = u // 4, u % 4
                    r = slice(64 * b, 64 * b + 64)
                    q = p - age
                    if kind == "K":
                        if u == 0:
                            wait(pe, xs["csp"], q + 1)
                        wait(pe, xs["kexp"], 8 * q + u - 1)
                        cols = slice(s * P, (s + 1) * P)
                        mm3(XB["k"][u % 2][:, :], (x_wh[r, 1, cols], x_wl[r, 1, cols]), (x_ch[r, :], x_cl[r, :]), True,
                            True).then_inc(xs["k"], 1)
                    elif kind == "Q":
                        if u == 0:
                            wait(pe, xs["xsp"], q + 1)
                        wait(pe, xs["qsub"], 8 * q + u - 1)
                        cols = slice(s * P, (s + 1) * P)
                        mm3(XB["q"][u % 2][:, :], (x_xh[r, cols], x_xl[r, cols]), (x_wh[r, 0, :], x_wl[r, 0, :]), True,
                            True).then_inc(xs["q"], 1)
                    elif kind == "KT":
                        wait(pe, xs["kexp"], 8 * q + u + 1)
                        wait(pe, xs["ekt"], 8 * q + u)
                        for n in range(4):
                            last = nc.tensor.transpose(XB["kt"][:, n * P:(n + 1) * P],
                                                       x_ek[:, u % 2, n * P:(n + 1) * P], ident[:, :])
                        last.then_inc(xs["kt"], 1)
                    elif kind == "QT":
                        wait(pe, xs["qn"], 8 * q + u + 1)
                        wait(pe, xs["qcp"], 8 * q + u)
                        for n in range(4):
                            last = nc.tensor.transpose(XB["qt"][:, n * P:(n + 1) * P],
                                                       x_en[:, u % 2, n * P:(n + 1) * P], ident[:, :])
                        last.then_inc(xs["qt"], 1)
                    elif kind == "G":
                        wait(pe, xs["ekt"], 8 * q + 4 * u + 4)
                        wait(pe, xs["ctin"], 16 * (q + 1))
                        if u == 0:
                            wait(pe, xt_ready, p - 1)
                        else:
                            wait(pe, xs["sd"], p - 1)
                        wait(pe, xs["mr"], 2 * q + u)
                        for n in range(4):
                            last = nc.tensor.matmul(XB["gm"][0:64, :], x_ct[:, n, 64 * u:64 * u + 64],
                                                    x_ekT[:, u, n, :], start=n == 0, stop=n == 3)
                        last.then_inc(xs["g"], 1)
                    elif kind == "M":
                        wait(pe, xs["gt"], 2 * q + u + 1)
                        for n in range(4):
                            last = nc.tensor.matmul(XB["gm"][:, n * P:(n + 1) * P], x_gt[0:64, u, n * P:(n + 1) * P],
                                                    x_u[0:64, n * P:(n + 1) * P], start=True, stop=True)
                        last.then_inc(xs["m"], 1)
                    elif kind == "OUT":
                        wait(pe, xs["mr"], 2 * q + u + 1)
                        wait(pe, xs["qcp"], 8 * q + 4 * u + 4)
                        wait(pe, xs["osq"], q)
                        for n in range(4):
                            last = nc.tensor.matmul(XB["out"][:, :], x_m[:, n, u, :], x_q[:, u, n, :],
                                                    start=(u == 0 and n == 0), stop=(u == 1 and n == 3))
                        last.then_inc(xs["out"], 1)
                    elif kind == "VAR":
                        wait(pe, xs["osq"], q + 1)
                        wait(pe, xt_ready, p - 1)
                        wait(pe, xs["mr"], 2 * NT if isinstance(p, int) and p == NT else 2 * p + 1)
                        nc.tensor.matmul(XB["gm"][:, :], x_blk[:, :], x_sq[:, :], start=True,
                                         stop=True).then_inc(xs["var"], 1)
                    elif kind == "XT":
                        wait(pe, ln_done, 8 + q + 1)
                        wait(pe, xs["sd"], q + 1)
                        wait(pe, xs["mr"], 2 * NT if isinstance(p, int) and p > NT else 2 * p)
                        for k in range(KT):
                            last = nc.tensor.transpose(XB["gm"][:, k * P:(k + 1) * P], x_xn[:, k * P:(k + 1) * P],
                                                       ident[:, :])
                        last.then_inc(xt_done, 1)
            x_run(run)
            with pe.Fori(2, NT - 1) as p:
                run(p, x_steps(True, True, True))
            x_end(run)

        def act_xattn(act):
            act.wait_ge(*stage_end("attn0"))
            act.wait_ge(xs["w0"], 16)
            nc.scalar.activation(x_wh[:, :, :], x_wraw[:, :, :], ACT.Copy).then_inc(xs["chi"], 1)
            act.wait_ge(xs["u"], 1)
            for h in range(2):
                last = nc.scalar.activation(
                    x_u[0:64, :].rearrange("p (k c o) -> p k c o", k=4, c=2)[:, :, h, :],
                    pb[5 + h][0:64, 0:4 * S].rearrange("p (k o) -> p k o", k=4), ACT.Copy)
            last.then_inc(xs["u_out"], 1)
            act.wait_ge(xs["bc"], 1)

            def split_high(q):
                wait(act, xs["cin"], 16 * (q + 1))
                wait(act, xs["k"], 8 * q)
                nc.scalar.activation(x_ch[:, :], x_craw[:, :], ACT.Copy).then_inc(xs["chi"], 1)
                wait(act, xs["q"], 8 * q)
                nc.scalar.activation(x_xh[:, :], xtile(q), ACT.Copy).then_inc(xs["xhi"], 1)

            def run(p, events):
                for kind, u, age in events:
                    b, s = u // 4, u % 4
                    q = p - age
                    if kind == "SP":
                        split_high(q)
                    elif kind == "K":
                        wait(act, xs["kneg"], 8 * q + u + 1)
                        wait(act, xs["kt"], 8 * q + u - 1)
                        wait(act, xs["krz"], 2 * (q - 1) + b + 1)
                        nc.scalar.activation(x_ek[:, u % 2, :], XB["k"][u % 2][:, :], ACT.Exp, bias=x_knm[:, u:u + 1],
                                             accum_out=x_kz[:, u:u + 1]).then_inc(xs["kexp"], 1)
                    elif kind == "Q":
                        wait(act, xs["qsub"], 8 * q + u + 1)
                        nc.scalar.activation(x_e[:, s, :], x_e[:, s, :], ACT.Exp).then_inc(xs["qexp"], 1)
                    elif kind == "KT":
                        wait(act, xs["kt"], 8 * q + u + 1)
                        wait(act, xs["g"], 2 * (q - 1) + b + 1)
                        nc.scalar.activation(x_ekT[:, b, :, s * P:(s + 1) * P],
                                             XB["kt"][:, :].rearrange("p (n d) -> p n d", n=4),
                                             ACT.Copy).then_inc(xs["ekt"], 1)
                    elif kind == "QT":
                        wait(act, xs["qt"], 8 * q + u + 1)
                        wait(act, xs["out"], 2 * (q - 1) + b + 1)
                        nc.scalar.activation(x_q[:, b, :, s * P:(s + 1) * P],
                                             XB["qt"][:, :].rearrange("p (h n) -> p h n", h=4),
                                             ACT.Copy).then_inc(xs["qcp"], 1)
                    elif kind == "G":
                        wait(act, xs["g"], 2 * q + u + 1)
                        nc.scalar.activation(x_gt[0:64, u, :], XB["gm"][0:64, :], ACT.Copy).then_inc(xs["gt"], 1)
                    elif kind == "OC":
                        wait(act, xs["out"], 2 * q + 2)
                        wait(act, xs["y"], q)
                        nc.scalar.activation(x_oc[:, :], XB["out"][:, :], ACT.Identity,
                                             bias=x_bc[:, 0:1]).then_inc(xs["oc"], 1)
                        wait(act, xs["var"], q)
                        nc.scalar.activation(x_sq[:, :], XB["out"][:, :], ACT.Square,
                                             bias=x_bc[:, 0:1]).then_inc(xs["osq"], 1)
                    elif kind == "VAR":
                        wait(act, xs["var"], q + 1)
                        wait(act, xs["rd"], 2 * q)
                        nc.scalar.activation(x_sd[:, :], XB["gm"][:, :], ACT.Sqrt,
                                             bias=x_eps[:, 0:1]).then_inc(xs["sd"], 1)
                    elif kind == "XT":
                        wait(act, xt_done, q + 1)
                        t0 = q * P
                        cols = slice(t0, t0 + P) if isinstance(p, int) else bass.ds(t0, P)
                        nc.scalar.activation(xTh[:, :, cols], XB["gm"][:, :].rearrange("p (k n) -> p k n", k=KT),
                                             ACT.Copy).then_inc(xt_hi, 1)
                        wait(act, ln_done, 8 + q + 1)
                        nc.scalar.activation(xtile(q), x_xn[:, :], ACT.Copy).then_inc(xs["xcp"], 1)
            act.wait_ge(ln_done, 8)
            split_high(0)
            x_run(run)
            with act.Fori(2, NT - 1) as p:
                run(p, x_steps(True, True, True))
            x_end(run)

        def dve_xattn(dve):
            dve.wait_ge(xs["w1"], 32)
            nc.vector.tensor_reduce(x_wos[:, :], x_wo[:, :, :], AX_X, ALU.add).then_inc(xs["wos"], 1)
            dve.wait_ge(xs["wos"], 1)
            nc.vector.scalar_tensor_tensor(
                x_woc[:, :, :], x_wos[:, :].rearrange("p (k o) -> p k o", o=1).to_broadcast([P, 4, S]), -1.0 / S,
                x_wo[:, :, :], ALU.mult, ALU.add).then_inc(xs["woc"], 1)
            dve.wait_ge(xs["chi"], 1)
            nc.vector.tensor_tensor(x_wl[:, :, :], x_wraw[:, :, :], f32(x_wh[:, :, :]),
                                    ALU.subtract).then_inc(xs["wsp"], 1)
            nc.vector.memset(x_eps[:, :], EPS)
            dve.wait_ge(xs["bm"], 1)
            nc.vector.tensor_tensor(x_bc[:, :], x_bg[:, 0:1], pb[7][:, 0:1], ALU.subtract).then_inc(xs["bc"], 1)

            def split_low(q):
                wait(dve, xs["chi"], q + 2)
                nc.vector.tensor_tensor(x_cl[:, :], x_craw[:, :], f32(x_ch[:, :]),
                                        ALU.subtract).then_inc(xs["csp"], 1)
                wait(dve, xs["xhi"], q + 1)
                nc.vector.tensor_tensor(x_xl[:, :], xtile(q), f32(x_xh[:, :]),
                                        ALU.subtract).then_inc(xs["xsp"], 1)

            def run(p, events):
                for kind, u, age in events:
                    b, s = u // 4, u % 4
                    q = p - age
                    if kind == "SP":
                        split_low(q)
                    elif kind == "K":
                        wait(dve, xs["k"], 8 * q + u + 1)
                        nc.vector.tensor_reduce(x_kmx[:, u:u + 1], XB["k"][u % 2][:, :], AX_X,
                                                ALU.max).then_inc(xs["kmax"], 1)
                        wait(dve, xs["kmax"], 8 * q + u + 1)
                        wait(dve, xs["kexp"], 8 * (q - 1) + u + 1)
                        nc.vector.tensor_scalar(x_knm[:, u:u + 1], x_kmx[:, u:u + 1], -1.0, None,
                                                ALU.mult).then_inc(xs["kneg"], 1)
                    elif kind == "Q":
                        bank = XB["q"][u % 2][:, :].rearrange("p (h d) -> p h d", h=XH)
                        wait(dve, xs["q"], 8 * q + u + 1)
                        nc.vector.tensor_reduce(x_qmx[:, s, :], bank, AX_X, ALU.max).then_inc(xs["qmax"], 1)
                        wait(dve, xs["qmax"], 8 * q + u + 1)
                        wait(dve, xs["qn"], 8 * q + u - 3)
                        nc.vector.tensor_tensor(
                            x_e[:, s, :].rearrange("p (h d) -> p h d", h=XH), bank,
                            x_qmx[:, s, :].rearrange("p (h o) -> p h o", o=1).to_broadcast([P, XH, XD]),
                            ALU.subtract).then_inc(xs["qsub"], 1)
                    elif kind == "QS":
                        wait(dve, xs["qexp"], 8 * q + u + 1)
                        nc.vector.tensor_reduce(x_qs[:, s, :], x_e[:, s, :].rearrange("p (h d) -> p h d", h=XH), AX_X,
                                                ALU.add).then_inc(xs["qsum"], 1)
                        wait(dve, xs["qsum"], 8 * q + u + 1)
                        nc.vector.reciprocal(x_qr[:, s, :], x_qs[:, s, :]).then_inc(xs["qrec"], 1)
                    elif kind == "G":
                        wait(dve, xs["kexp"], 8 * q + 4 * u + 4)
                        wait(dve, xs["mr"], 2 * (q - 1) + u + 1)
                        nc.vector.reciprocal(x_krz[:, 4 * u:4 * u + 4], x_kz[:, 4 * u:4 * u + 4]).then_inc(xs["krz"], 1)
                    elif kind == "M":
                        wait(dve, xs["m"], 2 * q + u + 1)
                        wait(dve, xs["krz"], 2 * q + u + 1)
                        wait(dve, xs["out"], 2 * (q - 1) + u + 1)
                        bank = XB["gm"][:, :].rearrange("p (h o) -> p h o", h=4)
                        for h in range(2):
                            r = slice(64 * h, 64 * h + 64)
                            last = nc.vector.scalar_tensor_tensor(
                                x_m[r, :, u, 64 * u:64 * u + 64], bank[r, :, 64 * h:64 * h + 64], XD ** -0.5,
                                x_krz[r, 4 * u:4 * u + 4].rearrange("p (h o) -> p h o", o=1).to_broadcast([64, 4, S]),
                                ALU.mult, ALU.mult)
                        last.then_inc(xs["mr"], 1)
                    elif kind == "RD":
                        wait(dve, xs["sd"], q + 1)
                        half = slice(u * DM // 2, (u + 1) * DM // 2)
                        nc.vector.reciprocal(x_rd[:, half], x_sd[:, half]).then_inc(xs["rd"], 1)
                    elif kind == "Y":
                        wait(dve, xs["rd"], 2 * q + 2)
                        nc.vector.scalar_tensor_tensor(x_y[:, :], x_oc[:, :], x_bg[:, 1:2], x_rd[:, :], ALU.mult,
                                                       ALU.mult).then_inc(xs["y"], 1)
                        wait(dve, xs["y"], q + 1)
                        nc.vector.tensor_tensor(x_r[:, :], x_y[:, :], xtile(q), ALU.add).then_inc(xs["r"], 1)
                        wait(dve, xs["r"], q + 1)
                        nc.vector.bn_stats(st6[:, 0, :], x_r[:, :]).then_inc(ln_bn, 1)
                        dve.wait_ge(ln_bn, 8 + q + 1)
                        carry_waits(dve, dve_passed)
                        nc.vector.bn_aggr(mv[:, 0, :], st6[:, 0, :]).then_inc(ln_ag, 1)
                        dve.wait_ge(ln_ag, 8 + q + 1)
                        nc.vector.tensor_scalar(var_eps[:, 0:1], mv[:, 0, 1:2], EPS, None,
                                                ALU.add).then_inc(ln_stat, 1)
                    elif kind == "XN":
                        dve.wait_ge(ln_rstd, 8 + q + 1)
                        nc.vector.tensor_scalar(x_xn[:, :], x_r[:, :], mv[:, 0, 0:1], rstd[:, 0:1],
                                                ALU.subtract, ALU.mult).then_inc(ln_done, 1)
                    elif kind == "XT":
                        dve.wait_ge(xt_hi, q + 1)
                        t0 = q * P
                        cols = slice(t0, t0 + P) if isinstance(p, int) else bass.ds(t0, P)
                        nc.vector.tensor_tensor(xTl[:, :, cols], XB["gm"][:, :].rearrange("p (k n) -> p k n", k=KT),
                                                f32(xTh[:, :, cols]), ALU.subtract).then_inc(xt_ready, 1)
            split_low(0)
            x_run(run)
            with dve.Fori(2, NT - 1) as p:
                run(p, x_steps(True, True, True))
            x_end(run)

        def pool_xattn(pool):
            pool.wait_ge(*stage_end("attn0"))
            nc.gpsimd.memset(x_m[:, :, :, :], 0.0).then_inc(xs["zero"], 1)

            def run(p, events):
                for kind, u, age in events:
                    s = u % 4
                    q = p - age
                    if kind == "QS":
                        wait(pool, xs["qrec"], 8 * q + u + 1)
                        wait(pool, xs["qt"], 8 * q + u - 1)
                        nc.gpsimd.tensor_tensor(
                            x_en[:, u % 2, :].rearrange("p (h d) -> p h d", h=XH),
                            x_e[:, s, :].rearrange("p (h d) -> p h d", h=XH),
                            x_qr[:, s, :].rearrange("p (h o) -> p h o", o=1).to_broadcast([P, XH, XD]),
                            ALU.mult).then_inc(xs["qn"], 1)
                    elif kind == "Y":
                        pool.wait_ge(ln_stat, 8 + q + 1)
                        nc.gpsimd.tensor_tensor(rstd[:, 0:1], var_eps[:, 0:1], mhalf[:, 0:1],
                                                ALU.pow).then_inc(ln_rstd, 1)
            x_run(run)
            with pool.Fori(2, NT - 1) as p:
                run(p, x_steps(True, True, True))
            x_end(run)

        def sp_ffn0(sp):
            sp.wait_ge(*stage_end("xattn0"))
            for h in range(2):
                sp.dma_start(f_c[:, :, :], a["ctxT"][:, 2 * h:2 * h + 2, :]).then_inc(fs["cin"], 16) if h == 0 else None

            def load(i):
                for c in range(3):
                    wait(sp, fs["dq"], 3 * (i - 1) + c + 1)
                    q, s = a["f_q"], a["f_s"]
                    if isinstance(i, int):
                        q, s = q[i, c], s[i:i + 1, c].to_broadcast([P, 1024])
                    else:
                        q = q[bass.ds(i, 1), c].rearrange("o p n -> p (o n)")
                        s = s[bass.ds(i, 1), c].to_broadcast([P, 1024])
                    sp.dma_start(f_q[:, c, :], q).then_inc(fs[f"in{c}"], 16)
                    sp.dma_start(f_s[:, c, :], s).then_inc(fs[f"in{c}"], 16)
            load(0)
            load(1)
            sp.wait_ge(fs["c"], 2)
            sp.dma_start(f_c[:, :, :], a["ctxT"][:, 2:4, :]).then_inc(fs["cin"], 16)
            with sp.Fori(2, NF) as i:
                load(i)

        def f_gate(m, which, k):
            return slice((which * KT + k) * P, (which * KT + k + 1) * P)

        def pe_ffn0(pe):
            pe.wait_ge(xt_ready, 8)

            def step(i):
                for u in range(4):
                    n, m = u // 2, u % 2
                    wait(pe, fs["w"], 3 * i + m + 1)
                    wait(pe, fs["it"], 4 * i + u - 1)
                    cols = slice(n * HALF, (n + 1) * HALF)
                    for which in range(2):
                        for k in range(KT):
                            w = f_gate(m, which, k)
                            last = mm3(pb[2 * which + u % 2][:, :], (f_wh[:, m, w], f_wl[:, m, w]),
                                       (xTh[:, k, cols], xTl[:, k, cols]), k == 0, k == KT - 1)
                    last.then_inc(fs["gu"], 1)
                for t in range(NT):
                    wait(pe, fs["w"], 3 * i + 3)
                    wait(pe, fs["i"], 4 * i + (2 if t < 4 else 4))
                    wait(pe, fs["add"], 8 * i + t - 1)
                    for m in range(2):
                        h = slice(t * P, (t + 1) * P)
                        w = slice(m * DM, (m + 1) * DM)
                        last = mm3(pb[4 + t % 2][:, :], (f_ih[:, m, h], f_il[:, m, h]),
                                   (f_wh[:, 2, w], f_wl[:, 2, w]), m == 0, m == 1)
                    last.then_inc(fs["dn"], 1)
            step(0)
            with pe.Fori(1, NF) as i:
                step(i)
            for t in range(NT):
                pe_transpose_tile(pe, "ffn0", t, pb[t % 2], (fs["it"], 4 * NF))

        def act_ffn0(act):
            act.wait_ge(*stage_end("xattn0"))

            def high_weight(i, c):
                wait(act, fs["dq"], 3 * i + c + 1)
                if c < 2:
                    wait(act, fs["gu"], 4 * (i - 1) + 3 + c)
                else:
                    wait(act, fs["dn"], 8 * i)
                nc.scalar.activation(f_wh[:, c, :], f_w[:, c, :], ACT.Copy).then_inc(fs["whi"], 1)

            def silu(i, u):
                wait(act, fs["gu"], 4 * i + u + 1)
                wait(act, fs["it"], 4 * i + u - 1)
                nc.scalar.activation(f_sg[:, u % 2, :], pb[u % 2][:, :], ACT.Silu).then_inc(fs["sg"], 1)

            def high_hidden(i, u):
                n, m = u // 2, u % 2
                wait(act, fs["it"], 4 * i + u + 1)
                wait(act, fs["dn"], 8 * (i - 1) + 4 * n + 4)
                nc.scalar.activation(f_ih[:, m, n * HALF:(n + 1) * HALF], f_it[:, u % 2, :],
                                     ACT.Copy).then_inc(fs["ihi"], 1)

            def step(i, more):
                for u in range(4):
                    silu(i, u)
                    if u >= 1:
                        high_hidden(i, u - 1)
                    if u == 2 and more:
                        high_weight(i + 1, 0)
                high_hidden(i, 3)
                if more:
                    high_weight(i + 1, 1)
                    high_weight(i + 1, 2)
            for c in range(3):
                high_weight(0, c)
            step(0, True)
            with act.Fori(1, NF - 1) as i:
                step(i, True)
            step(NF - 1, False)
            for t in range(NT):
                act_transpose_tile(act, "ffn0", t, pb[t % 2])

        def dve_ffn0(dve):
            def dequantise(i, c):
                for s in (f"in{c}",):
                    wait(dve, fs[s], 32 * (i + 1))
                wait(dve, fs["w"], 3 * (i - 1) + c + 1)
                nc.vector.tensor_tensor(f_w[:, c, :], f_q[:, c, :], f_s[:, c, :], ALU.mult).then_inc(fs["dq"], 1)

            def hidden(i, u):
                wait(dve, fs["sg"], 4 * i + u + 1)
                wait(dve, fs["i"], 4 * i + u - 1)
                nc.vector.tensor_tensor(f_it[:, u % 2, :], pb[2 + u % 2][:, :], f_sg[:, u % 2, :],
                                        ALU.mult).then_inc(fs["it"], 1)

            def step(i, more, last):
                hidden(i, 0)
                hidden(i, 1)
                hidden(i, 2)
                if more:
                    dequantise(i + 1, 0)
                hidden(i, 3)
                if more:
                    dequantise(i + 1, 1)
                    dequantise(i + 1, 2)
                for t in range(NT):
                    wait(dve, fs["dn"], 8 * i + t + 1)
                    wait(dve, fs["add"], 8 * (i - 1) + t + 1)
                    nc.vector.tensor_tensor(xtile(t), pb[4 + t % 2][:, :], xtile(t), ALU.add).then_inc(fs["add"], 1)
                    if last:
                        wait(dve, fs["add"], 8 * i + t + 1)
                        dve_norm_stats(dve, "ffn0", t, xtile(t))
                        if t >= 1:
                            dve_normalise(dve, "ffn0", t - 1, xtile(t - 1), xtile(t - 1))
            dve.wait_ge(xs["xcp"], 8)
            for c in range(3):
                dequantise(0, c)
            step(0, True, False)
            with dve.Fori(1, NF - 1) as i:
                step(i, True, False)
            step(NF - 1, False, True)
            dve_normalise(dve, "ffn0", NT - 1, xtile(NT - 1), xtile(NT - 1))
            for t in range(NT):
                dve_transpose_tile(dve, "ffn0", t, pb[t % 2])

        def pool_ffn0(pool):
            def low_weight(i, c):
                wait(pool, fs["whi"], 3 * i + c + 1)
                nc.gpsimd.tensor_tensor(f_wl[:, c, :], f_w[:, c, :], f32(f_wh[:, c, :]),
                                        ALU.subtract).then_inc(fs["w"], 1)

            def low_hidden(i, u):
                n, m = u // 2, u % 2
                cols = slice(n * HALF, (n + 1) * HALF)
                wait(pool, fs["ihi"], 4 * i + u + 1)
                nc.gpsimd.tensor_tensor(f_il[:, m, cols], f_it[:, u % 2, :], f32(f_ih[:, m, cols]),
                                        ALU.subtract).then_inc(fs["i"], 1)

            def split_context(h):
                pool.wait_ge(fs["cin"], 16 * (h + 1))
                for m in range(2):
                    k = 2 * h + m
                    carry_waits(pool, pool_passed)
                    nc.gpsimd.tensor_scalar(cTh[:, k, :], f_c[:, m, :], 1.0, 0.0, ALU.mult,
                                            ALU.add).then_inc(fs["chi"], 1)
                    pool.wait_ge(fs["chi"], k + 1)
                    nc.gpsimd.tensor_tensor(cTl[:, k, :], f_c[:, m, :], f32(cTh[:, k, :]),
                                            ALU.subtract).then_inc(fs["c"], 1)

            def step(i, more):
                for u in range(4):
                    low_hidden(i, u)
                    if u == 2 and more:
                        low_weight(i + 1, 0)
                if more:
                    low_weight(i + 1, 1)
                    low_weight(i + 1, 2)
            for c in range(3):
                low_weight(0, c)
            step(0, True)
            split_context(0)
            split_context(1)
            with pool.Fori(1, NF - 1) as i:
                step(i, True)
            step(NF - 1, False)
            for t in range(NT):
                pool_norm_root(pool, "ffn0", t)

        def g_part(tile, k, what):
            if what == "base":
                return tile[:, k * DM:(k + 1) * DM]
            if what == "gate":
                return tile[:, KT * DM + k * GC:KT * DM + (k + 1) * GC]
            return tile[:, KT * DM + KT * GC:]

        def sp_ffn1(sp):
            sp.wait_ge(*stage_end("xattn1"))
            sp.dma_start(g_raw[:, 0:KT * DM], a["g_base"]).then_inc(gs["in"], 16)
            sp.dma_start(g_raw[:, KT * DM:KT * DM + KT * GC], a["g_gate"]).then_inc(gs["in"], 16)
            sp.dma_start(g_raw[:, KT * DM + KT * GC:], a["g_b"]).then_inc(gs["in"], 16)
            sp.dma_start(g_bb[:, :], a["g_bbase"].to_broadcast([P, DM])).then_inc(gs["in"], 16)
            sp.dma_start(g_bt[:, :], a["g_bthr"].to_broadcast([P, 1])).then_inc(gs["in"], 16)
            for t in range(NT):
                sp.wait_ge(ln_done, 8 * LN_NORMS["ffn1"] + t + 1)
                sp.dma_start(a["out"][t * P:(t + 1) * P, :], g_o[:, t % 2, :]).then_inc(gs[f"out{t % 2}"], 16)
            for h in range(2):
                sp.wait_ge(gs[f"out{h}"], 16 * (NT // 2))

        def dve_ffn1(dve):
            dve.wait_ge(gs["hi"], 1)
            nc.vector.tensor_tensor(g_l[:, :], g_raw[:, :], f32(g_h[:, :]), ALU.subtract).then_inc(gs["w"], 1)
            NG = E_ * R_
            count = [0]

            def link(ins):
                ins.then_inc(gs["ch"], 1)
                count[0] += 1
                dve.wait_ge(gs["ch"], count[0])

            def route(t):
                dve.wait_ge(gs["p1"], t + 1)
                nc.vector.tensor_copy(g_hid[:, t, :], pb[2 + t % 2][:, 0:GC]).then_inc(gs["ev"], 1)
                dve.wait_ge(gs["ev"], t + 1)
                link(nc.vector.tensor_reduce(g_mx[:, t:t + 1], g_hid[:, t, NG:NG + E_], AX_X, ALU.max))
                nc.vector.tensor_scalar(g_e[:, t, E_:E_ + 2], g_hid[:, t, NG + E_:NG + E_ + 2], g_bt[:, 0:1], -1.0,
                                        ALU.add, ALU.mult)
                nc.vector.tensor_scalar(g_e[:, t, 0:E_], g_hid[:, t, NG:NG + E_], g_mx[:, t:t + 1], None,
                                        ALU.subtract).then_inc(gs["res"], 1)
                dve.wait_ge(gs["exp"], t + 1)
                nc.vector.tensor_scalar(g_sum[:, t, 1:2], g_e[:, t, E_:E_ + 1], 1.0, None, ALU.add)
                link(nc.vector.tensor_reduce(g_sum[:, t, 0:1], g_e[:, t, 0:E_], AX_X, ALU.add))
                link(nc.vector.reciprocal(g_rec[:, t, :], g_sum[:, t, :]))
                link(nc.vector.tensor_scalar(g_ad[:, t, :], g_e[:, t, 0:E_], g_rec[:, t, 0:1], None, ALU.mult))
                link(nc.vector.scalar_tensor_tensor(g_w[:, t, :], g_rec[:, t, 1:2].to_broadcast([P, E_]), -0.125,
                                                    g_ad[:, t, :], ALU.mult, ALU.add))
                link(nc.vector.tensor_scalar(g_wn[:, t, :], g_w[:, t, :], 0.0, None, ALU.max))
                link(nc.vector.tensor_reduce(g_ws[:, t, 0:1], g_wn[:, t, :], AX_X, ALU.add))
                link(nc.vector.tensor_scalar(g_ws[:, t, 1:2], g_ws[:, t, 0:1], 0.0, None, ALU.is_equal))
                link(nc.vector.tensor_tensor(g_ws[:, t, 0:1], g_ws[:, t, 0:1], g_ws[:, t, 1:2], ALU.add))
                link(nc.vector.reciprocal(g_wr[:, t:t + 1], g_ws[:, t, 0:1]))
                link(nc.vector.tensor_scalar(g_wn[:, t, :], g_wn[:, t, :], g_wr[:, t:t + 1], 2.0, ALU.mult, ALU.mult))
                nc.vector.tensor_tensor(
                    g_z[:, t, :].rearrange("p (e r) -> p e r", e=E_),
                    g_hid[:, t, 0:NG].rearrange("p (e r) -> p e r", e=E_),
                    g_wn[:, t, :].rearrange("p (e o) -> p e o", o=1).to_broadcast([P, E_, R_]),
                    ALU.mult).then_inc(gs["z"], 1)

            def low_z(t):
                dve.wait_ge(gs["zhi"], t + 1)
                nc.vector.tensor_tensor(g_zl[:, t % 2, :], pb[4 + t % 2][:, 0:P], f32(g_zh[:, t % 2, :]),
                                        ALU.subtract).then_inc(gs["zr"], 1)

            def finish(t):
                dve.wait_ge(gs["p2"], t + 1)
                link(nc.vector.tensor_tensor(xtile(t), pb[t % 2][:, :], xtile(t), ALU.add))
                link(nc.vector.tensor_tensor(xtile(t), xtile(t), g_bb[:, :], ALU.add))
                dve_norm_stats(dve, "ffn1", t, xtile(t))

            def emit(t):
                if t >= 2:
                    dve.wait_ge(gs[f"out{t % 2}"], 16 * (t // 2))
                dve_normalise(dve, "ffn1", t, xtile(t), g_o[:, t % 2, :])
            for t in range(NT):
                route(t)
                if t >= 1:
                    low_z(t - 1)
                if t >= 2:
                    finish(t - 2)
                if t >= 3:
                    emit(t - 3)
            low_z(NT - 1)
            finish(NT - 2)
            emit(NT - 3)
            finish(NT - 1)
            emit(NT - 2)
            emit(NT - 1)

        def pe_ffn1(pe):
            pe.wait_ge(gs["w"], 1)
            pe.wait_ge(xt_ready, 32)

            def first(t):
                h = slice(t * P, (t + 1) * P)
                if t >= 2:
                    pe.wait_ge(gs["ev"], t - 1)
                for k in range(KT):
                    last = mm3(pb[2 + t % 2][:, 0:GC], (xTh[:, k, h], xTl[:, k, h]),
                               (g_part(g_h, k, "gate"), g_part(g_l, k, "gate")), k == 0, k == KT - 1)
                last.then_inc(gs["p1"], 1)

            def base(t):
                h = slice(t * P, (t + 1) * P)
                if t >= 2:
                    pe.wait_ge(ln_bn, 8 * LN_NORMS["ffn1"] + t - 1)
                for k in range(KT):
                    mm3(pb[t % 2][:, :], (xTh[:, k, h], xTl[:, k, h]),
                        (g_part(g_h, k, "base"), g_part(g_l, k, "base")), k == 0, False)

            def transpose(t):
                pe.wait_ge(gs["z"], t + 1)
                if t >= 2:
                    pe.wait_ge(gs["zr"], t - 1)
                nc.tensor.transpose(pb[4 + t % 2][:, 0:P], g_z[:, t, :], ident[:, :]).then_inc(gs["zt"], 1)

            def experts(t):
                pe.wait_ge(gs["zr"], t + 1)
                mm3(pb[t % 2][:, :], (g_zh[:, t % 2, :], g_zl[:, t % 2, :]),
                    (g_part(g_h, 0, "up"), g_part(g_l, 0, "up")), False, True).then_inc(gs["p2"], 1)
            first(0)
            first(1)
            for t in range(NT):
                base(t)
                transpose(t)
                if t + 2 < NT:
                    first(t + 2)
                experts(t)

        def act_ffn1(act):
            act.wait_ge(*stage_end("xattn1"))
            act.wait_ge(gs["in"], 80)
            nc.scalar.activation(g_h[:, :], g_raw[:, :], ACT.Copy).then_inc(gs["hi"], 1)

            def high_z(t):
                act.wait_ge(gs["zt"], t + 1)
                if t >= 2:
                    act.wait_ge(gs["p2"], t - 1)
                nc.scalar.activation(g_zh[:, t % 2, :], pb[4 + t % 2][:, 0:P], ACT.Copy).then_inc(gs["zhi"], 1)
            for t in range(NT):
                act.wait_ge(gs["res"], t + 1)
                nc.scalar.activation(g_e[:, t, :], g_e[:, t, :], ACT.Exp).then_inc(gs["exp"], 1)
                high_z(t)

        block = ctx.enter_context(nc.Block())

        @block.sync
        def _(sp):
            sp.dma_start(ident[:, :], a["ident"]).then_inc(const_in, 16)
            sp.dma_start(own_half[:, :], a["own_half"]).then_inc(const_in, 16)
            for n in range(2):
                cols = slice(n * HALF, (n + 1) * HALF)
                sp.dma_start(probs[:, :, :, :].rearrange("p t g n -> p (t g n)").rearrange(
                    "p (k n) -> p k n", k=KT)[:, :, cols], a["xT"][:, :, cols]).then_inc(xr_in[n], 16)
            sp.dma_start(X[:, :].rearrange("p (t d) -> p t d", t=NT), a["x"]).then_inc(x_in, 16)
            sp_attention(sp, stages[0])
            sp_xattn(sp)
            sp_ffn0(sp)
            sp_attention(sp, stages[1])
            sp_attention(sp, stages[2])
            sp_ffn1(sp)

        @block.tensor
        def _(pe):
            pe_attention(pe, stages[0])
            pe_xattn(pe)
            pe_ffn0(pe)
            pe_attention(pe, stages[1])
            pe_attention(pe, stages[2])
            pe_ffn1(pe)

        @block.scalar
        def _(act):
            xin = probs[:, :, :, :].rearrange("p t g n -> p (t g n)").rearrange("p (k n) -> p k n", k=KT)
            for n in range(2):
                cols = slice(n * HALF, (n + 1) * HALF)
                act.wait_ge(xr_in[n], 16)
                nc.scalar.activation(xTh[:, :, cols], xin[:, :, cols], ACT.Copy).then_inc(x0_hi, 1)
            act_attention(act, stages[0])
            act_xattn(act)
            act_ffn0(act)
            act_attention(act, stages[1])
            act_attention(act, stages[2])
            act_ffn1(act)

        @block.vector
        def _(dve):
            xin = probs[:, :, :, :].rearrange("p t g n -> p (t g n)").rearrange("p (k n) -> p k n", k=KT)
            for n in range(2):
                cols = slice(n * HALF, (n + 1) * HALF)
                dve.wait_ge(x0_hi, n + 1)
                nc.vector.tensor_tensor(xTl[:, :, cols], xin[:, :, cols], f32(xTh[:, :, cols]),
                                        ALU.subtract).then_inc(x0_ready, 1)
            dve_attention(dve, stages[0])
            dve_xattn(dve)
            dve_ffn0(dve)
            dve_attention(dve, stages[1])
            dve_attention(dve, stages[2])
            dve_ffn1(dve)

        @block.gpsimd
        def _(pool):
            nc.gpsimd.memset(mhalf[:, :], -0.5).then_inc(const_set, 1)
            nc.gpsimd.memset(onecol[:, :], 1.0).then_inc(const_set, 1)
            pool.wait_ge(const_set, 2)
            pool_attention(pool, stages[0])
            pool_xattn(pool)
            pool_ffn0(pool)
            pool_attention(pool, stages[1])
            pool_attention(pool, stages[2])
            for t in range(NT):
                pool_norm_root(pool, "ffn1", t)


def kernel(**inputs):
    import numpy as np
    import concourse.bacc as bacc
    from concourse.bass_utils import run_bass_kernel_spmd

    v = {k: np.asarray(x) for k, x in inputs.items()}

    def col(w):
        return w.T.reshape(-1, P, w.shape[0]).transpose(1, 0, 2)

    def chunks(wq, wk, wv, order):
        q = col(wq).reshape(P, KT, NKV, G, HD).transpose(2, 3, 0, 1, 4)
        k = col(wk).reshape(P, KT, NKV, 1, HD).transpose(2, 3, 0, 1, 4)
        w = col(wv).reshape(P, KT, NKV, 1, HD).transpose(2, 3, 0, 1, 4)
        parts = {"q": q, "k": k, "v": w}
        return np.concatenate([parts[o] for o in order], axis=1).reshape(NKV, 6, P, KT * HD)

    def outs(wo):
        return wo.T.reshape(NKV, G, HD, DM)

    x2 = v["x"].reshape(TOK, DM)
    c2 = v["ctx_4096"].reshape(TOK, DM)
    cT = c2.T.reshape(KT, P, TOK).transpose(1, 0, 2)
    nq = NKV * G * HD
    wqkv = v["L1_attn_w_qkv"].T
    wkv = v["L0_xattn_Wkv"]
    twice = lambda w: np.concatenate([w, w], axis=0)

    def ffn_in(q):
        return q.T.reshape(KT, P, NF, 2, P)
    gq, uq = ffn_in(v["L0_ffn_gate_q"]), ffn_in(v["L0_ffn_up_q"])
    gu = np.stack([gq, uq]).transpose(3, 4, 2, 0, 1, 5).reshape(NF, 2, P, 1024)
    dq = v["L0_ffn_down_q"].T.reshape(NF, 1, 2, P, DM).transpose(0, 1, 3, 2, 4).reshape(NF, 1, P, 1024)
    f_q = np.concatenate([gu, dq], axis=1)
    sc = lambda s: s.T.reshape(KT, NF, 2, P)
    gus = np.stack([sc(v["L0_ffn_gate_s"]), sc(v["L0_ffn_up_s"])]).transpose(2, 3, 0, 1, 4).reshape(NF, 2, 1024)
    ds = v["L0_ffn_down_s"].T.reshape(NF, 1, 1024)
    f_s = np.concatenate([gus, ds], axis=1)

    pos = np.arange(S)
    rel = np.tile(pos[:, None] - pos[None, :], (2, 1))
    causal = np.where(rel >= 0, 0.0, NEG).astype(np.float32)
    slopes = ((2.0 ** (-8.0 / (NKV * G))) ** np.arange(1, NKV * G + 1, dtype=np.float32)).astype(np.float32)
    root = np.sqrt(np.maximum(rel, 0).astype(np.float32))
    alibi = np.where(rel[None] >= 0, -slopes[:, None, None] * root[None], np.float32(NEG)).astype(np.float32)
    alibi = alibi.reshape(NKV, G, P, S).transpose(0, 2, 1, 3).reshape(NKV, P, G * S)
    blk = np.kron(np.eye(2), np.full((S, S), 1.0 / S)).astype(np.float32)

    gate = np.concatenate([v["L1_ffn_A_w"].reshape(E_ * R_, DM), v["L1_ffn_W_gate"], v["L1_ffn_W_thr"][None],
                           np.zeros((1, DM), np.float32)], axis=0)
    up = v["L1_ffn_B_w"].transpose(0, 2, 1).reshape(E_ * R_, DM)

    data = {
        "x": x2.reshape(NT, P, DM).transpose(1, 0, 2),
        "xT": x2.T.reshape(KT, P, TOK).transpose(1, 0, 2),
        "ctx": c2.reshape(NT, P, DM),
        "ctxT": cT,
        "ctxT_pair": cT.reshape(P, KT, NT, P).transpose(2, 0, 1, 3).reshape(NT, P, KT * P),
        "ident": np.eye(P, dtype=np.float32),
        "own_half": np.kron(np.eye(2), np.ones((S, 1))).astype(np.float32),
        "causal": causal, "alibi": alibi,
        "mask": twice(v["mask_1x1xSxS2_ff0"].reshape(S, S)),
        "norm_w": np.stack([v["L1_xattn_q_norm_w"], v["L1_xattn_k_norm_w"]], axis=1),
        "a0_in": chunks(v["L0_attn_wq"], v["L0_attn_wk"], v["L0_attn_wv"], "kqv"),
        "a0_out": outs(v["L0_attn_wo"]),
        "a1_in": chunks(wqkv[:nq], wqkv[nq:nq + NKV * HD], wqkv[nq + NKV * HD:], "kqv"),
        "a1_out": outs(v["L1_attn_w_o"].T),
        "a2_in": chunks(v["L1_xattn_q_proj_w"], v["L1_xattn_k_proj_w"], v["L1_xattn_v_proj_w"], "kvq"),
        "a2_out": outs(v["L1_xattn_o_proj_w"]),
        "x_wqk": np.stack([twice(v["L0_xattn_Wq"].T), twice(wkv[:XW].T)], axis=1),
        "x_wv": wkv[XW:].reshape(4, P, S).transpose(1, 0, 2),
        "x_wo": v["L0_xattn_Wout"].T.reshape(4, P, S).transpose(1, 0, 2),
        "x_bg": np.stack([np.tile(v["L0_xattn_b_out"], 2), np.tile(v["L0_xattn_g"].reshape(S), 2)], axis=1),
        "x_blk": blk,
        "f_q": f_q, "f_s": f_s,
        "g_base": col(v["L1_ffn_W_base"]).reshape(P, KT * DM),
        "g_gate": col(gate).reshape(P, KT * GC),
        "g_b": up,
        "g_bbase": v["L1_ffn_b_base"].reshape(1, DM),
        "g_bthr": v["L1_ffn_b_thr"].reshape(1, 1),
    }
    nc = bacc.Bacc("TRN2", target_bir_lowering=False, num_devices=1)
    arrays, args = {}, {}
    for name, x in data.items():
        x = np.ascontiguousarray(x)
        arrays["in_" + name] = x
        args[name] = nc.dram_tensor("in_" + name, x.shape, mybir.dt.from_np(x.dtype), kind="ExternalInput").ap()
    args["out"] = nc.dram_tensor("out_0", (TOK, DM), F32, kind="ExternalOutput").ap()
    program(nc, args)
    r = run_bass_kernel_spmd(nc, [arrays], core_ids=[0])
    return r.results[0]["out_0"].reshape(B, S, DM)
```

```python
from contextlib import ExitStack

import concourse.bass as bass
from concourse import mybir

F32 = mybir.dt.float32
F32R = mybir.dt.float32r
I32 = mybir.dt.int32
ALU = mybir.AluOpType
ACT = mybir.ActivationFunctionType
AX_X = mybir.AxisListType.X

P = 128
B, S, DM = 16, 64, 512
TOK = B * S
NT = TOK // P
KT = DM // P
NKV, G, HD = 8, 4, 128
HALF = TOK // 2
EPS = 1e-5

XH, XD = 8, 64
XW = XH * XD

FI = 1792
FSTEP = 256
NF = FI // FSTEP

E_, R_ = 8, 16
GC = E_ * R_ + E_ + 2

NEG = -1.0e30


def wait(eng, sem, n):
    if isinstance(n, int) and n <= 0:
        return
    eng.wait_ge(sem, n)


def carry_waits(eng, waits_passed):
    eng.sem_inc(waits_passed, 1)


def units(rms):
    q = [("q", g, n) for g in range(G) for n in range(2)]
    if rms:
        return [("kv", 0, n) for n in range(4)] + q
    return [("k", 0, 0), ("k", 0, 1)] + q + [("v", 0, 0), ("v", 0, 1)]


def schedule(rms, project, attend, last=True):
    split = [("WS", c) for c in range(G)]
    if not project:
        ev = [("WP", 7), ("T", 0)] if rms else [("T", 0), ("WP", 7)]
        ev += [split[0], ("PV", 0), split[1], ("T", 1), split[2], split[3]]
        for t in range(NT):
            ev += [("PV", t + 1)] * (t + 1 < NT) + [("T", t + 2)] * (t + 2 < NT) + [("WO", t)]
        return ev
    ev = [("U", 0), ("WP", 7), ("U", 1)] + split + [("U", 2), ("T", 0), ("U", 3)]
    if rms:
        ev += [("U", 4), ("PV", 0), ("KT", 0), ("T", 1), ("U", 5), ("KT", 1), ("WO", 0), ("SQ", 0), ("SC", 0)]
        for t in range(1, NT - 1):
            ev += [("PV", t), ("SQ", t), ("T", t + 1), ("U", 5 + t), ("SC", t), ("WO", t)]
        ev += [("PV", 7), ("SQ", 7), ("SC", 7)]
    else:
        ev.append(("SC", 0))
        for t in range(NT - 1):
            ev += [("PV", t), ("T", t + 1), ("U", 4 + t), ("SC", t + 1)] + [("WO", t)] * (t < NT - 2)
        ev += [("PV", 7), ("U", 11), ("VT", 0), ("WO", 6), ("VT", 1)]
    if not last:
        ev.remove(("WP", 7))
    return ev if attend else [e for e in ev if e[0] not in ("WS", "T", "PV", "WO", "WP")]


def later(events, kinds, by):
    out, held = [], []
    for e in events:
        if e[0] in kinds:
            held.append([by, e])
            continue
        out.append(e)
        for h in held:
            h[0] -= 1
        while held and held[0][0] <= 0:
            out.append(held.pop(0)[1])
    return out + [h[1] for h in held]


def program(nc, a):
    with ExitStack() as ctx:
        def sem(name):
            return ctx.enter_context(nc.semaphore(name))

        def keep(name, shape, dt=F32):
            return ctx.enter_context(nc.sbuf_tensor(name, shape, dt))

        X = keep("X", [P, NT * DM])
        xTh = keep("xTh", [P, KT, TOK], F32R)
        xTl = keep("xTl", [P, KT, TOK], F32R)
        cTh = keep("cTh", [P, KT, TOK], F32R)
        cTl = keep("cTl", [P, KT, TOK], F32R)
        ident = keep("ident", [P, P])
        st6 = keep("st6", [P, NT, 6])
        mv = keep("mv", [P, NT, 2])
        var_eps = keep("var_eps", [P, NT])
        rstd = keep("rstd", [P, NT])
        mhalf = keep("mhalf", [P, 32])
        onecol = keep("onecol", [P, 1])
        own_half = keep("own_half", [P, 2])

        pb = [ctx.enter_context(nc.psum_tensor(f"pb{i}", [P, 512], F32)) for i in range(8)]

        xT, cT = (xTh, xTl), (cTh, cTl)

        with ExitStack() as sa:
            def sb(name, shape, dt=F32):
                return sa.enter_context(nc.sbuf_tensor(name, shape, dt))
            wh = sb("wh", [P, 6, KT, P], F32R)
            wl = sb("wl", [P, 6, KT, P], F32R)
            q_sb = sb("q_sb", [P, 2, HALF])
            k_sb = sb("k_sb", [P, TOK])
            kst = sb("kst", [P, NT, HD])
            sq = sb("sq", [P, 2, HALF])
            raw = sb("raw", [P, 5, 512])
            woh = sb("woh", [P, G, DM], F32R)
            wol = sb("wol", [P, G, DM], F32R)
            vh = sb("vh", [P, NT, HD], F32R)
            vl = sb("vl", [P, NT, HD], F32R)
            pth = sb("pth", [P, G * P], F32R)
            ptl = sb("ptl", [P, G * P], F32R)
            oth = sb("oth", [P, 2, G * P], F32R)
            otl = sb("otl", [P, 2, G * P], F32R)
            vst = sb("vst", [P, NT, HD])
            sc_sb = sb("sc_sb", [P, NT, G, S])
            probs = sb("probs", [P, NT, G, P])
            smax = sb("smax", [P, NT, G])
            ssum = sb("ssum", [P, NT, G])
            rs = sb("rs", [P, NT, G])
            rs2 = sb("rs2", [P, NT, G, 2])
            bias = sb("bias", [P, G, S])
            junk = sb("junk", [P, HD])
            kss = sb("kss", [P, NT])
            kms = sb("kms", [P, NT])
            rk = sb("rk", [P, NT])
            qms = sb("qms", [P, NT, G])
            rq = sb("rq", [P, NT, G])
            norm_w = sb("norm_w", [P, 2])
            kfac = sb("kfac", [P, 1])

        with ExitStack() as sx:
            def sb(name, shape, dt=F32):
                return sx.enter_context(nc.sbuf_tensor(name, shape, dt))
            x_wraw = sb("x_wraw", [P, 2, XW])
            x_wh = sb("x_wh", [P, 2, XW], F32R)
            x_wl = sb("x_wl", [P, 2, XW], F32R)
            x_xh = sb("x_xh", [P, DM], F32R)
            x_xl = sb("x_xl", [P, DM], F32R)
            x_craw = sb("x_craw", [P, DM])
            x_ch = sb("x_ch", [P, DM], F32R)
            x_cl = sb("x_cl", [P, DM], F32R)
            x_wv = sb("x_wv", [P, 4, S])
            x_wo = sb("x_wo", [P, 4, S])
            x_woc = sb("x_woc", [P, 4, S])
            x_wos = sb("x_wos", [P, 4])
            x_u = sb("x_u", [64, XH * S])
            x_bg = sb("x_bg", [P, 2])
            x_bc = sb("x_bc", [P, 1])
            x_blk = sb("x_blk", [P, P])
            x_eps = sb("x_eps", [P, 1])
            x_ek = sb("x_ek", [P, 2, 512])
            x_e = sb("x_e", [P, 4, 512])
            x_en = sb("x_en", [P, 2, 512])
            x_ekT = sb("x_ekT", [P, 2, 4, 512])
            x_q = sb("x_q", [P, 2, 4, 512])
            x_ct = sb("x_ct", [P, 2, KT, XD])
            x_kmx = sb("x_kmx", [P, 8])
            x_knm = sb("x_knm", [P, 8])
            x_kz = sb("x_kz", [P, 8])
            x_krz = sb("x_krz", [P, 8])
            x_qmx = sb("x_qmx", [P, 4, XH])
            x_qs = sb("x_qs", [P, 4, XH])
            x_qr = sb("x_qr", [P, 4, XH])
            x_gt = sb("x_gt", [64, 2, 512])
            x_m = sb("x_m", [P, 4, 2, P])
            x_oc = sb("x_oc", [P, DM])
            x_sq = sb("x_sq", [P, DM])
            x_sd = sb("x_sd", [P, DM])
            x_rd = sb("x_rd", [P, DM])
            x_y = sb("x_y", [P, DM])
            x_r = sb("x_r", [P, DM])
            x_xn = sb("x_xn", [P, DM])

        with ExitStack() as sf:
            def sb(name, shape, dt=F32):
                return sf.enter_context(nc.sbuf_tensor(name, shape, dt))
            f_q = sb("f_q", [P, 3, 1024], I32)
            f_s = sb("f_s", [P, 3, 1024])
            f_sg = sb("f_sg", [P, 2, HALF])
            f_w = sb("f_w", [P, 3, 1024])
            f_wh = sb("f_wh", [P, 3, 1024], F32R)
            f_wl = sb("f_wl", [P, 3, 1024], F32R)
            f_it = sb("f_it", [P, 2, HALF])
            f_ih = sb("f_ih", [P, 2, TOK], F32R)
            f_il = sb("f_il", [P, 2, TOK], F32R)
            f_c = sb("f_c", [P, 2, TOK])

        with ExitStack() as sg:
            def sb(name, shape, dt=F32):
                return sg.enter_context(nc.sbuf_tensor(name, shape, dt))
            NGW = KT * DM + KT * GC + DM
            g_raw = sb("g_raw", [P, NGW])
            g_h = sb("g_h", [P, NGW], F32R)
            g_l = sb("g_l", [P, NGW], F32R)
            g_bb = sb("g_bb", [P, DM])
            g_bt = sb("g_bt", [P, 1])
            g_hid = sb("g_hid", [P, NT, GC])
            g_mx = sb("g_mx", [P, NT])
            g_e = sb("g_e", [P, NT, E_ + 2])
            g_sum = sb("g_sum", [P, 2, NT])
            g_rec = sb("g_rec", [P, 2, NT])
            g_ad = sb("g_ad", [P, NT, E_])
            g_w = sb("g_w", [P, NT, E_])
            g_wn = sb("g_wn", [P, NT, E_])
            g_ws = sb("g_ws", [P, 2, NT])
            g_wr = sb("g_wr", [P, NT])
            g_z = sb("g_z", [P, NT, P])
            g_zh = sb("g_zh", [P, 2, P], F32R)
            g_zl = sb("g_zl", [P, 2, P], F32R)
            g_o = sb("g_o", [P, 4, DM])

        def f32(ap):
            return ap.bitcast(F32)

        def mm3(out, w, x, start, stop):
            (w_hi, w_lo), (x_hi, x_lo) = w, x
            nc.tensor.matmul(out, w_hi, x_hi, start=start, stop=False)
            nc.tensor.matmul(out, w_hi, x_lo, start=False, stop=False)
            return nc.tensor.matmul(out, w_lo, x_hi, start=False, stop=stop)

        def xtile(t):
            return X[:, t * DM:(t + 1) * DM] if isinstance(t, int) else X[:, bass.ds(t * DM, DM)]

        const_in = sem("const_in")
        const_set = sem("const_set")
        pool_passed = sem("pool_passed")
        dve_passed = sem("dve_passed")
        x_in = sem("x_in")
        xr_in = [sem(f"xr_in{n}") for n in range(4)]
        x0_hi = sem("x0_hi")
        x0_ready = sem("x0_ready")

        ln_bn = sem("ln_bn")
        ln_ag = sem("ln_ag")
        ln_stat = sem("ln_stat")
        ln_rstd = sem("ln_rstd")
        ln_done = sem("ln_done")
        xt_done = sem("xt_done")
        xt_hi = sem("xt_hi")
        xt_ready = sem("xt_ready")
        LN_NORMS = {"attn0": 0, "xattn0": 1, "ffn0": 2, "attn1": 3, "xattn1": 4, "ffn1": 5}
        XT_NORMS = {"xattn0": 0, "ffn0": 1, "attn1": 2, "xattn1": 3}

        names = dict(
            proj_done=96,
            t_done=64,
            pv_done=64,
            wo_done=64,
            sc_done=64,
            pt_hi=64, o_hi=64,
            exp_done=64,
            wo_hi=32,
            proj_free=96,
            pt_ready=64, o_ready=64,
            wo_ready=32,
            x_added=64,
            s_out=64,
            s_max=64, s_sub=64, s_sum=64, s_inv=64, s_rec=64,
            w_hi=48, w_ready=48,
            vt_done=16,
            v_hi=16, v_ready=16,
            p_ready=64,
        )
        A = {n: sem(n) for n in names}
        for n in ("q_sq", "k_ss", "k_ms", "k_rs", "k_nrm", "kt_done", "kt_ready", "kv_free", "q_free", "ss_done", "ss_out",
                  "q_rs", "s_msk", "kf_ready"):
            A[n] = sem(n)
        ld_w = [sem(f"ld_w{c}") for c in range(6)]
        ld_o = [sem(f"ld_o{c}") for c in range(4)]
        ld_b = sem("ld_b")

        xs = {n: sem("x_" + n) for n in (
            "w0", "w1", "w2", "wsp", "wos", "woc", "u", "u_out", "bm", "bc", "zero", "cin", "ctin0", "ctin1", "xhi", "xsp", "chi",
            "csp", "k", "kmax", "kneg", "kexp", "kt", "ekt", "g", "gt", "m", "krz", "mr", "q", "qmax", "qsub", "qexp",
            "qsum", "qrec", "qn", "qt", "qcp", "out", "oc", "osq", "var", "sd", "rd", "y", "r", "xcp")}
        fs = {n: sem("f_" + n) for n in (
            "in0", "in1", "in2", "dq", "whi", "w", "gu", "sg", "it", "ihi", "i", "dn", "add", "cin", "chi", "c")}
        gs = {n: sem("g_" + n) for n in (
            "in0", "in1", "in2", "in3", "hi", "w", "p1", "ev", "ch", "exp", "z", "zt", "zhi", "zr", "p2", "res", "xb",
            "out0", "out1", "out2", "out3")}

        def stage_end(name):
            return {"attn0": (A["x_added"], 64), "xattn0": (xs["xcp"], 8), "ffn0": (fs["add"], NF * NT),
                    "attn1": (A["x_added"], 128), "xattn1": (A["x_added"], 192)}[name]

        def dve_norm_stats(dve, name, t, src):
            n = 8 * LN_NORMS[name]
            nc.vector.bn_stats(st6[:, t, :], src).then_inc(ln_bn, 1)
            dve.wait_ge(ln_bn, n + t + 1)
            nc.vector.bn_aggr(mv[:, t, :], st6[:, t, :]).then_inc(ln_ag, 1)
            dve.wait_ge(ln_ag, n + t + 1)
            nc.vector.tensor_scalar(var_eps[:, t:t + 1], mv[:, t, 1:2], EPS, None, ALU.add).then_inc(ln_stat, 1)

        def pool_norm_root(pool, name, t):
            n = 8 * LN_NORMS[name]
            pool.wait_ge(ln_stat, n + t + 1)
            nc.gpsimd.tensor_tensor(rstd[:, t:t + 1], var_eps[:, t:t + 1], mhalf[:, 0:1],
                                    ALU.pow).then_inc(ln_rstd, 1)

        def dve_normalise(dve, name, t, src, dst):
            dve.wait_ge(ln_rstd, 8 * LN_NORMS[name] + t + 1)
            nc.vector.tensor_scalar(dst, src, mv[:, t, 0:1], rstd[:, t:t + 1],
                                    ALU.subtract, ALU.mult).then_inc(ln_done, 1)

        def pe_transpose_tile(pe, name, t, bank, free):
            n = 8 * XT_NORMS[name]
            pe.wait_ge(ln_done, 8 * LN_NORMS[name] + t + 1)
            wait(pe, *free) if t < 2 else pe.wait_ge(xt_ready, n + t - 1)
            for k in range(KT):
                last = nc.tensor.transpose(bank[:, k * P:(k + 1) * P], X[:, t * DM + k * P:t * DM + (k + 1) * P],
                                           ident[:, :])
            last.then_inc(xt_done, 1)

        def act_transpose_tile(act, name, t, bank):
            n = 8 * XT_NORMS[name]
            act.wait_ge(xt_done, n + t + 1)
            nc.scalar.activation(xTh[:, :, t * P:(t + 1) * P], bank[:, :].rearrange("p (k n) -> p k n", k=KT),
                                 ACT.Copy).then_inc(xt_hi, 1)

        def dve_transpose_tile(dve, name, t, bank):
            n = 8 * XT_NORMS[name]
            dve.wait_ge(xt_hi, n + t + 1)
            nc.vector.tensor_tensor(xTl[:, :, t * P:(t + 1) * P], bank[:, :].rearrange("p (k n) -> p k n", k=KT),
                                    f32(xTh[:, :, t * P:(t + 1) * P]), ALU.subtract).then_inc(xt_ready, 1)

        class Stage:
            def __init__(self, name, index, rms, before, w_in, w_out, bias_in, per_head_bias, scale):
                self.name, self.index, self.rms, self.before = name, index, rms, before
                self.w_in, self.w_out, self.bias_in = w_in, w_out, bias_in
                self.per_head_bias, self.scale = per_head_bias, scale
                self.units = units(rms)
                self.k_c, self.v_c, self.q_c = (0, 1, 2) if rms else (0, 5, 1)

            def unit_read(self, i, u):
                if u < 0:
                    i, u = i - 1, u + 12
                if not self.rms:
                    return self.at("proj_free", 12 * i + u + 1)
                if u < 4:
                    return A["kv_free"], 4 * i + u + 1
                return A["q_free"], 8 * i + u - 3

            def chunk_of(self, u):
                kind, g, _ = self.units[u]
                return {"k": self.k_c, "v": self.v_c, "kv": self.v_c, "q": self.q_c + g}[kind]

            def last_unit_of(self, c):
                if self.rms and c < 2:
                    return 3
                return max(u for u in range(12) if self.chunk_of(u) == c)

            def at(self, name, n):
                return A[name], names.get(name, 0) * self.index + n

            def need(self, eng, name, n):
                if isinstance(n, int) and n <= 0:
                    return
                eng.wait_ge(*self.at(name, n))

        stages = [
            Stage("attn0", 0, False, None, a["a0_in"], a["a0_out"], a["causal"], False, HD ** -0.5),
            Stage("attn1", 1, False, "ffn0", a["a1_in"], a["a1_out"], a["alibi"], True, HD ** -0.5),
            Stage("xattn1", 2, True, "attn1", a["a2_in"], a["a2_out"], a["mask"], False, 1.0),
        ]

        def hn(ap4, g, n):
            return ap4[:, 4 * n:4 * n + 4, g]

        def input_quarter(n):
            half, k = n // 2, 2 * (n % 2)
            cols = slice(half * HALF, (half + 1) * HALF)
            stage = probs[:, :, :, :].rearrange("p t g n -> p (t g n)").rearrange("p (k n) -> p k n", k=KT)
            return stage[:, k:k + 2, cols], a["xT"][:, k:k + 2, cols]

        def input_split(tile, n):
            half, k = n // 2, 2 * (n % 2)
            return tile[:, k:k + 2, half * HALF:(half + 1) * HALF]

        def sp_attention(sp, st):
            def load_w(i, c, slot):
                src = st.w_in[i, c] if isinstance(i, int) else \
                    st.w_in[bass.ds(i, 1), c].rearrange("o p n -> p (o n)")
                sp.dma_start(raw[:, slot, :], src).then_inc(ld_w[c], 16)

            def load_o(i, c, slot):
                src = st.w_out[i, c] if isinstance(i, int) else \
                    st.w_out[bass.ds(i, 1), c].rearrange("o p n -> p (o n)")
                sp.dma_start(raw[:, slot, :], src).then_inc(ld_o[c], 16)

            def load_bias(i):
                if st.per_head_bias:
                    src = st.bias_in[i] if isinstance(i, int) else \
                        st.bias_in[bass.ds(i, 1)].rearrange("o p n -> p (o n)")
                    st.need(sp, "s_msk" if st.rms else "s_out", 8 * i)
                    sp.dma_start(bias[:, :, :].rearrange("p g s -> p (g s)"), src).then_inc(ld_b, 16)

            if st.before:
                sp.wait_ge(*stage_end(st.before))
            if st.name == "attn0":
                load_w(0, 0, 0)
                for n in range(4):
                    dst, src = input_quarter(n)
                    sp.dma_start(dst, src).then_inc(xr_in[n], 16)
                    if n == 1:
                        load_w(0, 1, 1)
                sp.dma_start(ident[:, :], a["ident"]).then_inc(const_in, 16)
                sp.dma_start(own_half[:, :], a["own_half"]).then_inc(const_in, 16)
            if not st.per_head_bias:
                sp.dma_start(bias[:, 0, :], st.bias_in).then_inc(ld_b, 16)
            if st.rms:
                sp.dma_start(norm_w[:, :], a["norm_w"]).then_inc(const_in, 16)
            for c in range(2 if st.name == "attn0" else 0, 5):
                load_w(0, c, c)
            if st.name == "attn0":
                sp.dma_start(X[:, :].rearrange("p (t d) -> p t d", t=NT), a["x"]).then_inc(x_in, 16)
            load_bias(0)
            st.need(sp, "w_ready", 5)
            load_w(0, 5, 4)

            def step(i, more):
                if more:
                    for c in range(5):
                        if c < 4:
                            st.need(sp, "wo_ready", 4 * (i - 1) + c + 1)
                        else:
                            st.need(sp, "w_ready", 6 * i + 6)
                        load_w(i + 1, c, c)
                for c in range(4):
                    if more:
                        st.need(sp, "w_ready", 6 * (i + 1) + c + 1)
                    else:
                        st.need(sp, "wo_ready", 4 * (i - 1) + c + 1)
                    load_o(i, c, c)
                if more:
                    load_bias(i + 1)
                    st.need(sp, "w_ready", 6 * (i + 1) + 5)
                    load_w(i + 1, 5, 4)

            step(0, True)
            with sp.Fori(1, NKV - 1) as i:
                step(i, True)
            step(NKV - 1, False)

        def pe_attention(pe, st):
            def unit(i, u):
                kind, g, n = st.units[u]
                c = st.chunk_of(u)
                if n == 0:
                    st.need(pe, "w_ready", 6 * i + c + 1)
                if not (isinstance(i, int) and i == 0 and u < 2):
                    wait(pe, *st.unit_read(i, u - 2))
                bank = pb[u % 2]
                w = lambda k: (wh[:, c, k, :], wl[:, c, k, :])
                if kind != "kv":
                    cols = slice(n * HALF, (n + 1) * HALF)
                    for k in range(KT):
                        if st.name == "attn0" and isinstance(i, int) and u < 2 and k % 2 == 0:
                            pe.wait_ge(x0_ready, 2 * u + k // 2 + 1)
                        last = mm3(bank[:, :], w(k), (xTh[:, k, cols], xTl[:, k, cols]), k == 0, k == KT - 1)
                else:
                    for m in range(2):
                        t = 2 * n + m
                        for k in range(KT):
                            last = mm3(bank[:, 2 * m * HD:2 * (m + 1) * HD],
                                       (cTh[:, k, t * P:(t + 1) * P], cTl[:, k, t * P:(t + 1) * P]),
                                       (wh[:, 0:2, k, :], wl[:, 0:2, k, :]), k == 0, k == KT - 1)
                last.then_inc(A["proj_done"], 1)

            def scores(i, j):
                g, n = j // 2, j % 2
                u = (4 if st.rms else 2) + j
                wait(pe, *st.unit_read(i, u))
                if st.rms:
                    st.need(pe, "kt_ready", 2 * i + 2)
                st.need(pe, "s_out", 8 * i + j - 1)
                bank = pb[2 + j % 2]
                for m in range(4):
                    t = 4 * n + m
                    last = nc.tensor.matmul(bank[:, m * P:(m + 1) * P], q_sb[:, j % 2, m * P:(m + 1) * P],
                                            k_sb[:, t * P:(t + 1) * P], start=True, stop=True)
                last.then_inc(A["sc_done"], 1)

            def square_sums(i, j):
                st.need(pe, "q_sq", 8 * i + j + 1)
                if j == 0:
                    st.need(pe, "kt_ready", 2 * i + 2)
                else:
                    st.need(pe, "ss_out", 8 * i + j)
                for m in range(4):
                    last = nc.tensor.matmul(pb[7][:, m:m + 1], sq[:, j % 2, m * P:(m + 1) * P], onecol[:, :],
                                            start=True, stop=True)
                last.then_inc(A["ss_done"], 1)

            def transpose_k(i, n):
                st.need(pe, "k_nrm", 4 * i + 2 * n + 2)
                if n == 0:
                    st.need(pe, "ss_out", 8 * i)
                else:
                    st.need(pe, "kt_ready", 2 * i + n)
                for m in range(4):
                    last = nc.tensor.transpose(pb[7][:, m * P:(m + 1) * P], kst[:, 4 * n + m, :], ident[:, :])
                last.then_inc(A["kt_done"], 1)

            def transpose_v(i, n):
                if st.name == "attn0" and isinstance(i, int) and i == 0:
                    pe.wait_ge(const_in, 32)
                st.need(pe, "proj_free", 12 * i + 11 + n)
                st.need(pe, "v_ready", 2 * i + n)
                for m in range(4):
                    last = nc.tensor.transpose(pb[7][:, m * P:(m + 1) * P], vst[:, 4 * n + m, :], ident[:, :])
                last.then_inc(A["vt_done"], 1)

            def transpose_probs(i, t):
                st.need(pe, "p_ready", 8 * i + t + 1)
                st.need(pe, "pt_ready", 8 * i + t)
                for g in range(G):
                    last = nc.tensor.transpose(pb[4][:, g * P:(g + 1) * P], probs[:, t, g, :], ident[:, :])
                last.then_inc(A["t_done"], 1)

            def probs_v(i, t):
                st.need(pe, "pt_ready", 8 * i + t + 1)
                st.need(pe, "v_ready", 2 * i + 1 + t // 4)
                st.need(pe, "o_ready", 8 * i + t)
                mm3(pb[5][:, :], (vh[:, t, :], vl[:, t, :]), (pth[:, :], ptl[:, :]), True,
                    True).then_inc(A["pv_done"], 1)

            def project_out(i, t):
                st.need(pe, "o_ready", 8 * i + t + 1)
                st.need(pe, "x_added", 8 * i + t)
                for g in range(G):
                    if t == 0:
                        st.need(pe, "wo_ready", 4 * i + g + 1)
                    last = mm3(pb[6][:, :], (oth[:, t % 2, g * P:(g + 1) * P], otl[:, t % 2, g * P:(g + 1) * P]),
                               (woh[:, g, :], wol[:, g, :]), g == 0, g == G - 1)
                last.then_inc(A["wo_done"], 1)

            def run(i, events):
                for kind, n in events:
                    if kind == "U":
                        unit(i, n)
                    elif kind == "SC":
                        scores(i, n)
                    elif kind == "SQ":
                        square_sums(i, n)
                    elif kind == "KT":
                        transpose_k(i, n)
                    elif kind == "VT":
                        transpose_v(i, n)
                    elif kind == "T":
                        transpose_probs(i - 1, n)
                    elif kind == "PV":
                        probs_v(i - 1, n)
                    elif kind == "WO":
                        project_out(i - 1, n)
                    elif kind == "WP":
                        project_out(i - 2, n)

            if st.name != "attn0":
                pe.wait_ge(const_set, 2)
                pe.wait_ge(xt_ready, 8 * (2 if st.name == "attn1" else 3))
            if st.rms:
                pe.wait_ge(fs["c"], 4)
            run(0, schedule(st.rms, True, False))
            run(1, schedule(st.rms, True, True, False))
            with pe.Fori(2, NKV) as i:
                run(i, schedule(st.rms, True, True))
            i = NKV
            for kind, t in schedule(st.rms, False, True):
                run(i, [(kind, t)])
                if st.name == "attn0" and (kind, t) == ("WO", 4):
                    pe_xattn_setup(pe)
                if kind == "WO" and t >= 2 and st.name != "attn0":
                    pe_transpose_tile(pe, st.name, t - 2, pb[t % 2], st.unit_read(NKV, -1))
            if st.name != "attn0":
                for t in (NT - 2, NT - 1):
                    pe_transpose_tile(pe, st.name, t, pb[t % 2], st.unit_read(NKV, -1))

        def act_attention(act, st):
            def unit(i, u):
                kind, g, n = st.units[u]
                if kind == "kv":
                    for m in range(2):
                        st.need(act, "k_ss", 8 * i + 2 * n + m)
                        wait(act, *st.unit_read(i, u))
                        st.need(act, "k_ms", 4 * (i - 1) + n + 1)
                        nc.scalar.activation(junk[:, :], kst[:, 2 * n + m, :], ACT.Square,
                                             accum_out=kss[:, 2 * n + m:2 * n + m + 1]).then_inc(A["k_ss"], 1)
                    return
                st.need(act, "proj_done", 12 * i + u + 1)
                if st.rms:
                    j = u - 4
                    st.need(act, "ss_done", 8 * i + j - 1)
                    nc.scalar.activation(sq[:, j % 2, :], pb[u % 2][:, :], ACT.Square).then_inc(A["q_sq"], 1)
                cols = slice(n * HALF, (n + 1) * HALF)
                if kind == "k":
                    dst = k_sb[:, cols]
                elif kind == "v":
                    dst = vst[:, :, :].rearrange("p t d -> p (t d)")[:, cols]
                else:
                    dst = q_sb[:, (2 * g + n) % 2, :]
                nc.scalar.activation(dst, pb[u % 2][:, :],
                                     ACT.Copy).then_inc(A["q_free" if st.rms else "proj_free"], 1)

            def k_scale(i, n):
                st.need(act, "kt_done", 2 * i + n + 1)
                st.need(act, "kf_ready", 1)
                nc.scalar.activation(k_sb[:, n * HALF:(n + 1) * HALF], pb[7][:, :], ACT.Copy,
                                     scale=kfac[:, 0:1]).then_inc(A["kt_ready"], 1)

            def v_high(i, n):
                st.need(act, "vt_done", 2 * i + n + 1)
                nc.scalar.activation(vh[:, 4 * n:4 * n + 4, :], pb[7][:, :].rearrange("p (t d) -> p t d", t=4),
                                     ACT.Copy).then_inc(A["v_hi"], 1)

            def exponentials(i, j):
                g, n = j // 2, j % 2
                st.need(act, "s_sub", 8 * i + j + 1)
                nc.scalar.activation(hn(sc_sb, g, n), hn(sc_sb, g, n), ACT.Exp).then_inc(A["exp_done"], 1)

            def run(i, events):
                for kind, n in events:
                    if kind == "U":
                        unit(i, n)
                    elif kind == "KT":
                        k_scale(i, n)
                    elif kind == "VT":
                        v_high(i, n)
                    elif kind == "SC":
                        exponentials(i, n)
                    elif kind == "T":
                        st.need(act, "t_done", 8 * (i - 1) + n + 1)
                        nc.scalar.activation(pth[:, :], pb[4][:, :], ACT.Copy).then_inc(A["pt_hi"], 1)
                    elif kind == "PV":
                        st.need(act, "pv_done", 8 * (i - 1) + n + 1)
                        nc.scalar.activation(oth[:, n % 2, :], pb[5][:, :], ACT.Copy).then_inc(A["o_hi"], 1)
                    elif kind == "WS":
                        if n == 0:
                            st.need(act, "wo_done", 8 * (i - 1))
                        act.wait_ge(ld_o[n], 16 * (NKV * st.index + i))
                        nc.scalar.activation(woh[:, n, :], raw[:, n, :], ACT.Copy).then_inc(A["wo_hi"], 1)

            if st.before:
                act.wait_ge(*stage_end(st.before))
            run(0, later(schedule(st.rms, True, False), ("SC",), 1))
            run(1, later(schedule(st.rms, True, True, False), ("SC",), 1))
            with act.Fori(2, NKV) as i:
                run(i, later(schedule(st.rms, True, True), ("SC",), 1))
            for kind, t in schedule(st.rms, False, True):
                run(NKV, [(kind, t)])
                if st.name == "attn0" and (kind, t) in (("WO", 3), ("WO", 5)):
                    act_xattn_setup(act, int(t == 5))
                if kind == "WO" and t >= 2 and st.name != "attn0":
                    act_transpose_tile(act, st.name, t - 2, pb[t % 2])
            if st.name != "attn0":
                for t in (NT - 2, NT - 1):
                    act_transpose_tile(act, st.name, t, pb[t % 2])

        def dve_attention(dve, st):
            def unit(i, u):
                kind, g, n = st.units[u]
                bank = pb[u % 2]
                if kind == "kv":
                    st.need(dve, "proj_done", 12 * i + u + 1)
                    st.need(dve, "v_ready", 2 * (i - 1) + n // 2 + 1)
                    kv = bank[:, :].rearrange("p (t c d) -> p t c d", t=2, c=2)
                    nc.vector.tensor_copy(kst[:, 2 * n:2 * n + 2, :], kv[:, :, 0, :])
                    nc.vector.tensor_copy(vst[:, 2 * n:2 * n + 2, :], kv[:, :, 1, :]).then_inc(A["kv_free"], 1)

            def k_mean_square(i, n):
                st.need(dve, "k_ss", 8 * i + 2 * n + 2)
                nc.vector.tensor_scalar(kms[:, 2 * n:2 * n + 2], kss[:, 2 * n:2 * n + 2], 1.0 / HD, EPS,
                                        ALU.mult, ALU.add).then_inc(A["k_ms"], 1)

            def k_normalise(i, n):
                st.need(dve, "k_rs", 4 * i + n + 1)
                for m in range(2):
                    t = 2 * n + m
                    last = nc.vector.tensor_scalar(kst[:, t, :], kst[:, t, :], rk[:, t:t + 1], None, ALU.mult)
                last.then_inc(A["k_nrm"], 1)

            def v_low(i, n):
                st.need(dve, "v_hi", 2 * i + n + 1)
                nc.vector.tensor_tensor(vl[:, 4 * n:4 * n + 4, :], pb[7][:, :].rearrange("p (t d) -> p t d", t=4),
                                        f32(vh[:, 4 * n:4 * n + 4, :]), ALU.subtract).then_inc(A["v_ready"], 1)

            def q_mean_square(i, j):
                g, n = j // 2, j % 2
                st.need(dve, "ss_done", 8 * i + j + 1)
                st.need(dve, "q_rs", 8 * (i - 1) + j + 1)
                nc.vector.tensor_scalar(qms[:, 4 * n:4 * n + 4, g], pb[7][:, 0:4], 1.0 / HD, EPS,
                                        ALU.mult, ALU.add).then_inc(A["ss_out"], 1)

            def scores(i, j):
                g, n = j // 2, j % 2
                bank = pb[2 + j % 2][:, :].rearrange("p (t s) -> p t s", t=4)
                dst = hn(sc_sb, g, n)
                st.need(dve, "sc_done", 8 * i + j + 1)
                st.need(dve, "p_ready", 8 * i)
                if st.per_head_bias:
                    dve.wait_ge(ld_b, 16 * (1 + i + 1))
                else:
                    dve.wait_ge(ld_b, 16 * (1 if st.index == 0 else 10))
                b = bias[:, g if st.per_head_bias else 0, :].rearrange("p (o s) -> p o s", o=1)
                if st.rms:
                    st.need(dve, "q_rs", 8 * i + j + 1)
                for h in range(2):
                    p0, p1 = 64 * h, 64 * h + 64
                    if st.rms:
                        last = nc.vector.tensor_tensor(
                            dst[p0:p1], bank[p0:p1, :, p0:p1],
                            hn(rq, g, n)[p0:p1].rearrange("p (t o) -> p t o", o=1).to_broadcast([64, 4, S]), ALU.mult)
                    else:
                        last = nc.vector.scalar_tensor_tensor(
                            dst[p0:p1], bank[p0:p1, :, p0:p1], st.scale, b[p0:p1].to_broadcast([64, 4, S]),
                            ALU.mult, ALU.add)
                last.then_inc(A["s_out"], 1)
                st.need(dve, "s_out", 8 * i + j + 1)
                if st.rms:
                    nc.vector.tensor_tensor(dst, dst, b.to_broadcast([P, 4, S]), ALU.add).then_inc(A["s_msk"], 1)
                    st.need(dve, "s_msk", 8 * i + j + 1)
                nc.vector.tensor_reduce(hn(smax, g, n), dst, AX_X, ALU.max).then_inc(A["s_max"], 1)
                st.need(dve, "s_max", 8 * i + j + 1)
                nc.vector.tensor_tensor(
                    dst, dst, hn(smax, g, n).rearrange("p (t o) -> p t o", o=1).to_broadcast([P, 4, S]),
                    ALU.subtract).then_inc(A["s_sub"], 1)

            def sums(i, j):
                g, n = j // 2, j % 2
                st.need(dve, "exp_done", 8 * i + j + 1)
                nc.vector.tensor_reduce(hn(ssum, g, n), hn(sc_sb, g, n), AX_X, ALU.add).then_inc(A["s_sum"], 1)
                st.need(dve, "s_sum", 8 * i + j + 1)
                nc.vector.reciprocal(hn(rs, g, n), hn(ssum, g, n)).then_inc(A["s_inv"], 1)
                st.need(dve, "s_inv", 8 * i + j + 1)
                nc.vector.tensor_tensor(
                    hn(rs2, g, n), hn(rs, g, n).rearrange("p (t o) -> p t o", o=1).to_broadcast([P, 4, 2]),
                    own_half[:, :].rearrange("p (o c) -> p o c", o=1).to_broadcast([P, 4, 2]),
                    ALU.mult).then_inc(A["s_rec"], 1)

            def run(i, events):
                for kind, n in events:
                    if kind == "U":
                        unit(i, n)
                        if st.rms and 1 <= n < 5:
                            k_mean_square(i, n - 1)
                        if st.rms and 2 <= n < 6:
                            k_normalise(i, n - 2)
                    elif kind == "VT":
                        v_low(i, n)
                    elif kind == "SQ":
                        q_mean_square(i, n)
                    elif kind == "SC":
                        scores(i, n)
                    elif kind == "SUM":
                        sums(i, n)
                    elif kind == "T":
                        st.need(dve, "pt_hi", 8 * (i - 1) + n + 1)
                        nc.vector.tensor_tensor(ptl[:, :], pb[4][:, :], f32(pth[:, :]),
                                                ALU.subtract).then_inc(A["pt_ready"], 1)
                    elif kind == "PV":
                        st.need(dve, "o_hi", 8 * (i - 1) + n + 1)
                        nc.vector.tensor_tensor(otl[:, n % 2, :], pb[5][:, :], f32(oth[:, n % 2, :]),
                                                ALU.subtract).then_inc(A["o_ready"], 1)
                    elif kind in ("WO", "WP"):
                        done = 8 * (i - (1 if kind == "WO" else 2)) + n + 1
                        st.need(dve, "wo_done", done)
                        nc.vector.tensor_tensor(xtile(n), pb[6][:, :], xtile(n), ALU.add).then_inc(A["x_added"], 1)
                    elif kind == "WS":
                        st.need(dve, "wo_hi", 4 * (i - 1) + n + 1)
                        nc.vector.tensor_tensor(wol[:, n, :], raw[:, n, :], f32(woh[:, n, :]),
                                                ALU.subtract).then_inc(A["wo_ready"], 1)

            def order(project, attend, last=True):
                ev = schedule(st.rms, project, attend, last)
                both = []
                for e in ev:
                    both.append(e)
                    if e[0] == "SC":
                        both.append(("SUM", e[1]))
                return later(both, ("SUM",), 3 if st.rms else 2)

            if st.before:
                dve.wait_ge(*stage_end(st.before))
            else:
                dve.wait_ge(const_in, 32)
            if st.rms:
                dve.wait_ge(const_in, 16 * 3)
                nc.vector.scalar_tensor_tensor(kfac[:, :], norm_w[:, 0:1], HD ** -0.5, norm_w[:, 1:2],
                                               ALU.mult, ALU.mult).then_inc(A["kf_ready"], 1)
                dve.wait_ge(A["kf_ready"], 1)
            run(0, order(True, False))
            if not st.before:
                dve.wait_ge(x_in, 16)
            run(1, order(True, True, False))
            with dve.Fori(2, NKV) as i:
                run(i, order(True, True))
            for kind, t in schedule(st.rms, False, True):
                run(NKV, [(kind, t)])
                if st.name == "attn0" and (kind, t) in (("WO", 2), ("WO", 5)):
                    dve_xattn_setup(dve, int(t == 5))
                if kind == "WO":
                    st.need(dve, "x_added", 56 + t + 1)
                    dve_norm_stats(dve, st.name, t, xtile(t))
                    if t >= 1:
                        dve_normalise(dve, st.name, t - 1, xtile(t - 1), xtile(t - 1))
                if kind == "WO" and t >= 2 and st.name != "attn0":
                    dve_transpose_tile(dve, st.name, t - 2, pb[t % 2])
            dve_normalise(dve, st.name, NT - 1, xtile(NT - 1), xtile(NT - 1))
            if st.name != "attn0":
                for t in (NT - 2, NT - 1):
                    dve_transpose_tile(dve, st.name, t, pb[t % 2])

        def pool_attention(pool, st):
            def split_chunk(i, c):
                slot = c if c < 5 else 4
                pool.wait_ge(ld_w[c], 16 * (NKV * st.index + i + 1))
                st.need(pool, "proj_done", 12 * (i - 1) + st.last_unit_of(c) + 1)
                src = raw[:, slot, :]
                hi, lo = (w[:, c].rearrange("p k n -> p (k n)") for w in (wh, wl))
                carry_waits(pool, pool_passed)
                nc.gpsimd.tensor_scalar(hi, src, 1.0, 0.0, ALU.mult, ALU.add).then_inc(A["w_hi"], 1)
                st.need(pool, "w_hi", 6 * i + c + 1)
                nc.gpsimd.tensor_tensor(lo, src, f32(hi), ALU.subtract).then_inc(A["w_ready"], 1)

            def split_v(i, n):
                st.need(pool, "kv_free", 4 * i + 2 * n + 2)
                st.need(pool, "pv_done", 8 * (i - 1) + 4 * n + 4)
                hi, lo, src = vh[:, 4 * n:4 * n + 4, :], vl[:, 4 * n:4 * n + 4, :], vst[:, 4 * n:4 * n + 4, :]
                carry_waits(pool, pool_passed)
                nc.gpsimd.tensor_scalar(hi, src, 1.0, 0.0, ALU.mult, ALU.add).then_inc(A["v_hi"], 1)
                st.need(pool, "v_hi", 2 * i + n + 1)
                nc.gpsimd.tensor_tensor(lo, src, f32(hi), ALU.subtract).then_inc(A["v_ready"], 1)

            def normalise(i, t):
                st.need(pool, "s_rec", 8 * i + (7 if t < 4 else 8))
                st.need(pool, "t_done", 8 * (i - 1) + t + 1)
                nc.gpsimd.tensor_tensor(
                    probs[:, t, :, :].rearrange("p g (c s) -> p g c s", c=2),
                    sc_sb[:, t, :, :].rearrange("p g (o s) -> p g o s", o=1).to_broadcast([P, G, 2, S]),
                    rs2[:, t, :, :].rearrange("p g (c o) -> p g c o", o=1).to_broadcast([P, G, 2, S]),
                    ALU.mult).then_inc(A["p_ready"], 1)

            def k_root(i, n):
                st.need(pool, "k_ms", 4 * i + n + 1)
                nc.gpsimd.tensor_tensor(rk[:, 2 * n:2 * n + 2], kms[:, 2 * n:2 * n + 2], mhalf[:, 0:2],
                                        ALU.pow).then_inc(A["k_rs"], 1)

            def q_root(i, j):
                g, n = j // 2, j % 2
                st.need(pool, "ss_out", 8 * i + j + 1)
                nc.gpsimd.tensor_tensor(hn(rq, g, n), hn(qms, g, n), mhalf[:, 0:4], ALU.pow).then_inc(A["q_rs"], 1)

            def step(i, more):
                if st.rms:
                    for n in range(4):
                        k_root(i, n)
                    if more:
                        split_chunk(i + 1, 0)
                        split_chunk(i + 1, 1)
                    for j in range(8):
                        q_root(i, j)
                        if more and j % 2 and j < 6:
                            split_chunk(i + 1, 2 + j // 2)
                    split_v(i, 0)
                    for t in range(4):
                        normalise(i, t)
                    split_v(i, 1)
                    for t in range(4, NT):
                        normalise(i, t)
                    if more:
                        split_chunk(i + 1, 5)
                else:
                    if more:
                        for c in range(5):
                            split_chunk(i + 1, c)
                    for t in range(NT):
                        normalise(i, t)
                    if more:
                        split_chunk(i + 1, 5)

            if st.before:
                pool.wait_ge(*stage_end(st.before))
            for c in range(2):
                split_chunk(0, c)
            if not st.before:
                pool.wait_ge(x0_ready, 4)
            for c in range(2, 6):
                split_chunk(0, c)
            step(0, True)
            with pool.Fori(1, NKV - 1) as i:
                step(i, True)
            step(NKV - 1, False)
            if st.name == "xattn1":
                pool_split_ffn1(pool, 0)
                pool_split_ffn1(pool, 1)
            for t in range(NT):
                pool_norm_root(pool, st.name, t)
                if st.name == "attn0" and t == 3:
                    pool_xattn_setup(pool)
                if st.name == "attn0" and t == 5:
                    context_low(pool, 0)
                    first_input_low(pool)
                if st.name == "xattn1" and t + 2 < len(G_PARTS):
                    pool_split_ffn1(pool, t + 2)

        XB = dict(k=(pb[0], pb[7]), q=(pb[1], pb[2]), kt=pb[3], qt=pb[4], gm=pb[5], out=pb[6])

        def sp_xattn(sp):
            sp.wait_ge(A["proj_done"], 96)
            sp.dma_start(x_wraw[:, :, :], a["x_wqk"]).then_inc(xs["w0"], 16)
            sp.dma_start(x_wv[:, :, :], a["x_wv"]).then_inc(xs["w1"], 16)
            sp.dma_start(x_wo[:, :, :], a["x_wo"]).then_inc(xs["w1"], 16)
            sp.dma_start(x_bg[:, :], a["x_bg"]).then_inc(xs["w2"], 16)
            sp.dma_start(x_blk[:, :], a["x_blk"]).then_inc(xs["w2"], 16)

            def load(p):
                wait(sp, xs["csp"], p)
                src = a["ctx"][p] if isinstance(p, int) else a["ctx"][bass.ds(p, 1)].rearrange("o p n -> p (o n)")
                sp.dma_start(x_craw[:, :], src).then_inc(xs["cin"], 16)
                if isinstance(p, int):
                    sp.wait_ge(*stage_end("attn0"))
                for b in range(2):
                    wait(sp, xs["g"], 2 * (p - 1) + b + 1)
                    src = a["ctxT_pair"][p, b] if isinstance(p, int) else \
                        a["ctxT_pair"][bass.ds(p, 1), b].rearrange("o p n -> p (o n)")
                    sp.dma_start(x_ct[:, b, :, :].rearrange("p k n -> p (k n)"), src).then_inc(xs[f"ctin{b}"], 16)
            load(0)
            with sp.Fori(1, NT) as p:
                load(p)

        def x_steps(new, mid, old):
            ev = [("QS", 7, 1), ("XL", 0, 0), ("OUT", 0, 1), ("KT", 7, 1), ("K", 0, 0), ("Q", 0, 0), ("QT", 6, 1)]
            ev += [("K", 1, 0), ("Q", 1, 0), ("QS", 0, 0), ("KT", 0, 0), ("QT", 7, 1), ("Y", 0, 2)]
            ev += [("K", 2, 0), ("Q", 2, 0), ("QS", 1, 0), ("KT", 1, 0), ("G", 1, 1), ("QT", 0, 0)]
            ev += [("XN", 0, 2)]
            ev += [("K", 3, 0), ("Q", 3, 0), ("QS", 2, 0), ("KT", 2, 0), ("QT", 1, 0), ("M", 1, 1)]
            ev += [("K", 4, 0), ("Q", 4, 0), ("QS", 3, 0), ("OUT", 1, 1), ("XT", 0, 2), ("KT", 3, 0), ("QT", 2, 0)]
            ev += [("OC", 0, 1), ("K", 5, 0), ("Q", 5, 0), ("QS", 4, 0), ("KT", 4, 0), ("QT", 3, 0), ("G", 0, 0)]
            ev += [("K", 6, 0), ("Q", 6, 0), ("QS", 5, 0), ("KT", 5, 0), ("QT", 4, 0), ("M", 0, 0)]
            ev += [("K", 7, 0), ("Q", 7, 0), ("QS", 6, 0), ("SP", 0, -1), ("KT", 6, 0), ("QT", 5, 0), ("VAR", 0, 1)]
            live = {-1: new, 0: new, 1: mid, 2: old}
            return [e for e in ev if live[e[2]] and (mid or e[0] != "XL")]

        def x_run(run):
            run(0, x_steps(True, False, False))
            run(1, x_steps(True, True, False))

        def x_end(run, prepare_ffn0=None):
            run(NT - 1, [e for e in x_steps(True, True, True) if e[0] != "SP"])
            for e in x_steps(False, True, True):
                run(NT, [e])
                if prepare_ffn0:
                    prepare_ffn0(e[0])
            run(NT + 1, x_steps(False, False, True))

        def pe_xattn_setup(pe):
            pe.wait_ge(A["proj_free"], 96)
            pe.wait_ge(xs["woc"], 1)
            for h in range(XH):
                r0 = 64 * (h % 2)
                last = nc.tensor.matmul(pb[h % 2][0:64, (h // 2) * S:(h // 2 + 1) * S], x_wv[r0:r0 + 64, h // 2, :],
                                        x_woc[r0:r0 + 64, h // 2, :], start=True, stop=True)
            last.then_inc(xs["u"], 1)
            pe.wait_ge(xs["w2"], 32)
            pe.wait_ge(A["s_out"], 64)
            nc.tensor.matmul(pb[2][:, 0:1], x_blk[:, :], x_bg[:, 0:1], start=True, stop=True).then_inc(xs["bm"], 1)

        def pe_xattn(pe):
            pe.wait_ge(xs["wsp"], 1)
            pe.wait_ge(xs["u_out"], 1)

            def run(p, events):
                for kind, u, age in events:
                    b, s = u // 4, u % 4
                    r = slice(64 * b, 64 * b + 64)
                    q = p - age
                    if kind == "K":
                        if u == 0:
                            wait(pe, xs["csp"], q + 1)
                        wait(pe, xs["kexp"], 8 * q + u - 1)
                        cols = slice(s * P, (s + 1) * P)
                        mm3(XB["k"][u % 2][:, :], (x_wh[r, 1, cols], x_wl[r, 1, cols]), (x_ch[r, :], x_cl[r, :]), True,
                            True).then_inc(xs["k"], 1)
                    elif kind == "Q":
                        if u == 0:
                            wait(pe, xs["xsp"], q + 1)
                        wait(pe, xs["qsub"], 8 * q + u - 1)
                        cols = slice(s * P, (s + 1) * P)
                        mm3(XB["q"][u % 2][:, :], (x_xh[r, cols], x_xl[r, cols]), (x_wh[r, 0, :], x_wl[r, 0, :]), True,
                            True).then_inc(xs["q"], 1)
                    elif kind == "KT":
                        wait(pe, xs["kexp"], 8 * q + u + 1)
                        wait(pe, xs["ekt"], 8 * q + u)
                        for n in range(4):
                            last = nc.tensor.transpose(XB["kt"][:, n * P:(n + 1) * P],
                                                       x_ek[:, u % 2, n * P:(n + 1) * P], ident[:, :])
                        last.then_inc(xs["kt"], 1)
                    elif kind == "QT":
                        wait(pe, xs["qn"], 8 * q + u + 1)
                        wait(pe, xs["qcp"], 8 * q + u)
                        for n in range(4):
                            last = nc.tensor.transpose(XB["qt"][:, n * P:(n + 1) * P],
                                                       x_en[:, u % 2, n * P:(n + 1) * P], ident[:, :])
                        last.then_inc(xs["qt"], 1)
                    elif kind == "G":
                        wait(pe, xs["ekt"], 8 * q + 4 * u + 4)
                        wait(pe, xs[f"ctin{u}"], 16 * (q + 1))
                        if u == 0:
                            wait(pe, xt_ready, p - 1)
                        else:
                            wait(pe, xs["sd"], p - 1)
                        wait(pe, xs["mr"], 2 * q + u)
                        for n in range(4):
                            last = nc.tensor.matmul(XB["gm"][0:64, :], x_ct[:, u, n, :],
                                                    x_ekT[:, u, n, :], start=n == 0, stop=n == 3)
                        last.then_inc(xs["g"], 1)
                    elif kind == "M":
                        wait(pe, xs["gt"], 2 * q + u + 1)
                        for n in range(4):
                            last = nc.tensor.matmul(XB["gm"][:, n * P:(n + 1) * P], x_gt[0:64, u, n * P:(n + 1) * P],
                                                    x_u[0:64, n * P:(n + 1) * P], start=True, stop=True)
                        last.then_inc(xs["m"], 1)
                    elif kind == "OUT":
                        wait(pe, xs["mr"], 2 * q + u + 1)
                        wait(pe, xs["qcp"], 8 * q + 4 * u + 4)
                        wait(pe, xs["osq"], q)
                        for n in range(4):
                            last = nc.tensor.matmul(XB["out"][:, :], x_m[:, n, u, :], x_q[:, u, n, :],
                                                    start=(u == 0 and n == 0), stop=(u == 1 and n == 3))
                        last.then_inc(xs["out"], 1)
                    elif kind == "VAR":
                        wait(pe, xs["osq"], q + 1)
                        wait(pe, xt_ready, p - 1)
                        wait(pe, xs["mr"], 2 * NT if isinstance(p, int) and p == NT else 2 * p + 1)
                        nc.tensor.matmul(XB["gm"][:, :], x_blk[:, :], x_sq[:, :], start=True,
                                         stop=True).then_inc(xs["var"], 1)
                    elif kind == "XT":
                        wait(pe, ln_done, 8 + q + 1)
                        wait(pe, xs["sd"], q + 1)
                        wait(pe, xs["mr"], 2 * NT if isinstance(p, int) and p > NT else 2 * p)
                        for k in range(KT):
                            last = nc.tensor.transpose(XB["gm"][:, k * P:(k + 1) * P], x_xn[:, k * P:(k + 1) * P],
                                                       ident[:, :])
                        last.then_inc(xt_done, 1)
            x_run(run)
            with pe.Fori(2, NT - 1) as p:
                run(p, x_steps(True, True, True))

            def prepare_ffn0(after):
                if after == "VAR":
                    pe_ffn0(pe, True)
            x_end(run, prepare_ffn0)

        def act_xattn_setup(act, part):
            if part == 0:
                act.wait_ge(xs["w0"], 16)
                nc.scalar.activation(x_wh[:, :, :], x_wraw[:, :, :], ACT.Copy).then_inc(xs["chi"], 1)
                return
            act.wait_ge(xs["u"], 1)
            for h in range(2):
                last = nc.scalar.activation(
                    x_u[0:64, :].rearrange("p (k c o) -> p k c o", k=4, c=2)[:, :, h, :],
                    pb[h][0:64, 0:4 * S].rearrange("p (k o) -> p k o", k=4), ACT.Copy)
            last.then_inc(xs["u_out"], 1)
            act.wait_ge(xs["cin"], 16)
            nc.scalar.activation(x_ch[:, :], x_craw[:, :], ACT.Copy).then_inc(xs["chi"], 1)
            act.wait_ge(ln_done, 1)
            nc.scalar.activation(x_xh[:, :], xtile(0), ACT.Copy).then_inc(xs["xhi"], 1)

        def act_xattn(act):
            act.wait_ge(xs["bc"], 1)

            def split_high(q):
                wait(act, xs["cin"], 16 * (q + 1))
                wait(act, xs["k"], 8 * q)
                nc.scalar.activation(x_ch[:, :], x_craw[:, :], ACT.Copy).then_inc(xs["chi"], 1)
                wait(act, xs["q"], 8 * q)
                nc.scalar.activation(x_xh[:, :], xtile(q), ACT.Copy).then_inc(xs["xhi"], 1)

            def run(p, events):
                for kind, u, age in events:
                    b, s = u // 4, u % 4
                    q = p - age
                    if kind == "SP":
                        split_high(q)
                    elif kind == "K":
                        wait(act, xs["kneg"], 8 * q + u + 1)
                        wait(act, xs["kt"], 8 * q + u - 1)
                        wait(act, xs["krz"], 2 * (q - 1) + b + 1)
                        nc.scalar.activation(x_ek[:, u % 2, :], XB["k"][u % 2][:, :], ACT.Exp, bias=x_knm[:, u:u + 1],
                                             accum_out=x_kz[:, u:u + 1]).then_inc(xs["kexp"], 1)
                    elif kind == "Q":
                        wait(act, xs["qsub"], 8 * q + u + 1)
                        nc.scalar.activation(x_e[:, s, :], x_e[:, s, :], ACT.Exp).then_inc(xs["qexp"], 1)
                    elif kind == "KT":
                        wait(act, xs["kt"], 8 * q + u + 1)
                        wait(act, xs["g"], 2 * (q - 1) + b + 1)
                        nc.scalar.activation(x_ekT[:, b, :, s * P:(s + 1) * P],
                                             XB["kt"][:, :].rearrange("p (n d) -> p n d", n=4),
                                             ACT.Copy).then_inc(xs["ekt"], 1)
                    elif kind == "QT":
                        wait(act, xs["qt"], 8 * q + u + 1)
                        wait(act, xs["out"], 2 * (q - 1) + b + 1)
                        nc.scalar.activation(x_q[:, b, :, s * P:(s + 1) * P],
                                             XB["qt"][:, :].rearrange("p (h n) -> p h n", h=4),
                                             ACT.Copy).then_inc(xs["qcp"], 1)
                    elif kind == "G":
                        wait(act, xs["g"], 2 * q + u + 1)
                        nc.scalar.activation(x_gt[0:64, u, :], XB["gm"][0:64, :], ACT.Copy).then_inc(xs["gt"], 1)
                    elif kind == "OC":
                        wait(act, xs["out"], 2 * q + 2)
                        wait(act, xs["y"], q)
                        nc.scalar.activation(x_oc[:, :], XB["out"][:, :], ACT.Identity,
                                             bias=x_bc[:, 0:1]).then_inc(xs["oc"], 1)
                        wait(act, xs["var"], q)
                        nc.scalar.activation(x_sq[:, :], XB["out"][:, :], ACT.Square,
                                             bias=x_bc[:, 0:1]).then_inc(xs["osq"], 1)
                    elif kind == "VAR":
                        wait(act, xs["var"], q + 1)
                        nc.scalar.activation(x_sd[:, :], XB["gm"][:, :], ACT.Ln,
                                             bias=x_eps[:, 0:1]).then_inc(xs["sd"], 1)
                        wait(act, xs["sd"], q + 1)
                        wait(act, xs["y"], q)
                        nc.scalar.activation(x_rd[:, :], x_sd[:, :], ACT.Exp, scale=-0.5).then_inc(xs["rd"], 1)
                    elif kind == "XT":
                        wait(act, xt_done, q + 1)
                        t0 = q * P
                        cols = slice(t0, t0 + P) if isinstance(p, int) else bass.ds(t0, P)
                        nc.scalar.activation(xTh[:, :, cols], XB["gm"][:, :].rearrange("p (k n) -> p k n", k=KT),
                                             ACT.Copy).then_inc(xt_hi, 1)
                        wait(act, ln_done, 8 + q + 1)
                        nc.scalar.activation(xtile(q), x_xn[:, :], ACT.Copy).then_inc(xs["xcp"], 1)
            x_run(run)
            with act.Fori(2, NT - 1) as p:
                run(p, x_steps(True, True, True))

            def prepare_ffn0(after):
                if after == "M":
                    act.wait_ge(xs["g"], 2 * NT)
                    high_weight(act, 0, 0)
                    high_weight(act, 0, 1)
                elif after == "VAR":
                    high_weight(act, 0, 2)
            x_end(run, prepare_ffn0)

        def dve_xattn_setup(dve, part):
            if part == 0:
                dve.wait_ge(xs["w1"], 32)
                nc.vector.tensor_reduce(x_wos[:, :], x_wo[:, :, :], AX_X, ALU.add).then_inc(xs["wos"], 1)
                nc.vector.memset(x_eps[:, :], EPS)
                dve.wait_ge(xs["wos"], 1)
                nc.vector.scalar_tensor_tensor(
                    x_woc[:, :, :], x_wos[:, :].rearrange("p (k o) -> p k o", o=1).to_broadcast([P, 4, S]), -1.0 / S,
                    x_wo[:, :, :], ALU.mult, ALU.add).then_inc(xs["woc"], 1)
                return
            dve.wait_ge(xs["bm"], 1)
            nc.vector.tensor_tensor(x_bc[:, :], x_bg[:, 0:1], pb[2][:, 0:1], ALU.subtract).then_inc(xs["bc"], 1)

        def dve_xattn(dve):
            def run(p, events):
                for kind, u, age in events:
                    b, s = u // 4, u % 4
                    q = p - age
                    if kind == "XL":
                        wait(dve, xs["xhi"], q + 1)
                        nc.vector.tensor_tensor(x_xl[:, :], xtile(q), f32(x_xh[:, :]),
                                                ALU.subtract).then_inc(xs["xsp"], 1)
                    elif kind == "K":
                        wait(dve, xs["k"], 8 * q + u + 1)
                        nc.vector.tensor_reduce(x_kmx[:, u:u + 1], XB["k"][u % 2][:, :], AX_X,
                                                ALU.max).then_inc(xs["kmax"], 1)
                        wait(dve, xs["kmax"], 8 * q + u + 1)
                        wait(dve, xs["kexp"], 8 * (q - 1) + u + 1)
                        nc.vector.tensor_scalar(x_knm[:, u:u + 1], x_kmx[:, u:u + 1], -1.0, None,
                                                ALU.mult).then_inc(xs["kneg"], 1)
                    elif kind == "Q":
                        bank = XB["q"][u % 2][:, :].rearrange("p (h d) -> p h d", h=XH)
                        wait(dve, xs["q"], 8 * q + u + 1)
                        nc.vector.tensor_reduce(x_qmx[:, s, :], bank, AX_X, ALU.max).then_inc(xs["qmax"], 1)
                        wait(dve, xs["qmax"], 8 * q + u + 1)
                        wait(dve, xs["qn"], 8 * q + u - 3)
                        nc.vector.tensor_tensor(
                            x_e[:, s, :].rearrange("p (h d) -> p h d", h=XH), bank,
                            x_qmx[:, s, :].rearrange("p (h o) -> p h o", o=1).to_broadcast([P, XH, XD]),
                            ALU.subtract).then_inc(xs["qsub"], 1)
                    elif kind == "QS":
                        wait(dve, xs["qexp"], 8 * q + u + 1)
                        nc.vector.tensor_reduce(x_qs[:, s, :], x_e[:, s, :].rearrange("p (h d) -> p h d", h=XH), AX_X,
                                                ALU.add).then_inc(xs["qsum"], 1)
                        wait(dve, xs["qsum"], 8 * q + u + 1)
                        nc.vector.reciprocal(x_qr[:, s, :], x_qs[:, s, :]).then_inc(xs["qrec"], 1)
                    elif kind == "G":
                        wait(dve, xs["kexp"], 8 * q + 4 * u + 4)
                        wait(dve, xs["mr"], 2 * (q - 1) + u + 1)
                        nc.vector.reciprocal(x_krz[:, 4 * u:4 * u + 4], x_kz[:, 4 * u:4 * u + 4]).then_inc(xs["krz"], 1)
                    elif kind == "M":
                        if isinstance(q, int) and q == 0:
                            dve.wait_ge(xs["zero"], 1)
                        wait(dve, xs["m"], 2 * q + u + 1)
                        wait(dve, xs["krz"], 2 * q + u + 1)
                        wait(dve, xs["out"], 2 * (q - 1) + u + 1)
                        bank = XB["gm"][:, :].rearrange("p (h o) -> p h o", h=4)
                        for h in range(2):
                            r = slice(64 * h, 64 * h + 64)
                            last = nc.vector.scalar_tensor_tensor(
                                x_m[r, :, u, 64 * u:64 * u + 64], bank[r, :, 64 * h:64 * h + 64], XD ** -0.5,
                                x_krz[r, 4 * u:4 * u + 4].rearrange("p (h o) -> p h o", o=1).to_broadcast([64, 4, S]),
                                ALU.mult, ALU.mult)
                        last.then_inc(xs["mr"], 1)
                    elif kind == "Y":
                        wait(dve, xs["rd"], q + 1)
                        nc.vector.scalar_tensor_tensor(x_y[:, :], x_oc[:, :], x_bg[:, 1:2], x_rd[:, :], ALU.mult,
                                                       ALU.mult).then_inc(xs["y"], 1)
                        wait(dve, xs["y"], q + 1)
                        nc.vector.tensor_tensor(x_r[:, :], x_y[:, :], xtile(q), ALU.add).then_inc(xs["r"], 1)
                        wait(dve, xs["r"], q + 1)
                        nc.vector.bn_stats(st6[:, 0, :], x_r[:, :]).then_inc(ln_bn, 1)
                        dve.wait_ge(ln_bn, 8 + q + 1)
                        carry_waits(dve, dve_passed)
                        nc.vector.bn_aggr(mv[:, 0, :], st6[:, 0, :]).then_inc(ln_ag, 1)
                        dve.wait_ge(ln_ag, 8 + q + 1)
                        nc.vector.tensor_scalar(var_eps[:, 0:1], mv[:, 0, 1:2], EPS, None,
                                                ALU.add).then_inc(ln_stat, 1)
                    elif kind == "XN":
                        dve.wait_ge(ln_rstd, 8 + q + 1)
                        nc.vector.tensor_scalar(x_xn[:, :], x_r[:, :], mv[:, 0, 0:1], rstd[:, 0:1],
                                                ALU.subtract, ALU.mult).then_inc(ln_done, 1)
                    elif kind == "XT":
                        dve.wait_ge(xt_hi, q + 1)
                        t0 = q * P
                        cols = slice(t0, t0 + P) if isinstance(p, int) else bass.ds(t0, P)
                        nc.vector.tensor_tensor(xTl[:, :, cols], XB["gm"][:, :].rearrange("p (k n) -> p k n", k=KT),
                                                f32(xTh[:, :, cols]), ALU.subtract).then_inc(xt_ready, 1)
            x_run(run)
            with dve.Fori(2, NT - 1) as p:
                run(p, x_steps(True, True, True))

            def prepare_ffn0(after):
                if after == "M":
                    dve.wait_ge(xs["kt"], 8 * NT)
                    dve.wait_ge(xs["qt"], 8 * NT)
                    for c in range(3):
                        dequantise(dve, 0, c)
            x_end(run, prepare_ffn0)

        def pool_xattn_setup(pool):
            pool.wait_ge(xs["chi"], 1)
            nc.gpsimd.tensor_tensor(x_wl[:, :, :], x_wraw[:, :, :], f32(x_wh[:, :, :]),
                                    ALU.subtract).then_inc(xs["wsp"], 1)

        def context_low(pool, q):
            wait(pool, xs["chi"], q + 2)
            nc.gpsimd.tensor_tensor(x_cl[:, :], x_craw[:, :], f32(x_ch[:, :]), ALU.subtract).then_inc(xs["csp"], 1)

        def first_input_low(pool):
            pool.wait_ge(xs["xhi"], 1)
            nc.gpsimd.tensor_tensor(x_xl[:, :], xtile(0), f32(x_xh[:, :]), ALU.subtract).then_inc(xs["xsp"], 1)

        def pool_xattn(pool):
            pool.wait_ge(*stage_end("attn0"))
            nc.gpsimd.memset(x_m[:, :, :, :], 0.0).then_inc(xs["zero"], 1)


            def run(p, events):
                for kind, u, age in events:
                    s = u % 4
                    q = p - age
                    if kind == "QS":
                        wait(pool, xs["qrec"], 8 * q + u + 1)
                        wait(pool, xs["qt"], 8 * q + u - 1)
                        nc.gpsimd.tensor_tensor(
                            x_en[:, u % 2, :].rearrange("p (h d) -> p h d", h=XH),
                            x_e[:, s, :].rearrange("p (h d) -> p h d", h=XH),
                            x_qr[:, s, :].rearrange("p (h o) -> p h o", o=1).to_broadcast([P, XH, XD]),
                            ALU.mult).then_inc(xs["qn"], 1)
                    elif kind == "Y":
                        pool.wait_ge(ln_stat, 8 + q + 1)
                        nc.gpsimd.tensor_tensor(rstd[:, 0:1], var_eps[:, 0:1], mhalf[:, 0:1],
                                                ALU.pow).then_inc(ln_rstd, 1)
                    elif kind == "SP":
                        context_low(pool, q)
            x_run(run)
            with pool.Fori(2, NT - 1) as p:
                run(p, x_steps(True, True, True))

            def prepare_ffn0(after):
                if after == "VAR":
                    low_weight(pool, 0, 0)
                    low_weight(pool, 0, 1)
            x_end(run, prepare_ffn0)

        def sp_ffn0(sp):
            def load(i):
                for c in range(3):
                    wait(sp, fs["dq"], 3 * (i - 1) + c + 1)
                    q, s = a["f_q"], a["f_s"]
                    if isinstance(i, int):
                        q, s = q[i, c], s[i:i + 1, c].to_broadcast([P, 1024])
                    else:
                        q = q[bass.ds(i, 1), c].rearrange("o p n -> p (o n)")
                        s = s[bass.ds(i, 1), c].to_broadcast([P, 1024])
                    sp.dma_start(f_q[:, c, :], q).then_inc(fs[f"in{c}"], 16)
                    sp.dma_start(f_s[:, c, :], s).then_inc(fs[f"in{c}"], 16)
            sp.wait_ge(xs["k"], 64)
            sp.wait_ge(xs["q"], 64)
            load(0)
            load(1)
            sp.wait_ge(*stage_end("xattn0"))
            sp.dma_start(f_c[:, :, :], a["ctxT"][:, 0:2, :]).then_inc(fs["cin"], 16)
            sp.wait_ge(fs["c"], 2)
            sp.dma_start(f_c[:, :, :], a["ctxT"][:, 2:4, :]).then_inc(fs["cin"], 16)
            with sp.Fori(2, NF) as i:
                load(i)

        def f_gate(m, which, k):
            return slice((which * KT + k) * P, (which * KT + k + 1) * P)

        def pe_ffn0(pe, first_half):
            def step(i, units):
                for u in units:
                    n, m = u // 2, u % 2
                    wait(pe, fs["w"], 3 * i + m + 1)
                    wait(pe, fs["it"], 4 * i + u - 1)
                    cols = slice(n * HALF, (n + 1) * HALF)
                    for which in range(2):
                        for k in range(KT):
                            w = f_gate(m, which, k)
                            last = mm3(pb[2 * which + u % 2][:, :], (f_wh[:, m, w], f_wl[:, m, w]),
                                       (xTh[:, k, cols], xTl[:, k, cols]), k == 0, k == KT - 1)
                    last.then_inc(fs["gu"], 1)
                if units[-1] != 3:
                    return
                for t in range(NT):
                    wait(pe, fs["w"], 3 * i + 3)
                    wait(pe, fs["i"], 4 * i + (2 if t < 4 else 4))
                    wait(pe, fs["add"], 8 * i + t - 1)
                    for m in range(2):
                        h = slice(t * P, (t + 1) * P)
                        w = slice(m * DM, (m + 1) * DM)
                        last = mm3(pb[4 + t % 2][:, :], (f_ih[:, m, h], f_il[:, m, h]),
                                   (f_wh[:, 2, w], f_wl[:, 2, w]), m == 0, m == 1)
                    last.then_inc(fs["dn"], 1)
            if first_half:
                step(0, [0, 1])
                return
            pe.wait_ge(xt_ready, 8)
            step(0, range(2, 4))
            with pe.Fori(1, NF) as i:
                step(i, range(4))
            for t in range(NT):
                pe_transpose_tile(pe, "ffn0", t, pb[t % 2], (fs["it"], 4 * NF))

        def high_weight(act, i, c):
            wait(act, fs["dq"], 3 * i + c + 1)
            if c < 2:
                wait(act, fs["gu"], 4 * (i - 1) + 3 + c)
            else:
                wait(act, fs["dn"], 8 * i)
            nc.scalar.activation(f_wh[:, c, :], f_w[:, c, :], ACT.Copy).then_inc(fs["whi"], 1)

        def act_ffn0(act):
            def silu(i, u):
                wait(act, fs["gu"], 4 * i + u + 1)
                wait(act, fs["it"], 4 * i + u - 1)
                nc.scalar.activation(f_sg[:, u % 2, :], pb[u % 2][:, :], ACT.Silu).then_inc(fs["sg"], 1)

            def high_hidden(i, u):
                n, m = u // 2, u % 2
                wait(act, fs["it"], 4 * i + u + 1)
                wait(act, fs["dn"], 8 * (i - 1) + 4 * n + 4)
                nc.scalar.activation(f_ih[:, m, n * HALF:(n + 1) * HALF], f_it[:, u % 2, :],
                                     ACT.Copy).then_inc(fs["ihi"], 1)

            def step(i, more):
                for u in range(4):
                    silu(i, u)
                    if u >= 1:
                        high_hidden(i, u - 1)
                    if u == 2 and more:
                        high_weight(act, i + 1, 0)
                high_hidden(i, 3)
                if more:
                    high_weight(act, i + 1, 1)
                    high_weight(act, i + 1, 2)
            step(0, True)
            with act.Fori(1, NF - 1) as i:
                step(i, True)
            step(NF - 1, False)
            for t in range(NT):
                act_transpose_tile(act, "ffn0", t, pb[t % 2])

        def dequantise(dve, i, c):
            wait(dve, fs[f"in{c}"], 32 * (i + 1))
            wait(dve, fs["w"], 3 * (i - 1) + c + 1)
            nc.vector.tensor_tensor(f_w[:, c, :], f_q[:, c, :], f_s[:, c, :], ALU.mult).then_inc(fs["dq"], 1)

        def dve_ffn0(dve):
            def hidden(i, u):
                wait(dve, fs["sg"], 4 * i + u + 1)
                wait(dve, fs["i"], 4 * i + u - 1)
                nc.vector.tensor_tensor(f_it[:, u % 2, :], pb[2 + u % 2][:, :], f_sg[:, u % 2, :],
                                        ALU.mult).then_inc(fs["it"], 1)

            def step(i, more, last):
                hidden(i, 0)
                hidden(i, 1)
                hidden(i, 2)
                if more:
                    dequantise(dve, i + 1, 0)
                hidden(i, 3)
                for t in range(NT):
                    if more and t in (2, 5):
                        dequantise(dve, i + 1, 1 if t == 2 else 2)
                    wait(dve, fs["dn"], 8 * i + t + 1)
                    wait(dve, fs["add"], 8 * (i - 1) + t + 1)
                    nc.vector.tensor_tensor(xtile(t), pb[4 + t % 2][:, :], xtile(t), ALU.add).then_inc(fs["add"], 1)
                    if last:
                        wait(dve, fs["add"], 8 * i + t + 1)
                        dve_norm_stats(dve, "ffn0", t, xtile(t))
                        if t >= 1:
                            dve_normalise(dve, "ffn0", t - 1, xtile(t - 1), xtile(t - 1))
            dve.wait_ge(xs["xcp"], 8)
            step(0, True, False)
            with dve.Fori(1, NF - 1) as i:
                step(i, True, False)
            step(NF - 1, False, True)
            dve_normalise(dve, "ffn0", NT - 1, xtile(NT - 1), xtile(NT - 1))
            for t in range(NT):
                dve_transpose_tile(dve, "ffn0", t, pb[t % 2])

        def low_weight(pool, i, c):
            wait(pool, fs["whi"], 3 * i + c + 1)
            nc.gpsimd.tensor_tensor(f_wl[:, c, :], f_w[:, c, :], f32(f_wh[:, c, :]),
                                    ALU.subtract).then_inc(fs["w"], 1)

        def pool_ffn0(pool):
            def low_hidden(i, u):
                n, m = u // 2, u % 2
                cols = slice(n * HALF, (n + 1) * HALF)
                wait(pool, fs["ihi"], 4 * i + u + 1)
                nc.gpsimd.tensor_tensor(f_il[:, m, cols], f_it[:, u % 2, :], f32(f_ih[:, m, cols]),
                                        ALU.subtract).then_inc(fs["i"], 1)

            def split_context(h):
                pool.wait_ge(fs["cin"], 16 * (h + 1))
                for m in range(2):
                    k = 2 * h + m
                    carry_waits(pool, pool_passed)
                    nc.gpsimd.tensor_scalar(cTh[:, k, :], f_c[:, m, :], 1.0, 0.0, ALU.mult,
                                            ALU.add).then_inc(fs["chi"], 1)
                    pool.wait_ge(fs["chi"], k + 1)
                    nc.gpsimd.tensor_tensor(cTl[:, k, :], f_c[:, m, :], f32(cTh[:, k, :]),
                                            ALU.subtract).then_inc(fs["c"], 1)

            def step(i, more):
                for u in range(4):
                    low_hidden(i, u)
                    if u == 2 and more:
                        low_weight(pool, i + 1, 0)
                if more:
                    low_weight(pool, i + 1, 1)
                    low_weight(pool, i + 1, 2)
            pool.wait_ge(xs["out"], 2 * NT)
            low_weight(pool, 0, 2)
            step(0, True)
            split_context(0)
            split_context(1)
            with pool.Fori(1, NF - 1) as i:
                step(i, True)
            step(NF - 1, False)
            for t in range(NT):
                pool_norm_root(pool, "ffn0", t)

        G_PARTS = [slice(KT * DM, KT * DM + KT * GC), slice(KT * DM + KT * GC, None)] + \
            [slice(k * DM, (k + 1) * DM) for k in range(KT)]

        def g_part(tile, k, what):
            if what == "base":
                return tile[:, k * DM:(k + 1) * DM]
            if what == "gate":
                return tile[:, KT * DM + k * GC:KT * DM + k * GC + 2 * P]
            return tile[:, KT * DM + KT * GC:]

        def sp_ffn1(sp):
            sp.wait_ge(A["sc_done"], 192)
            sp.dma_start(g_raw[:, KT * DM:KT * DM + KT * GC], a["g_gate"]).then_inc(gs["in0"], 16)
            sp.dma_start(g_raw[:, KT * DM + KT * GC:], a["g_b"]).then_inc(gs["in1"], 16)
            sp.dma_start(g_raw[:, 0:KT * DM], a["g_base"]).then_inc(gs["in2"], 16)
            sp.wait_ge(A["wo_ready"], 96)
            sp.dma_start(g_bb[:, :], a["g_bbase"].to_broadcast([P, DM])).then_inc(gs["in3"], 16)
            sp.dma_start(g_bt[:, :], a["g_bthr"].to_broadcast([P, 1])).then_inc(gs["in3"], 16)
            for t in range(NT):
                sp.wait_ge(ln_done, 8 * LN_NORMS["ffn1"] + t + 1)
                sp.dma_start(a["out"][t * P:(t + 1) * P, :], g_o[:, t % 4, :]).then_inc(gs[f"out{t % 4}"], 16)
            for h in range(4):
                sp.wait_ge(gs[f"out{h}"], 16 * (NT // 4))

        def pool_split_ffn1(pool, n):
            cols = G_PARTS[n]
            pool.wait_ge(gs["in0"] if n == 0 else gs["in1"] if n == 1 else gs["in2"], 16)
            nc.gpsimd.tensor_scalar(g_h[:, cols], g_raw[:, cols], 1.0, 0.0, ALU.mult, ALU.add).then_inc(gs["hi"], 1)
            pool.wait_ge(gs["hi"], n + 1)
            nc.gpsimd.tensor_tensor(g_l[:, cols], g_raw[:, cols], f32(g_h[:, cols]),
                                    ALU.subtract).then_inc(gs["w"], 1)

        def pool_ffn1(pool):
            pool.wait_ge(gs["in3"], 32)
            for t in range(NT):
                pool.wait_ge(xt_done, 24 + t + 1)
                nc.gpsimd.tensor_tensor(xtile(t), xtile(t), g_bb[:, :], ALU.add).then_inc(gs["xb"], 1)
            for t in range(NT):
                pool_norm_root(pool, "ffn1", t)

        def dve_ffn1(dve):
            NG = E_ * R_
            count = [0]

            def link(ins):
                ins.then_inc(gs["ch"], 1)
                count[0] += 1
                dve.wait_ge(gs["ch"], count[0])

            def spread(per_tile, n):
                return per_tile.rearrange("p (t o) -> p t o", o=1).to_broadcast([P, NT, n])

            def route():
                link(nc.vector.tensor_reduce(g_mx[:, :], g_hid[:, :, NG:NG + E_], AX_X, ALU.max))
                dve.wait_ge(gs["in3"], 32)
                nc.vector.tensor_scalar(g_e[:, :, E_:E_ + 2], g_hid[:, :, NG + E_:NG + E_ + 2], g_bt[:, 0:1], -1.0,
                                        ALU.add, ALU.mult)
                nc.vector.tensor_tensor(g_e[:, :, 0:E_], g_hid[:, :, NG:NG + E_], spread(g_mx[:, :], E_),
                                        ALU.subtract).then_inc(gs["res"], 1)
                dve.wait_ge(gs["exp"], 1)
                nc.vector.tensor_scalar(g_sum[:, 1, :], g_e[:, :, E_], 1.0, None, ALU.add)
                link(nc.vector.tensor_reduce(g_sum[:, 0, :], g_e[:, :, 0:E_], AX_X, ALU.add))
                link(nc.vector.reciprocal(g_rec[:, :, :], g_sum[:, :, :]))
                link(nc.vector.tensor_tensor(g_ad[:, :, :], g_e[:, :, 0:E_], spread(g_rec[:, 0, :], E_), ALU.mult))
                link(nc.vector.scalar_tensor_tensor(g_w[:, :, :], spread(g_rec[:, 1, :], E_), -0.125,
                                                    g_ad[:, :, :], ALU.mult, ALU.add))
                link(nc.vector.tensor_scalar(g_w[:, :, :], g_w[:, :, :], 0.0, None, ALU.max))
                link(nc.vector.tensor_reduce(g_ws[:, 0, :], g_w[:, :, :], AX_X, ALU.add))
                link(nc.vector.tensor_scalar(g_ws[:, 1, :], g_ws[:, 0, :], 0.0, None, ALU.is_equal))
                link(nc.vector.tensor_tensor(g_ws[:, 0, :], g_ws[:, 0, :], g_ws[:, 1, :], ALU.add))
                link(nc.vector.reciprocal(g_wr[:, :], g_ws[:, 0, :]))
                link(nc.vector.tensor_tensor(g_wn[:, :, :], g_w[:, :, :], spread(g_wr[:, :], E_), ALU.mult))

            def weigh(t):
                nc.vector.scalar_tensor_tensor(
                    g_z[:, t, :].rearrange("p (e r) -> p e r", e=E_),
                    g_hid[:, t, 0:NG].rearrange("p (e r) -> p e r", e=E_), 2.0,
                    g_wn[:, t, :].rearrange("p (e o) -> p e o", o=1).to_broadcast([P, E_, R_]),
                    ALU.mult, ALU.mult).then_inc(gs["z"], 1)

            def low_z(t):
                dve.wait_ge(gs["zhi"], t + 1)
                nc.vector.tensor_tensor(g_zl[:, t % 2, :], pb[6 + t % 2][:, 0:P], f32(g_zh[:, t % 2, :]),
                                        ALU.subtract).then_inc(gs["zr"], 1)

            def finish(t):
                dve.wait_ge(gs["p2"], t + 1)
                dve.wait_ge(gs["xb"], t + 1)
                link(nc.vector.tensor_tensor(xtile(t), pb[t % 6][:, :], xtile(t), ALU.add))
                dve_norm_stats(dve, "ffn1", t, xtile(t))

            def emit(t):
                if t >= 4:
                    dve.wait_ge(gs[f"out{t % 4}"], 16 * (t // 4))
                dve_normalise(dve, "ffn1", t, xtile(t), g_o[:, t % 4, :])

            for t in range(NT):
                dve.wait_ge(gs["p1"], t + 1)
                nc.vector.tensor_copy(g_hid[:, t, :], pb[6 + t % 2][:, 0:GC]).then_inc(gs["ev"], 1)
            dve.wait_ge(gs["ev"], NT)
            route()
            for t in range(NT):
                weigh(t)
            low_z(0)
            low_z(1)
            for t in range(NT):
                finish(t)
                if t + 2 < NT:
                    low_z(t + 2)
                if t >= 1:
                    emit(t - 1)
            emit(NT - 1)

        def pe_ffn1(pe):
            def first(t):
                h = slice(t * P, (t + 1) * P)
                pe.wait_ge(xt_ready, 24 + t + 1)
                if t >= 2:
                    pe.wait_ge(gs["ev"], t - 1)
                for k in range(KT):
                    last = mm3(pb[6 + t % 2][:, 0:2 * P], (xTh[:, k, h], xTl[:, k, h]),
                               (g_part(g_h, k, "gate"), g_part(g_l, k, "gate")), k == 0, k == KT - 1)
                last.then_inc(gs["p1"], 1)

            def base(t):
                h = slice(t * P, (t + 1) * P)
                if t >= 6:
                    pe.wait_ge(ln_bn, 8 * LN_NORMS["ffn1"] + t - 5)
                for k in range(KT):
                    mm3(pb[t % 6][:, :], (xTh[:, k, h], xTl[:, k, h]),
                        (g_part(g_h, k, "base"), g_part(g_l, k, "base")), k == 0, False)

            def transpose(t):
                pe.wait_ge(gs["z"], t + 1)
                if t >= 2:
                    pe.wait_ge(gs["zr"], t - 1)
                nc.tensor.transpose(pb[6 + t % 2][:, 0:P], g_z[:, t, :], ident[:, :]).then_inc(gs["zt"], 1)

            def experts(t):
                pe.wait_ge(gs["zr"], t + 1)
                mm3(pb[t % 6][:, :], (g_zh[:, t % 2, :], g_zl[:, t % 2, :]),
                    (g_part(g_h, 0, "up"), g_part(g_l, 0, "up")), False, True).then_inc(gs["p2"], 1)

            pe.wait_ge(A["x_added"], 192)
            pe.wait_ge(gs["w"], 2)
            for t in range(NT):
                first(t)
            pe.wait_ge(gs["w"], len(G_PARTS))
            for t in range(6):
                base(t)
            transpose(0)
            transpose(1)
            for t in range(NT):
                experts(t)
                if t + 2 < NT:
                    transpose(t + 2)
                if 2 <= t < 4:
                    base(t + 4)

        def act_ffn1(act):
            act.wait_ge(gs["res"], 1)
            nc.scalar.activation(g_e[:, :, :], g_e[:, :, :], ACT.Exp).then_inc(gs["exp"], 1)
            for t in range(NT):
                act.wait_ge(gs["zt"], t + 1)
                if t >= 2:
                    act.wait_ge(gs["p2"], t - 1)
                nc.scalar.activation(g_zh[:, t % 2, :], pb[6 + t % 2][:, 0:P], ACT.Copy).then_inc(gs["zhi"], 1)

        block = ctx.enter_context(nc.Block())

        @block.sync
        def _(sp):
            sp_attention(sp, stages[0])
            sp_xattn(sp)
            sp_ffn0(sp)
            sp_attention(sp, stages[1])
            sp_attention(sp, stages[2])
            sp_ffn1(sp)

        @block.tensor
        def _(pe):
            pe_attention(pe, stages[0])
            pe_xattn(pe)
            pe_ffn0(pe, False)
            pe_attention(pe, stages[1])
            pe_attention(pe, stages[2])
            pe_ffn1(pe)

        @block.scalar
        def _(act):
            for n in range(4):
                act.wait_ge(xr_in[n], 16)
                nc.scalar.activation(input_split(xTh, n), input_quarter(n)[0], ACT.Copy).then_inc(x0_hi, 1)
            act_attention(act, stages[0])
            act_xattn(act)
            act_ffn0(act)
            act_attention(act, stages[1])
            act_attention(act, stages[2])
            act_ffn1(act)

        @block.vector
        def _(dve):
            for n in range(4):
                dve.wait_ge(x0_hi, n + 1)
                nc.vector.tensor_tensor(input_split(xTl, n), input_quarter(n)[0], f32(input_split(xTh, n)),
                                        ALU.subtract).then_inc(x0_ready, 1)
            dve_attention(dve, stages[0])
            dve_xattn(dve)
            dve_ffn0(dve)
            dve_attention(dve, stages[1])
            dve_attention(dve, stages[2])
            dve_ffn1(dve)

        @block.gpsimd
        def _(pool):
            nc.gpsimd.memset(mhalf[:, :], -0.5).then_inc(const_set, 1)
            nc.gpsimd.memset(onecol[:, :], 1.0).then_inc(const_set, 1)
            pool.wait_ge(const_set, 2)
            pool_attention(pool, stages[0])
            pool_xattn(pool)
            pool_ffn0(pool)
            pool_attention(pool, stages[1])
            pool_attention(pool, stages[2])
            pool_ffn1(pool)


def kernel(**inputs):
    import numpy as np
    import concourse.bacc as bacc
    from concourse.bass_utils import run_bass_kernel_spmd

    v = {k: np.asarray(x) for k, x in inputs.items()}

    def col(w):
        return w.T.reshape(-1, P, w.shape[0]).transpose(1, 0, 2)

    def chunks(wq, wk, wv, order):
        q = col(wq).reshape(P, KT, NKV, G, HD).transpose(2, 3, 0, 1, 4)
        k = col(wk).reshape(P, KT, NKV, 1, HD).transpose(2, 3, 0, 1, 4)
        w = col(wv).reshape(P, KT, NKV, 1, HD).transpose(2, 3, 0, 1, 4)
        parts = {"q": q, "k": k, "v": w}
        return np.concatenate([parts[o] for o in order], axis=1).reshape(NKV, 6, P, KT * HD)

    def outs(wo):
        return wo.T.reshape(NKV, G, HD, DM)

    x2 = v["x"].reshape(TOK, DM)
    c2 = v["ctx_4096"].reshape(TOK, DM)
    cT = c2.T.reshape(KT, P, TOK).transpose(1, 0, 2)
    nq = NKV * G * HD
    wqkv = v["L1_attn_w_qkv"].T
    wkv = v["L0_xattn_Wkv"]
    twice = lambda w: np.concatenate([w, w], axis=0)

    def ffn_in(q):
        return q.T.reshape(KT, P, NF, 2, P)
    gq, uq = ffn_in(v["L0_ffn_gate_q"]), ffn_in(v["L0_ffn_up_q"])
    gu = np.stack([gq, uq]).transpose(3, 4, 2, 0, 1, 5).reshape(NF, 2, P, 1024)
    dq = v["L0_ffn_down_q"].T.reshape(NF, 1, 2, P, DM).transpose(0, 1, 3, 2, 4).reshape(NF, 1, P, 1024)
    f_q = np.concatenate([gu, dq], axis=1)
    sc = lambda s: s.T.reshape(KT, NF, 2, P)
    gus = np.stack([sc(v["L0_ffn_gate_s"]), sc(v["L0_ffn_up_s"])]).transpose(2, 3, 0, 1, 4).reshape(NF, 2, 1024)
    ds = v["L0_ffn_down_s"].T.reshape(NF, 1, 1024)
    f_s = np.concatenate([gus, ds], axis=1)

    pos = np.arange(S)
    rel = np.tile(pos[:, None] - pos[None, :], (2, 1))
    causal = np.where(rel >= 0, 0.0, NEG).astype(np.float32)
    slopes = ((2.0 ** (-8.0 / (NKV * G))) ** np.arange(1, NKV * G + 1, dtype=np.float32)).astype(np.float32)
    root = np.sqrt(np.maximum(rel, 0).astype(np.float32))
    alibi = np.where(rel[None] >= 0, -slopes[:, None, None] * root[None], np.float32(NEG)).astype(np.float32)
    alibi = alibi.reshape(NKV, G, P, S).transpose(0, 2, 1, 3).reshape(NKV, P, G * S)
    blk = np.kron(np.eye(2), np.full((S, S), 1.0 / S)).astype(np.float32)

    gate = np.concatenate([v["L1_ffn_A_w"].reshape(E_ * R_, DM), v["L1_ffn_W_gate"], v["L1_ffn_W_thr"][None],
                           np.zeros((1, DM), np.float32)], axis=0)
    up = v["L1_ffn_B_w"].transpose(0, 2, 1).reshape(E_ * R_, DM)

    data = {
        "x": x2.reshape(NT, P, DM).transpose(1, 0, 2),
        "xT": x2.T.reshape(KT, P, TOK).transpose(1, 0, 2),
        "ctx": c2.reshape(NT, P, DM),
        "ctxT": cT,
        "ctxT_pair": cT.reshape(P, KT, NT, 2, S).transpose(2, 3, 0, 1, 4).reshape(NT, 2, P, KT * S),
        "ident": np.eye(P, dtype=np.float32),
        "own_half": np.kron(np.eye(2), np.ones((S, 1))).astype(np.float32),
        "causal": causal, "alibi": alibi,
        "mask": twice(v["mask_1x1xSxS2_ff0"].reshape(S, S)),
        "norm_w": np.stack([v["L1_xattn_q_norm_w"], v["L1_xattn_k_norm_w"]], axis=1),
        "a0_in": chunks(v["L0_attn_wq"], v["L0_attn_wk"], v["L0_attn_wv"], "kqv"),
        "a0_out": outs(v["L0_attn_wo"]),
        "a1_in": chunks(wqkv[:nq], wqkv[nq:nq + NKV * HD], wqkv[nq + NKV * HD:], "kqv"),
        "a1_out": outs(v["L1_attn_w_o"].T),
        "a2_in": chunks(v["L1_xattn_q_proj_w"], v["L1_xattn_k_proj_w"], v["L1_xattn_v_proj_w"], "kvq"),
        "a2_out": outs(v["L1_xattn_o_proj_w"]),
        "x_wqk": np.stack([twice(v["L0_xattn_Wq"].T), twice(wkv[:XW].T)], axis=1),
        "x_wv": wkv[XW:].reshape(4, P, S).transpose(1, 0, 2),
        "x_wo": v["L0_xattn_Wout"].T.reshape(4, P, S).transpose(1, 0, 2),
        "x_bg": np.stack([np.tile(v["L0_xattn_b_out"], 2), np.tile(v["L0_xattn_g"].reshape(S), 2)], axis=1),
        "x_blk": blk,
        "f_q": f_q, "f_s": f_s,
        "g_base": col(v["L1_ffn_W_base"]).reshape(P, KT * DM),
        "g_gate": col(gate).reshape(P, KT * GC),
        "g_b": up,
        "g_bbase": v["L1_ffn_b_base"].reshape(1, DM),
        "g_bthr": v["L1_ffn_b_thr"].reshape(1, 1),
    }
    nc = bacc.Bacc("TRN2", target_bir_lowering=False, num_devices=1)
    arrays, args = {}, {}
    for name, x in data.items():
        x = np.ascontiguousarray(x)
        arrays["in_" + name] = x
        args[name] = nc.dram_tensor("in_" + name, x.shape, mybir.dt.from_np(x.dtype), kind="ExternalInput").ap()
    args["out"] = nc.dram_tensor("out_0", (TOK, DM), F32, kind="ExternalOutput").ap()
    program(nc, args)
    r = run_bass_kernel_spmd(nc, [arrays], core_ids=[0])
    return r.results[0]["out_0"].reshape(B, S, DM)
```
